# Optimizing a Trainium2 kernel written in Bass

```python
import numpy as np
import jax
import jax.numpy as jnp

def _softmax(x, axis=-1):
    return jax.nn.softmax(x, axis=axis)

def _gelu(x):
    return jax.nn.gelu(x, approximate=True)

def _silu(x):
    return jax.nn.silu(x)

def _sigmoid(x):
    return jax.nn.sigmoid(x)

def _layernorm(x, axis=-1, eps=1e-05):
    m = jnp.mean(x, axis=axis, keepdims=True)
    v = jnp.var(x, axis=axis, keepdims=True)
    return (x - m) / jnp.sqrt(v + eps)

def _scatter_add(tgt, idx, src, axis=0):
    return tgt.at[idx].add(src)

def _segment_sum(src, seg, n):
    return jax.ops.segment_sum(src, seg, n)
kernel_name = 'mk_gnn_preln_d4_gnn_r32_57c94d'

def setup_inputs(seed: int=0):
    np.random.seed(seed)
    _w = jnp.asarray

    def _rec_inputs():
        import jax
        import jax.numpy as jnp
        _gk = jax.random.key(seed)
        x = -0.000202 + 1 * jax.random.normal(jax.random.fold_in(_gk, 1), (3125, 64), jnp.float32)
        src = jax.random.randint(jax.random.fold_in(_gk, 2), (50000,), 0, 3125, jnp.int32)
        dst = jnp.minimum((3125 * jax.random.uniform(jax.random.fold_in(_gk, 3), (50000,)) ** 2.0).astype(jnp.int32), 99999)
        _o = jnp.argsort(dst, stable=True)
        src = src[_o]
        dst = dst[_o]
        edge_attr_16 = 0.000196303 + 1.00016 * jax.random.normal(jax.random.fold_in(_gk, 12), (50000, 16), jnp.float32)
        edge_attr_3 = 0.000669165 + 0.999965 * jax.random.normal(jax.random.fold_in(_gk, 13), (50000, 3), jnp.float32)
        edge_weight = jax.random.uniform(jax.random.fold_in(_gk, 15), (50000,), jnp.float32, 0.0, 1)
        return (x, src, dst, edge_attr_16, edge_attr_3, edge_weight)
    x, src, dst, edge_attr_16, edge_attr_3, edge_weight = _rec_inputs()

    def _L0_gnn_setup():
        import jax, jax.numpy as jnp
        import numpy as np
        N, E = (3125, 50000)
        IN_DIM, EMBED_DIM, EDGE_DIM = (64, 64, 16)
        EPS = 0.0
        key = jax.random.key(seed)
        ks = jax.random.split(key, 10)
        s = lambda fan_in: 1.0 / np.sqrt(fan_in)
        return {'x': jax.random.normal(ks[0], (N, IN_DIM), dtype=jnp.float32), 'edge_index': jax.random.randint(ks[1], (2, E), 0, N, dtype=jnp.int64), 'edge_attr': jax.random.normal(ks[2], (E, EDGE_DIM), dtype=jnp.float32), 'We': jax.random.uniform(ks[3], (EDGE_DIM, IN_DIM), jnp.float32, -s(EDGE_DIM), s(EDGE_DIM)), 'be': jax.random.uniform(ks[4], (IN_DIM,), jnp.float32, -s(EDGE_DIM), s(EDGE_DIM)), 'W1': jax.random.uniform(ks[5], (IN_DIM, EMBED_DIM), jnp.float32, -s(IN_DIM), s(IN_DIM)), 'b1': jax.random.uniform(ks[6], (EMBED_DIM,), jnp.float32, -s(IN_DIM), s(IN_DIM)), 'W2': jax.random.uniform(ks[7], (EMBED_DIM, EMBED_DIM), jnp.float32, -s(EMBED_DIM), s(EMBED_DIM)), 'b2': jax.random.uniform(ks[8], (EMBED_DIM,), jnp.float32, -s(EMBED_DIM), s(EMBED_DIM))}
    _L0_gnn_all = _L0_gnn_setup()
    _L0_gnn_in = {k: v for k, v in _L0_gnn_all.items() if k in ('We', 'be', 'W1', 'b1', 'W2', 'b2')}
    del _L0_gnn_all

    def _L1_gnn_setup():
        import jax, jax.numpy as jnp
        import numpy as np
        N = 3125
        E = 100000
        D = 64
        K = 10
        ALPHA = 0.1
        key = jax.random.key(seed)
        k1, k2, k3, k4 = jax.random.split(key, 4)
        feat = jax.random.normal(k1, (N, D), dtype=jnp.float32)
        src = jax.random.randint(k2, (E,), 0, N, dtype=jnp.int32)
        dst = jax.random.randint(k3, (E,), 0, N, dtype=jnp.int32)
        edge_weight = jax.random.uniform(k4, (E,), dtype=jnp.float32)
        return {'feat': feat, 'edge_weight': edge_weight, 'src': src, 'dst': dst}
    _L1_gnn_all = _L1_gnn_setup()
    _L1_gnn_in = {k: v for k, v in _L1_gnn_all.items() if k in ()}
    del _L1_gnn_all

    def _L2_gnn_setup():
        import jax, jax.numpy as jnp
        import numpy as np
        N, E = (50000, 25000)
        C, ED, L = (64, 3, 3)
        EPS = 1e-05

        def _layer_norm(h, g, b):
            mu = jnp.mean(h, axis=-1, keepdims=True)
            var = jnp.var(h, axis=-1, keepdims=True)
            return (h - mu) * jax.lax.rsqrt(var + EPS) * g + b
        key = jax.random.key(seed)
        ks = jax.random.split(key, 20)
        s = 0.1
        inp = {'x': jax.random.normal(ks[0], (N, C), dtype=jnp.float32), 'edge_index': jax.random.randint(ks[1], (2, E), 0, N, dtype=jnp.int64), 'edge_attr': jax.random.normal(ks[2], (E, ED), dtype=jnp.float32), 'W_node': jax.random.normal(ks[3], (L, C, C), dtype=jnp.float32) * s, 'W_e1': jax.random.normal(ks[4], (L, ED, C), dtype=jnp.float32) * s, 'b_e1': jnp.zeros((L, C), dtype=jnp.float32), 'W_e2': jax.random.normal(ks[5], (L, C, C), dtype=jnp.float32) * s, 'b_e2': jnp.zeros((L, C), dtype=jnp.float32), 'Wa1': jax.random.normal(ks[6], (L, 2 * C + ED, C), dtype=jnp.float32) * s, 'ba1': jnp.zeros((L, C), dtype=jnp.float32), 'Wa2': jax.random.normal(ks[7], (L, C, 1), dtype=jnp.float32) * s, 'ba2': jnp.zeros((L, 1), dtype=jnp.float32), 'bias': jnp.zeros((L, C), dtype=jnp.float32), 'ln_g': jnp.ones((L, C), dtype=jnp.float32), 'ln_b': jnp.zeros((L, C), dtype=jnp.float32)}
        return inp
    _L2_gnn_all = _L2_gnn_setup()
    _L2_gnn_in = {k: v for k, v in _L2_gnn_all.items() if k in ('W_node', 'W_e1', 'b_e1', 'W_e2', 'b_e2', 'Wa1', 'ba1', 'Wa2', 'ba2', 'bias', 'ln_g', 'ln_b')}
    del _L2_gnn_all

    def _L3_gnn_setup():
        import jax, jax.numpy as jnp
        import numpy as np
        N_NODES = 3125
        N_EDGES = 50000
        C_IN = 64
        C_OUT = 64
        BN_EPS = 1e-05
        key = jax.random.key(seed)
        k1, k2, k3, k4, k5 = jax.random.split(key, 5)
        x_bk_c = jax.random.normal(k1, (N_NODES, C_IN), dtype=jnp.float32)
        edge_index_batched = jax.random.randint(k2, (2, N_EDGES), 0, N_NODES, dtype=jnp.int64)
        W = jax.random.normal(k3, (C_OUT, 2 * C_IN), dtype=jnp.float32) / np.sqrt(2 * C_IN)
        bn_gamma = jnp.ones((C_OUT,), dtype=jnp.float32)
        bn_beta = jnp.zeros((C_OUT,), dtype=jnp.float32)
        bn_mean = 0.1 * jax.random.normal(k4, (C_OUT,), dtype=jnp.float32)
        bn_var = jnp.abs(1.0 + 0.1 * jax.random.normal(k5, (C_OUT,), dtype=jnp.float32))
        return {'x_bk_c': x_bk_c, 'edge_index_batched': edge_index_batched, 'W': W, 'bn_gamma': bn_gamma, 'bn_beta': bn_beta, 'bn_mean': bn_mean, 'bn_var': bn_var}
    _L3_gnn_all = _L3_gnn_setup()
    _L3_gnn_in = {k: v for k, v in _L3_gnn_all.items() if k in ('W', 'bn_gamma', 'bn_beta', 'bn_mean', 'bn_var')}
    del _L3_gnn_all
    return {'x': x, 'src': src, 'dst': dst, 'edge_attr_16': edge_attr_16, 'edge_attr_3': edge_attr_3, 'edge_weight': edge_weight, 'L0_gnn_We': _L0_gnn_in['We'], 'L0_gnn_be': _L0_gnn_in['be'], 'L0_gnn_W1': _L0_gnn_in['W1'], 'L0_gnn_b1': _L0_gnn_in['b1'], 'L0_gnn_W2': _L0_gnn_in['W2'], 'L0_gnn_b2': _L0_gnn_in['b2'], 'L2_gnn_W_node': _L2_gnn_in['W_node'], 'L2_gnn_W_e1': _L2_gnn_in['W_e1'], 'L2_gnn_b_e1': _L2_gnn_in['b_e1'], 'L2_gnn_W_e2': _L2_gnn_in['W_e2'], 'L2_gnn_b_e2': _L2_gnn_in['b_e2'], 'L2_gnn_Wa1': _L2_gnn_in['Wa1'], 'L2_gnn_ba1': _L2_gnn_in['ba1'], 'L2_gnn_Wa2': _L2_gnn_in['Wa2'], 'L2_gnn_ba2': _L2_gnn_in['ba2'], 'L2_gnn_bias': _L2_gnn_in['bias'], 'L2_gnn_ln_g': _L2_gnn_in['ln_g'], 'L2_gnn_ln_b': _L2_gnn_in['ln_b'], 'L3_gnn_W': _L3_gnn_in['W'], 'L3_gnn_bn_gamma': _L3_gnn_in['bn_gamma'], 'L3_gnn_bn_beta': _L3_gnn_in['bn_beta'], 'L3_gnn_bn_mean': _L3_gnn_in['bn_mean'], 'L3_gnn_bn_var': _L3_gnn_in['bn_var']}

def reference(x, src, dst, edge_attr_16, edge_attr_3, edge_weight, L0_gnn_We, L0_gnn_be, L0_gnn_W1, L0_gnn_b1, L0_gnn_W2, L0_gnn_b2, L2_gnn_W_node, L2_gnn_W_e1, L2_gnn_b_e1, L2_gnn_W_e2, L2_gnn_b_e2, L2_gnn_Wa1, L2_gnn_ba1, L2_gnn_Wa2, L2_gnn_ba2, L2_gnn_bias, L2_gnn_ln_g, L2_gnn_ln_b, L3_gnn_W, L3_gnn_bn_gamma, L3_gnn_bn_beta, L3_gnn_bn_mean, L3_gnn_bn_var):
    import jax
    import jax.numpy as jnp

    def _L0_gnn_ref(x, edge_index, edge_attr, We, be, W1, b1, W2, b2):
        import jax, jax.numpy as jnp
        import numpy as np
        N, E = (3125, 50000)
        IN_DIM, EMBED_DIM, EDGE_DIM = (64, 64, 16)
        EPS = 0.0
        src, dst = (edge_index[0], edge_index[1])
        e = edge_attr @ We + be
        msg = jax.nn.relu(x[src] + e)
        aggr = jax.ops.segment_sum(msg, dst, num_segments=x.shape[0])
        h = (1.0 + EPS) * x + aggr
        h = jax.nn.gelu(h @ W1 + b1, approximate=False)
        return h @ W2 + b2

    def _L1_gnn_ref(feat, edge_weight, src, dst):
        import jax, jax.numpy as jnp
        import numpy as np
        N = 3125
        E = 100000
        D = 64
        K = 10
        ALPHA = 0.1
        n = feat.shape[0]
        loop = jnp.arange(n, dtype=src.dtype)
        s = jnp.concatenate([src, loop])
        d = jnp.concatenate([dst, loop])
        w = jnp.concatenate([edge_weight, jnp.ones((n,), feat.dtype)])
        deg_out = jax.ops.segment_sum(w, s, num_segments=n)
        deg_in = jax.ops.segment_sum(w, d, num_segments=n)
        inv_sqrt_out = jnp.where(deg_out > 0, jax.lax.rsqrt(deg_out), 0.0)
        inv_sqrt_in = jnp.where(deg_in > 0, jax.lax.rsqrt(deg_in), 0.0)
        wn = w * inv_sqrt_out[s] * inv_sqrt_in[d]
        feat_0 = feat

        def step(h, _):
            agg = jax.ops.segment_sum(h[s] * wn[:, None], d, num_segments=n)
            return ((1.0 - ALPHA) * agg + ALPHA * feat_0, None)
        h, _ = jax.lax.scan(step, feat, None, length=K)
        return h

    def _L2_gnn_ref(x, edge_index, edge_attr, W_node, W_e1, b_e1, W_e2, b_e2, Wa1, ba1, Wa2, ba2, bias, ln_g, ln_b):
        import jax, jax.numpy as jnp
        import numpy as np
        N, E = (50000, 25000)
        C, ED, L = (64, 3, 3)
        EPS = 1e-05

        def _layer_norm(h, g, b):
            mu = jnp.mean(h, axis=-1, keepdims=True)
            var = jnp.var(h, axis=-1, keepdims=True)
            return (h - mu) * jax.lax.rsqrt(var + EPS) * g + b
        src = edge_index[0]
        dst = edge_index[1]
        n = x.shape[0]
        h = x
        for l in range(W_node.shape[0]):
            h_in = h
            hx = h @ W_node[l]
            ef = jax.nn.relu(edge_attr @ W_e1[l] + b_e1[l]) @ W_e2[l] + b_e2[l]
            xi = hx[dst]
            xj = hx[src]
            att_in = jnp.concatenate([xi, xj, edge_attr], axis=-1)
            a = jax.nn.sigmoid(jax.nn.relu(att_in @ Wa1[l] + ba1[l]) @ Wa2[l] + ba2[l])
            msg = a * (xj + ef)
            out = jax.ops.segment_sum(msg, dst, num_segments=n) + bias[l]
            out = _layer_norm(out, ln_g[l], ln_b[l])
            if l < W_node.shape[0] - 1:
                out = jax.nn.relu(out)
            h = out + h_in
        return h

    def _L3_gnn_ref(x_bk_c, edge_index_batched, W, bn_gamma, bn_beta, bn_mean, bn_var):
        import jax, jax.numpy as jnp
        import numpy as np
        N_NODES = 3125
        N_EDGES = 50000
        C_IN = 64
        C_OUT = 64
        BN_EPS = 1e-05
        row = edge_index_batched[0]
        col = edge_index_batched[1]
        x_i = x_bk_c[row]
        x_j = x_bk_c[col]
        e = jnp.concatenate((x_i, x_j - x_i), axis=1)
        h = jnp.einsum('ec,oc->eo', e, W)
        inv = bn_gamma * jax.lax.rsqrt(bn_var + BN_EPS)
        h = h * inv + (bn_beta - bn_mean * inv)
        h = h * jax.nn.sigmoid(h)
        x_out = jax.ops.segment_sum(h, row, num_segments=x_bk_c.shape[0])
        return x_out
    edge_index = jnp.stack([src, dst])
    h = jnp.maximum(_layernorm(x, axis=-1), 0.0)
    x = x + _L0_gnn_ref(h, edge_index, edge_attr_16, L0_gnn_We, L0_gnn_be, L0_gnn_W1, L0_gnn_b1, L0_gnn_W2, L0_gnn_b2)
    h = jnp.maximum(_layernorm(x, axis=-1), 0.0)
    x = x + _L1_gnn_ref(h, edge_weight, src, dst)
    h = jnp.maximum(_layernorm(x, axis=-1), 0.0)
    x = x + _L2_gnn_ref(h, edge_index, edge_attr_3, L2_gnn_W_node, L2_gnn_W_e1, L2_gnn_b_e1, L2_gnn_W_e2, L2_gnn_b_e2, L2_gnn_Wa1, L2_gnn_ba1, L2_gnn_Wa2, L2_gnn_ba2, L2_gnn_bias, L2_gnn_ln_g, L2_gnn_ln_b)
    h = jnp.maximum(_layernorm(x, axis=-1), 0.0)
    x = x + _L3_gnn_ref(h, edge_index, L3_gnn_W, L3_gnn_bn_gamma, L3_gnn_bn_beta, L3_gnn_bn_mean, L3_gnn_bn_var)
    return x

_drawn_inputs = setup_inputs


def setup_inputs(seed=0):
    import zlib

    import numpy as np

    out = dict(_drawn_inputs(seed))
    spreads = {'L2_gnn_b_e1': (0.0, 0.307),
     'L2_gnn_b_e2': (0.0, 0.1),
     'L2_gnn_ba1': (0.0, 0.8),
     'L2_gnn_ba2': (0.0, 0.8),
     'L2_gnn_bias': (0.0, 0.519),
     'L2_gnn_ln_g': (1.0, 0.2),
     'L2_gnn_ln_b': (0.0, 0.1),
     'L3_gnn_bn_gamma': (1.0, 0.2),
     'L3_gnn_bn_beta': (0.0, 0.1)}
    factors = {'edge_attr_3': 3.197,
     'edge_weight': 4.115,
     'L0_gnn_b1': 3.156,
     'L2_gnn_W_e1': 2.993,
     'L2_gnn_Wa1': 8.0,
     'L2_gnn_Wa2': 8.0}
    for name, (base, spread) in spreads.items():
        noise = np.random.default_rng([zlib.crc32(name.encode()), seed]).standard_normal(out[name].shape)
        drawn = base * np.exp(spread * noise) if base else spread * noise
        out[name] = jnp.asarray(drawn.astype(out[name].dtype))
    for name, factor in factors.items():
        out[name] = (out[name] * factor).astype(out[name].dtype)
    return out
```

```python
from contextlib import ExitStack

import concourse.bass as bass
from concourse import mybir

F32 = mybir.dt.float32
BF16 = mybir.dt.bfloat16
I32 = mybir.dt.int32
ALU = mybir.AluOpType
ACT = mybir.ActivationFunctionType
AX_X = mybir.AxisListType.X

N, E, D = 3125, 50000, 64
LO, HI = 125, 25
EP, EJ = 125, 400
DA, DB = 16, 3
T = 416
K = 4
U = 8
CH = 2
CT = K * U // CH
BODY = K * U
NB = T // BODY
assert NB * BODY == T and T >= E // 128 + HI
R = 4
STEPS, ALPHA = 10, 0.1
LAYERS = 3
LN_EPS = 1e-5
C = 24
C_ATT3, C_ONE, C_W, C_KEY, C_OTHER = DA, DA + DB, DA + DB + 1, DA + DB + 2, DA + DB + 3
C2, C2_KEY, C2_OTHER = 4, 0, 1
SG = 8
ROUND = 12582912.0
EP_L0, EP_L1, EP_L2, EP_L3 = 0, 1, 1 + STEPS, 1 + STEPS + LAYERS
PB = 5
NP = HI // PB


def gnn_kernel(nc, x, src, dst, edge_attr_16, edge_attr_3, edge_weight,
               We, be, W1, b1, W2, b2,
               W_node, W_e1, b_e1, W_e2, b_e2, Wa1, ba1, Wa2, ba2, bias2, ln_g, ln_b,
               W3, bn_gamma, bn_beta, bn_mean, bn_var, out):
    with ExitStack() as ctx:
        def sb(name, shape, dt=F32):
            return ctx.enter_context(nc.sbuf_tensor(name, shape, dt))

        def sem(name):
            return ctx.enter_context(nc.semaphore(name))

        rows_dst = nc.dram_tensor("rows_dst", [128 * T, C], F32).ap()
        rows_src = nc.dram_tensor("rows_src", [128 * T, C2], F32).ap()
        table = nc.dram_tensor("table", [N, D], F32).ap()
        table2 = nc.dram_tensor("table2", [N, 2 * D], F32).ap()

        iota_row = sb("iota_row", [128, 128])
        iota_p = sb("iota_p", [128, 1])
        iota_hi = sb("iota_hi", [128, HI])
        iota_t = sb("iota_t", [1, T])
        ident = sb("ident", [128, 128])
        ident_b = sb("ident_b", [128, 128], BF16)
        before = sb("before", [128, 128])
        ones = sb("ones", [128, EJ])
        zeros = sb("zeros", [128, 512])
        zeros_b = sb("zeros_b", [128, 512], BF16)

        key_i = sb("key_i", [EP, 2, EJ], I32)
        key = sb("key", [EP, 2, EJ])
        lo = sb("lo", [EP, 2, EJ])
        hi = sb("hi", [EP, 2, EJ])
        pos = sb("pos", [EP, 2, EJ])
        ta = sb("ta", [EP, 2, EJ])
        tb = sb("tb", [EP, 2, EJ])
        wgt = sb("wgt", [EP, EJ])
        at16 = sb("at16", [EP, EJ, DA])
        at3 = sb("at3", [EP, EJ, DB])
        cnt = sb("cnt", [EP, 2, HI])
        tiles = sb("tiles", [EP, 2, HI])
        base = sb("base", [EP, 2, HI])
        tsum = sb("tsum", [EP, 2, HI])
        blkc = sb("blkc", [1, 2, T])
        blk = sb("blk", [1, 2, T], I32)
        oh_lo = sb("oh_lo", [EP, 2, SG, LO])
        oh_hi = sb("oh_hi", [EP, 2, SG, HI])
        stage = sb("stage", [EP, 2, SG, C])
        stage_at = sb("stage_at", [EP, 2, SG], I32)

        xs = sb("xs", [LO, HI, D])
        hs = sb("hs", [LO, HI, D])
        fs = sb("fs", [LO, HI, D])
        gs = sb("gs", [LO, HI, D])
        t1 = sb("t1", [LO, HI, D])
        t2 = sb("t2", [LO, HI, D])
        space = at16[:].rearrange("p j c -> p (j c)")
        tab2 = space[:, 0:HI * 2 * D].rearrange("p (h c) -> p h c", h=HI)
        local_b = space[:, HI * 2 * D:HI * 2 * D + 3 * HI * D // 2].bitcast(BF16).rearrange("p (s h d) -> p s h d", s=3, h=HI)
        mean = sb("mean", [LO, HI])
        var = sb("var", [LO, HI])
        rstd = sb("rstd", [LO, HI])
        deg = sb("deg", [LO, 2, HI])
        inv_deg = sb("inv_deg", [LO, 2, HI])
        keep = sb("keep", [LO, HI])
        last_in = sb("last_in", [LO, HI])

        wl0 = sb("wl0", [K * C, K, D])
        w1s = sb("w1s", [D, D])
        w2s = sb("w2s", [D, D])
        b1c = sb("b1c", [D, 1])
        b2r = sb("b2r", [LO, D])
        wz = sb("wz", [K * C, K, D])
        wt = sb("wt", [K * C, K // 2, 2 * D])
        we2 = sb("we2", [128, 2 * D])
        wn = sb("wn", [D, D])
        wnT = sb("wnT", [D, D])
        wa1 = sb("wa1", [D, 2, D])
        wcat = sb("wcat", [D, 3 * D])
        wa2r = sb("wa2r", [128, D])
        ba2c = sb("ba2c", [128, 1])
        be2r = sb("be2r", [LO, D])
        biasr = sb("biasr", [LO, D])
        lngr = sb("lngr", [LO, D])
        lnbr = sb("lnbr", [LO, D])
        floors = sb("floors", [LO, LAYERS])
        floor = sb("floor", [LO, 1])
        w3s = sb("w3s", [D, 2 * D])
        bnc = sb("bnc", [D, 2])
        bnr = sb("bnr", [LO, 4, D])
        w3d = sb("w3d", [D, 2, D])
        w3T = sb("w3T", [D, 2 * D])

        pay = sb("pay", [128, CH, CT, C])
        pay2 = sb("pay2", [128, CH, CT, C2])
        at = sb("at", [128, CH, CT], I32)
        rows = sb("rows", [128, U, K, 2 * D])
        space2 = rows[:].rearrange("p u k c -> p (u k c)")
        fill = space2[:, 0:T // 8 * C].rearrange("p (t c) -> p t c", c=C)
        fill2 = space2[:, T // 8 * C:T // 8 * C + T * C2].rearrange("p (t c) -> p t c", c=C2)
        oh = sb("oh", [128, R, K, LO])
        ohb = sb("ohb", [128, R, K, LO], BF16)
        ohT = sb("ohT", [LO, R, K, 128], BF16)
        payT = sb("payT", [K * C, R, 128])
        hid = sb("hid", [128, R, K // 2, 128])
        s1 = sb("s1", [128, R, 2, K, D])
        zr = sb("zr", [128, R, K, D])
        logit = sb("logit", [128, R, K])
        att = sb("att", [128, R, K])
        msg = sb("msg", [128, R, K, D])
        st = sb("st", [LO, PB, D])
        hT = sb("hT", [D, PB, 128])
        uT = sb("uT", [D, PB, 128])

        ps = ctx.enter_context(nc.psum_tensor("ps", [128, 8, 512], F32))
        flat = ps[:].rearrange("p b c -> p (b c)")
        acc = flat[:, 0:HI * D]
        acc3 = acc[0:LO, :].rearrange("p (h d) -> p h d", d=D)

        def lin(u):
            return ps[:, 4 + u % 2, :].rearrange("p (s k d) -> p s k d", s=2, k=K)

        def payT_ps(bank):
            return ps[0:K * C, bank, 0:128]
        hid_ps = ps[:, 7, 0:256].rearrange("p (q e) -> p q e", q=K // 2)
        ohT_ps = ps[0:LO, 6, 128:128 + K * 64].bitcast(BF16).rearrange("p (k e) -> p k e", k=K)

        loaded = sem("loaded")
        consts = sem("consts")
        dve_consts = sem("dve_consts")
        filled = sem("filled")
        dve_step = sem("dve_step")
        act_step = sem("act_step")
        rank_loop = sem("rank_loop")
        counted = sem("counted")
        prefixed = sem("prefixed")
        placed = sem("placed")
        staged = sem("staged")
        scattered = [sem("scattered0"), sem("scattered1")]
        deg_oh = sem("deg_oh")
        deg_mm = sem("deg_mm")
        deg_ready = sem("deg_ready")
        deg_read = sem("deg_read")
        node_ready = sem("node_ready")
        table_in = sem("table_in")
        local_ready = sem("local_ready")
        pay_in = [sem(f"pay_in{c}") for c in range(CH)]
        at_ready = sem("at_ready")
        gathered = [sem(f"gathered{u}") for u in range(U)]
        slots_free = sem("slots_free")
        acc_done = sem("acc_done")
        acc_read = sem("acc_read")
        oh_ready = sem("oh_ready")
        tr_ready = sem("tr_ready")
        payT_ready = sem("payT_ready")
        lin_ready = sem("lin_ready")
        sum_ready = sem("sum_ready")
        msg_ready = sem("msg_ready")
        ohb_ready = sem("ohb_ready")
        ohT_done = sem("ohT_done")
        ohT_ready = sem("ohT_ready")
        hid_done = sem("hid_done")
        hid_ready = sem("hid_ready")
        zr_ready = sem("zr_ready")
        logit_ready = sem("logit_ready")
        att_ready = sem("att_ready")
        st_ready = sem("st_ready")
        stT_done = sem("stT_done")
        hT_ready = sem("hT_ready")
        mlp_done = sem("mlp_done")
        uT_ready = sem("uT_ready")
        proj_done = sem("proj_done")
        proj_read = sem("proj_read")
        layer_w = sem("layer_w")
        layer_w_free = sem("layer_w_free")
        w_prep = sem("w_prep")
        w_mm = sem("w_mm")
        sqrt_in = sem("sqrt_in")
        sqrt_out = sem("sqrt_out")
        hs_ready = sem("hs_ready")
        out_done = sem("out_done")
        held = sem("held")

        loads = []
        loads += [(key_i[:, 1, :], dst.rearrange("(p j) -> p j", p=EP)),
                  (key_i[:, 0, :], src.rearrange("(p j) -> p j", p=EP)),
                  (xs[:], x.rearrange("(p h) d -> p h d", p=LO)),
                  (wgt[:], edge_weight.rearrange("(p j) -> p j", p=EP)),
                  (at16[:], edge_attr_16.rearrange("(p j) c -> p j c", p=EP)),
                  (at3[:], edge_attr_3.rearrange("(p j) c -> p j c", p=EP)),
                  (w1s[:], W1), (w2s[:], W2), (b1c[:], b1.unsqueeze(1)),
                  (b2r[:], b2.partition_broadcast(LO)), (w3s[:], W3),
                  (bnc[:, 0:1], bn_gamma.unsqueeze(1)), (bnc[:, 1:2], bn_var.unsqueeze(1))]
        loads += [(bnr[:, i, :], v.partition_broadcast(LO))
                  for i, v in enumerate((bn_gamma, bn_beta, bn_mean, bn_var))]
        block_loads = []
        for k in range(K):
            block_loads += [(wl0[C * k:C * k + DA, k, :], We), (wl0[C * k + C_ONE:C * k + C_ONE + 1, k, :], be.unsqueeze(0))]

        def layer_loads(l):
            a = [(wn[:], W_node[l]), (wa1[:, 0, :], Wa1[l, D:2 * D]), (wa1[:, 1, :], Wa1[l, 0:D]),
                 (we2[0:D, 0:D], W_e2[l]), (we2[D:2 * D, D:2 * D], W_e2[l]),
                 (wa2r[:], Wa2[l].rearrange("c o -> (c o)").partition_broadcast(128)),
                 (ba2c[:], ba2[l].partition_broadcast(128)),
                 (be2r[:], b_e2[l].partition_broadcast(LO)), (biasr[:], bias2[l].partition_broadcast(LO)),
                 (lngr[:], ln_g[l].partition_broadcast(LO)), (lnbr[:], ln_b[l].partition_broadcast(LO))]
            for k in range(K):
                q, f = k // 2, (k % 2) * D
                r, o = C * k + C_ATT3, C * k + C_ONE
                a += [(wz[r:r + DB, k, :], Wa1[l, 2 * D:2 * D + DB]), (wz[o:o + 1, k, :], ba1[l].unsqueeze(0)),
                      (wt[r:r + DB, q, f:f + D], W_e1[l]), (wt[o:o + 1, q, f:f + D], b_e1[l].unsqueeze(0))]
            return a
        LW = 11 + 4 * K

        def hold(eng, semaphore, value):
            eng.wait_ge(semaphore, value)
            eng.sem_inc(held, 1)

        block = ctx.enter_context(nc.Block())

        @block.sync
        def _(sp):
            for to, frm in loads:
                sp.dma_start(to, frm).then_inc(loaded, 16)
            sp.wait_ge(consts, 1)
            for to, frm in block_loads:
                sp.dma_start(to, frm).then_inc(loaded, 16)
            by_part = rows_dst.rearrange("(p t) c -> p t c", p=128)
            for i in range(8):
                n = T // 8
                sp.dma_start(by_part[:, i * n:(i + 1) * n, :], fill).then_inc(filled, 16)
            sp.dma_start(rows_src.rearrange("(p t) c -> p t c", p=128), fill2).then_inc(filled, 16)

            def write_table(to, frm, n):
                sp.wait_ge(node_ready, n + 1)
                sp.dma_start(to, frm).then_inc(table_in, 16)

            def stream(ep, frm, to):
                view = frm.rearrange("(p t) c -> p t c", p=128)
                with sp.Fori(0, NB) as i:
                    m = ep * NB + i
                    for c in range(CH):
                        sp.wait_ge(slots_free, m * U + (c + 1) * (U // CH))
                        sp.dma_start(to[:, c, :, :], view[:, bass.ds(i * BODY + c * CT, CT), :]).then_inc(pay_in[c], 16)

            table_sb = table.rearrange("(p h) d -> p h d", p=LO)
            table2_sb = table2.rearrange("(p h) d -> p h d", p=LO)
            write_table(table_sb, hs[:], EP_L0)
            for h in range(2):
                sp.wait_ge(scattered[h], 16 * SG * (EJ // SG // 2))
            stream(EP_L0, rows_dst, pay)
            with sp.Fori(0, STEPS) as s:
                write_table(table_sb, hs[:], s + EP_L1)
                stream(s + EP_L1, rows_dst, pay)
            with sp.Fori(0, LAYERS) as l:
                sp.wait_ge(layer_w_free, l + 1)
                for to, frm in layer_loads(l):
                    sp.dma_start(to, frm).then_inc(layer_w, 16)
                write_table(table2_sb, tab2, l + (EP_L2 + 1))
                stream(l + EP_L2, rows_dst, pay)
            write_table(table_sb, t1[:], EP_L3 + 1)
            for h in range(2):
                sp.wait_ge(scattered[h], 2 * 16 * SG * (EJ // SG // 2))
            stream(EP_L3, rows_src, pay2)
            sp.wait_ge(node_ready, EP_L3 + 3)
            sp.dma_start(out.rearrange("(p h) d -> p h d", p=LO), xs[:]).then_inc(out_done, 16)
            sp.wait_ge(out_done, 16)

        @block.gpsimd
        def _(pool):
            nc.gpsimd.iota(iota_row[:], [[1, 128]], base=0, channel_multiplier=0, allow_small_or_imprecise_dtypes=True)
            nc.gpsimd.iota(iota_p[:], [[0, 1]], base=0, channel_multiplier=1, allow_small_or_imprecise_dtypes=True)
            nc.gpsimd.iota(iota_hi[:], [[1, HI]], base=0, channel_multiplier=0, allow_small_or_imprecise_dtypes=True)
            nc.gpsimd.iota(iota_t[:], [[1, T]], base=0, channel_multiplier=0, allow_small_or_imprecise_dtypes=True)
            nc.gpsimd.memset(wl0[:], 0.0)
            nc.gpsimd.memset(wz[:], 0.0)
            nc.gpsimd.memset(wt[:], 0.0)
            nc.gpsimd.memset(we2[:], 0.0)
            nc.gpsimd.memset(floors[:, 0:LAYERS - 1], 0.0)
            nc.gpsimd.memset(floors[:, LAYERS - 1:LAYERS], -3.0e38)
            nc.gpsimd.memset(fill[:, :, 0:C_KEY], 0.0)
            nc.gpsimd.memset(fill[:, :, C_KEY:C_KEY + 1], -1.0)
            nc.gpsimd.memset(fill[:, :, C_KEY + 1:C], 0.0)
            nc.gpsimd.memset(fill2[:, :, C2_KEY:C2_KEY + 1], -1.0)
            nc.gpsimd.memset(fill2[:, :, C2_KEY + 1:C2], 0.0)
            pool.drain()
            pool.sem_inc(consts, 1)

            def scatter(which, to, width):
                with pool.Fori(0, EJ // SG // 2) as i:
                    for h in range(2):
                        hold(pool, staged, (i + which * (EJ // SG // 2)) * 2 + h + 1)
                        for j in range(SG):
                            nc.gpsimd.indirect_dma_start(
                                to, bass.IndirectOffsetOnAxis(ap=stage_at[:, h, j:j + 1], axis=0),
                                stage[:, h, j, 0:width], None).then_inc(scattered[h], 16)

            def gather(ep, p, c_other, frm, width):
                hold(pool, table_in, 16 * (ep + 1))
                with pool.Fori(0, NB) as i:
                    m = ep * NB + i
                    for c in range(CH):
                        pool.wait_ge(pay_in[c], 16 * (m + 1))
                        hold(pool, slots_free, m * U + (c + 1) * (U // CH))
                        nc.gpsimd.tensor_copy(at[:, c, :], p[:, c, :, c_other]).then_inc(at_ready, 1)
                        hold(pool, at_ready, m * CH + c + 1)
                        for u in range(c * U // CH, (c + 1) * U // CH):
                            for k in range(K):
                                j = (u * K + k) % CT
                                nc.gpsimd.indirect_dma_start(
                                    rows[:, u, k, 0:width], None, frm,
                                    bass.IndirectOffsetOnAxis(ap=at[:, c, j:j + 1], axis=0)).then_inc(gathered[u], 16)

            pool.wait_ge(filled, 16 * 9)
            scatter(0, rows_dst, C)
            gather(EP_L0, pay, C_OTHER, table, D)
            scatter(1, rows_src, C2)
            with pool.Fori(0, STEPS) as s:
                gather(s + EP_L1, pay, C_OTHER, table, D)
            with pool.Fori(0, LAYERS) as l:
                gather(l + EP_L2, pay, C_OTHER, table2, 2 * D)
            gather(EP_L3, pay2, C2_OTHER, table, D)

        @block.vector
        def _(v):
            done = [0]

            def link(ins):
                done[0] += 1
                ins.then_inc(dve_step, 1)
                v.wait_ge(dve_step, done[0])

            def steps(loop, count, index):
                start, n = done[0], [0]

                def link_in(ins):
                    n[0] += 1
                    ins.then_inc(dve_step, 1)
                    v.wait_ge(dve_step, index * count + (start + n[0]))
                return link_in

            def over_d(a):
                return a.unsqueeze(2).to_broadcast([LO, HI, D])

            def over_hi(a):
                return a.unsqueeze(1).to_broadcast([LO, HI, D])

            sqrts = [0]

            def layer_norm(link, frm, to, tmp, n):
                link(nc.vector.tensor_reduce(mean[:], frm, AX_X, ALU.add))
                link(nc.vector.tensor_scalar(mean[:], mean[:], 1.0 / D, None, ALU.mult))
                link(nc.vector.tensor_tensor(to, frm, over_d(mean[:]), ALU.subtract))
                link(nc.vector.tensor_tensor(tmp, to, to, ALU.mult))
                link(nc.vector.tensor_reduce(var[:], tmp, AX_X, ALU.add))
                nc.vector.tensor_scalar(var[:], var[:], 1.0 / D, LN_EPS, ALU.mult, ALU.add).then_inc(sqrt_in, 1)
                v.wait_ge(sqrt_out, n + 1)
                link(nc.vector.reciprocal(rstd[:], rstd[:]))
                link(nc.vector.tensor_tensor(to, to, over_d(rstd[:]), ALU.mult))

            LN_LINKS = 7

            v.sem_inc(proj_read, 1)
            v.sem_inc(layer_w_free, 1)
            v.wait_ge(consts, 1)
            nc.vector.memset(ones[:], 1.0)
            nc.vector.memset(zeros[:], 0.0)
            nc.vector.memset(zeros_b[:], 0.0)
            nc.vector.tensor_scalar(ident[:], iota_row[:], iota_p[:, 0:1], None, ALU.is_equal)
            nc.vector.tensor_scalar(ident_b[:], iota_row[:], iota_p[:, 0:1], None, ALU.is_equal)
            link(nc.vector.tensor_scalar(before[:], iota_row[:], iota_p[:, 0:1], None, ALU.is_gt))
            nc.vector.memset(tb[:, 0, 0:1], 0.0).then_inc(dve_consts, 1)

            v.wait_ge(loaded, 16 * (len(loads) + len(block_loads)))
            v.wait_ge(dve_consts, 1)
            link(nc.vector.tensor_copy(key[:], key_i[:]))
            link(nc.vector.tensor_scalar(ta[:], key[:], 1.0 / HI, -0.48, ALU.mult, ALU.add))
            link(nc.vector.tensor_scalar(ta[:], ta[:], ROUND, None, ALU.add))
            link(nc.vector.tensor_scalar(lo[:], ta[:], -ROUND, None, ALU.add))
            link(nc.vector.scalar_tensor_tensor(hi[:], lo[:], -float(HI), key[:], ALU.mult, ALU.add))

            layer_norm(link, xs[:], t1[:], t2[:], 0)
            nc.vector.tensor_scalar(hs[:], t1[:], 0.0, None, ALU.max).then_inc(node_ready, 1)

            with v.Fori(0, HI) as b:
                lk = steps(v, 2, b)
                lk(nc.vector.tensor_scalar(ta[:], hi[:], iota_hi[0:EP, bass.ds(b, 1)], None, ALU.is_equal))
                lk(nc.vector.tensor_reduce(cnt[:, :, bass.ds(b, 1)], ta[:], AX_X, ALU.add))
            done[0] += 2 * HI
            v.sem_inc(counted, 1)
            v.wait_ge(prefixed, 1)
            pre = ps[0:EP, 7, 0:2 * HI].rearrange("p (s h) -> p s h", s=2)
            tot = ps[0:EP, 7, 2 * HI:4 * HI].rearrange("p (s h) -> p s h", s=2)
            link(nc.vector.tensor_scalar(tiles[:], tot, 1.0 / 128, 0.5 - 1.0 / 256, ALU.mult, ALU.add))
            link(nc.vector.tensor_scalar(tiles[:], tiles[:], ROUND, None, ALU.add))
            link(nc.vector.tensor_scalar(tiles[:], tiles[:], -ROUND, 1.0, ALU.add, ALU.max))
            for s in range(2):
                link(nc.vector.tensor_tensor_scan(tsum[:, s, :], ones[0:EP, 0:HI], tiles[:, s, :], 0.0, ALU.mult, ALU.add))
            link(nc.vector.tensor_tensor(tsum[:], tsum[:], tiles[:], ALU.subtract))
            link(nc.vector.scalar_tensor_tensor(base[:], tsum[:], 128.0, pre, ALU.mult, ALU.add))
            link(nc.vector.tensor_scalar(base[:], base[:], -1.0, None, ALU.add))
            link(nc.vector.memset(pos[:], 0.0))
            with v.Fori(0, HI) as b:
                lk = steps(v, 4 + 2, b)
                lk(nc.vector.tensor_scalar(ta[:], hi[:], iota_hi[0:EP, bass.ds(b, 1)], None, ALU.is_equal))
                nc.vector.tensor_tensor_scan(tb[:, 0, :], ones[0:EP, :], ta[:, 0, :], 0.0, ALU.mult, ALU.add)
                lk(nc.vector.tensor_tensor_scan(tb[:, 1, :], ones[0:EP, :], ta[:, 1, :], 0.0, ALU.mult, ALU.add))
                for s in range(2):
                    lk(nc.vector.scalar_tensor_tensor(tb[:, s, :], tb[:, s, :], base[:, s, bass.ds(b, 1)], ta[:, s, :],
                                                      ALU.add, ALU.mult))
                lk(nc.vector.tensor_tensor(pos[:], pos[:], tb[:], ALU.add))
                lk(nc.vector.memset(tb[:, 0, 0:1], 0.0))
            done[0] += 6 * HI
            link(nc.vector.tensor_scalar(ta[:], pos[:], 1.0 / 128, -(0.5 - 1.0 / 256), ALU.mult, ALU.add))
            link(nc.vector.tensor_scalar(ta[:], ta[:], ROUND, None, ALU.add))
            link(nc.vector.tensor_scalar(ta[:], ta[:], -ROUND, None, ALU.add))
            link(nc.vector.scalar_tensor_tensor(pos[:], ta[:], -128.0, pos[:], ALU.mult, ALU.add))
            nc.vector.scalar_tensor_tensor(pos[:], pos[:], float(T), ta[:], ALU.mult, ALU.add).then_inc(placed, 1)
            link(nc.vector.memset(blkc[:], 0.0))
            for s in range(2):
                for b in range(1, HI):
                    link(nc.vector.scalar_tensor_tensor(blkc[:, s, :], iota_t[:], tsum[0:1, s, b:b + 1], blkc[:, s, :],
                                                        ALU.is_ge, ALU.add))
            nc.vector.tensor_scalar(blk[:], blkc[:], float(D), None, ALU.mult).then_inc(placed, 1)

            G2 = EJ // SG // 2
            for s in range(2):
                with v.Fori(0, G2) as i:
                    for h in range(2):
                        j = (i * 2 + h) * SG
                        g = (i + s * G2) * 2 + h
                        v.wait_ge(deg_mm, g + 1)
                        nc.vector.tensor_tensor(oh_lo[:, h], iota_row[0:EP, 0:LO].unsqueeze(1).to_broadcast([EP, SG, LO]),
                                                lo[:, s, bass.ds(j, SG)].unsqueeze(2).to_broadcast([EP, SG, LO]), ALU.is_equal)
                        nc.vector.tensor_tensor(oh_hi[:, h], iota_hi[0:EP].unsqueeze(1).to_broadcast([EP, SG, HI]),
                                                hi[:, s, bass.ds(j, SG)].unsqueeze(2).to_broadcast([EP, SG, HI]),
                                                ALU.is_equal).then_inc(rank_loop, 1)
                        v.wait_ge(rank_loop, g + 1)
                        nc.vector.tensor_tensor(oh_hi[:, h], oh_hi[:, h],
                                                wgt[:, bass.ds(j, SG)].unsqueeze(2).to_broadcast([EP, SG, HI]),
                                                ALU.mult).then_inc(deg_oh, 1)
            v.wait_ge(deg_ready, 1)
            deg_ps = ps[0:LO, 6, 0:2 * HI].rearrange("p (s h) -> p s h", s=2)
            nc.vector.tensor_scalar(deg[:], deg_ps, 1.0, None, ALU.add).then_inc(deg_read, 1)
            v.wait_ge(deg_read, 1)
            nc.vector.tensor_scalar(inv_deg[:], deg[:], 1e-30, None, ALU.max).then_inc(sqrt_in, 1)
            v.wait_ge(sqrt_out, 2)
            link(nc.vector.reciprocal(inv_deg[:], inv_deg[:]))
            link(nc.vector.scalar_tensor_tensor(inv_deg[:], deg[:], 0.0, inv_deg[:], ALU.is_gt, ALU.mult))
            nc.vector.tensor_scalar(last_in[:], inv_deg[:, 1, :], 1.0 - ALPHA, None, ALU.mult)
            link(nc.vector.scalar_tensor_tensor(keep[:], inv_deg[:, 0, :], 1.0 - ALPHA, inv_deg[:, 1, :], ALU.mult, ALU.mult))

            def one_hots(n, u, p, c_key, c_w=None):
                c = u // (U // CH)
                v.wait_ge(slots_free, n + U - R + 1)
                for k in range(K):
                    j = (u * K + k) % CT
                    ins = nc.vector.tensor_scalar(oh[:, u % R, k, :], iota_row[:, 0:LO], p[:, c, j, c_key:c_key + 1],
                                                  None if c_w is None else p[:, c, j, c_w:c_w + 1], ALU.is_equal,
                                                  *(() if c_w is None else (ALU.mult,)))
                ins.then_inc(oh_ready, 1)

            with v.Fori(0, NB) as i:
                for u in range(U):
                    n = i * U + u
                    if u % (U // CH) == 0:
                        v.wait_ge(pay_in[u // (U // CH)], 16 * (i + 1))
                    one_hots(n, u, pay, C_KEY)
                    v.wait_ge(lin_ready, n + 1)
                    v.wait_ge(gathered[u], 16 * K * (i + 1))
                    nc.vector.tensor_tensor(s1[:, u % R, 0], lin(u)[:, 0], rows[:, u, :, 0:D], ALU.add).then_inc(sum_ready, 1)
            v.wait_ge(acc_done, 1)
            nc.vector.tensor_tensor(hs[:], hs[:], acc3, ALU.add).then_inc(acc_read, 1)
            v.wait_ge(acc_read, 1)
            v.sem_inc(hs_ready, 1)
            with v.Fori(0, NP) as i:
                v.wait_ge(proj_done, i + 2)
                y = ps[0:LO, 2, 0:PB * D].rearrange("p (k d) -> p k d", k=PB)
                nc.vector.tensor_tensor(t1[:, bass.ds(i * PB, PB), :], y, b2r[:].unsqueeze(1).to_broadcast([LO, PB, D]),
                                        ALU.add).then_inc(proj_read, 1)
            v.wait_ge(proj_read, NP + 1)
            link(nc.vector.tensor_tensor(xs[:], xs[:], t1[:], ALU.add))

            layer_norm(link, xs[:], t1[:], t2[:], 2)
            link(nc.vector.tensor_scalar(t1[:], t1[:], 0.0, None, ALU.max))
            nc.vector.tensor_scalar(gs[:], t1[:], ALPHA, None, ALU.mult)
            link(nc.vector.tensor_tensor(t1[:], t1[:], over_d(inv_deg[:, 0, :]), ALU.mult))
            nc.vector.tensor_scalar(fs[:], t1[:], ALPHA, None, ALU.mult)
            nc.vector.tensor_copy(hs[:], t1[:]).then_inc(node_ready, 1)
            v.wait_ge(node_ready, EP_L1 + 1)
            start = done[0]
            with v.Fori(0, STEPS) as s:
                with v.Fori(0, NB) as i:
                    m = (s + EP_L1) * NB + i
                    for u in range(U):
                        if u % (U // CH) == 0:
                            v.wait_ge(pay_in[u // (U // CH)], 16 * (m + 1))
                        one_hots(m * U + u, u, pay, C_KEY, C_W)
                v.wait_ge(acc_done, s + EP_L1 + 1)
                v.wait_ge(table_in, 16 * (s + EP_L1 + 1))
                lk = steps(v, 2, s)
                nc.vector.tensor_tensor(t2[:], hs[:], acc3, ALU.add).then_inc(acc_read, 1)
                v.wait_ge(acc_read, s + EP_L1 + 1)
                lk(nc.vector.tensor_tensor(t1[:], t2[:], over_d(keep[:]), ALU.mult))
                lk(nc.vector.tensor_tensor(hs[:], t1[:], fs[:], ALU.add))
                v.sem_inc(node_ready, 1)
            done[0] += 2 * STEPS
            link(nc.vector.tensor_tensor(t1[:], t2[:], over_d(last_in[:]), ALU.mult))
            link(nc.vector.tensor_tensor(t1[:], t1[:], gs[:], ALU.add))
            link(nc.vector.tensor_tensor(xs[:], xs[:], t1[:], ALU.add))

            layer_norm(link, xs[:], t1[:], t2[:], 3)
            link(nc.vector.tensor_scalar(hs[:], t1[:], 0.0, None, ALU.max))
            COUNT = 16 + LN_LINKS
            with v.Fori(0, LAYERS) as l:
                ln = [0]
                lstart = done[0]

                def lk(ins):
                    ln[0] += 1
                    ins.then_inc(dve_step, 1)
                    v.wait_ge(dve_step, l * COUNT + (lstart + ln[0]))
                v.wait_ge(layer_w, 16 * LW * (l + 1))
                lk(nc.vector.tensor_copy(floor[:], floors[:, bass.ds(l, 1)]))
                v.wait_ge(w_mm, 2 * l + 1)
                nc.vector.tensor_copy(wnT[:], ps[0:D, 7, 0:D]).then_inc(w_prep, 1)
                v.wait_ge(w_mm, 2 * l + 2)
                nc.vector.tensor_copy(wcat[:, 0:D], wn[:])
                lk(nc.vector.tensor_copy(wcat[:, D:3 * D], ps[0:D, 7, 128:128 + 2 * D]))
                v.sem_inc(hs_ready, 1)
                hold(v, table_in, 16 * (l + EP_L2))
                with v.Fori(0, NP) as i:
                    q = (l + 1) * NP + i
                    v.wait_ge(proj_done, q + 2)
                    y = flat[0:LO, 0:PB * 256].rearrange("p (k c) -> p k c", k=PB)
                    bl = bass.ds(i * PB, PB)
                    nc.vector.tensor_tensor(tab2[:, bl, 0:D], y[:, :, 0:D], be2r[:].unsqueeze(1).to_broadcast([LO, PB, D]), ALU.add)
                    nc.vector.tensor_copy(tab2[:, bl, D:2 * D], y[:, :, D:2 * D])
                    nc.vector.tensor_copy(t1[:, bl, :], y[:, :, 2 * D:3 * D]).then_inc(proj_read, 1)
                v.wait_ge(proj_read, (l + 2) * NP + 1)
                v.sem_inc(node_ready, 1)
                lk(nc.vector.tensor_copy(local_b[:, 0], t1[:]))
                lk(nc.vector.tensor_tensor(t1[:], t1[:], local_b[:, 0], ALU.subtract))
                lk(nc.vector.tensor_copy(local_b[:, 1], t1[:]))
                lk(nc.vector.tensor_tensor(t1[:], t1[:], local_b[:, 1], ALU.subtract))
                lk(nc.vector.tensor_copy(local_b[:, 2], t1[:]))
                v.sem_inc(local_ready, 1)
                with v.Fori(0, NB) as i:
                    m = (l + EP_L2) * NB + i
                    for u in range(U):
                        n2 = (l * NB + i) * U + u
                        r = u % R
                        for w in ([0, 1] if u == 0 else [u + 1] if u + 1 < U else []):
                            if w % (U // CH) == 0:
                                v.wait_ge(pay_in[w // (U // CH)], 16 * (m + 1))
                            one_hots(m * U + w, w, pay, C_KEY)
                        v.wait_ge(lin_ready, n2 + (NB * U + 1))
                        v.wait_ge(gathered[u], 16 * K * (m + 1))
                        nc.vector.tensor_tensor(s1[:, r], lin(u), rows[:, u].rearrange("p k (s d) -> p s k d", s=2),
                                                ALU.add).then_inc(sum_ready, 1)
                        v.wait_ge(sum_ready, n2 + (NB * U + 1))
                        nc.vector.scalar_tensor_tensor(zr[:, r], s1[:, r, 1], 0.0, wa2r[:].unsqueeze(1).to_broadcast([128, K, D]),
                                                       ALU.max, ALU.mult).then_inc(zr_ready, 1)
                        v.wait_ge(zr_ready, n2 + 1)
                        nc.vector.tensor_reduce(logit[:, r], zr[:, r], AX_X, ALU.add).then_inc(logit_ready, 1)
                        v.wait_ge(att_ready, n2 + 1)
                        nc.vector.tensor_tensor(msg[:, r], s1[:, r, 0], att[:, r].unsqueeze(2).to_broadcast([128, K, D]),
                                                ALU.mult).then_inc(msg_ready, 1)
                v.wait_ge(acc_done, l + EP_L2 + 1)
                nc.vector.tensor_tensor(t1[:], acc3, over_hi(biasr[:]), ALU.add).then_inc(acc_read, 1)
                v.wait_ge(acc_read, l + EP_L2 + 1)
                layer_norm(lk, t1[:], t2[:], t1[:], l + 4)
                lk(nc.vector.tensor_tensor(t2[:], t2[:], over_hi(lngr[:]), ALU.mult))
                lk(nc.vector.tensor_tensor(t2[:], t2[:], over_hi(lnbr[:]), ALU.add))
                lk(nc.vector.tensor_scalar(t2[:], t2[:], floor[:, 0:1], None, ALU.max))
                lk(nc.vector.tensor_tensor(hs[:], hs[:], t2[:], ALU.add))
                v.sem_inc(layer_w_free, 1)
                for _ in range(COUNT - ln[0]):
                    lk(nc.vector.memset(rstd[:, 0:1], 0.0))
            done[0] += COUNT * LAYERS
            link(nc.vector.tensor_tensor(xs[:], xs[:], hs[:], ALU.add))

            layer_norm(link, xs[:], t1[:], t2[:], 4 + LAYERS)
            link(nc.vector.tensor_scalar(hs[:], t1[:], 0.0, None, ALU.max))
            nc.vector.tensor_scalar(bnc[:, 1:2], bnc[:, 1:2], LN_EPS, None, ALU.add)
            nc.vector.tensor_scalar(bnr[:, 3, :], bnr[:, 3, :], LN_EPS, None, ALU.add).then_inc(sqrt_in, 1)
            v.wait_ge(sqrt_out, 6 + LAYERS)
            link(nc.vector.reciprocal(bnc[:, 1:2], bnc[:, 1:2]))
            link(nc.vector.reciprocal(bnr[:, 3, :], bnr[:, 3, :]))
            link(nc.vector.tensor_tensor(bnc[:, 0:1], bnc[:, 0:1], bnc[:, 1:2], ALU.mult))
            link(nc.vector.tensor_tensor(bnr[:, 0, :], bnr[:, 0, :], bnr[:, 3, :], ALU.mult))
            link(nc.vector.tensor_tensor(bnr[:, 2, :], bnr[:, 2, :], bnr[:, 0, :], ALU.mult))
            link(nc.vector.tensor_tensor(bnr[:, 1, :], bnr[:, 1, :], bnr[:, 2, :], ALU.subtract))
            link(nc.vector.tensor_tensor(w3d[:, 0, :], w3s[:, 0:D], w3s[:, D:2 * D], ALU.subtract))
            link(nc.vector.tensor_scalar(w3d[:, 0, :], w3d[:, 0, :], bnc[:, 0:1], None, ALU.mult))
            nc.vector.tensor_scalar(w3d[:, 1, :], w3s[:, D:2 * D], bnc[:, 0:1], None, ALU.mult).then_inc(w_prep, 1)
            v.wait_ge(w_mm, 2 * LAYERS + 1)
            link(nc.vector.tensor_copy(w3T[:], ps[0:D, 7, 0:2 * D]))
            v.sem_inc(hs_ready, 1)
            with v.Fori(0, NP) as i:
                v.wait_ge(proj_done, i + (LAYERS + 1) * NP + 2)
                y = flat[0:LO, 0:PB * 256].rearrange("p (k c) -> p k c", k=PB)
                bl = bass.ds(i * PB, PB)
                nc.vector.tensor_tensor(t2[:, bl, :], y[:, :, 0:D], bnr[:, 1, :].unsqueeze(1).to_broadcast([LO, PB, D]), ALU.add)
                nc.vector.tensor_copy(t1[:, bl, :], y[:, :, D:2 * D]).then_inc(proj_read, 1)
            v.wait_ge(proj_read, (LAYERS + 2) * NP + 1)
            v.sem_inc(node_ready, 1)
            link(nc.vector.tensor_copy(local_b[:, 0], t2[:]))
            link(nc.vector.tensor_tensor(t2[:], t2[:], local_b[:, 0], ALU.subtract))
            link(nc.vector.tensor_copy(local_b[:, 1], t2[:]))
            link(nc.vector.tensor_tensor(t2[:], t2[:], local_b[:, 1], ALU.subtract))
            link(nc.vector.tensor_copy(local_b[:, 2], t2[:]))
            v.sem_inc(local_ready, 1)
            with v.Fori(0, NB) as i:
                m = i + EP_L3 * NB
                for u in range(U):
                    n = i * U + (LAYERS + 1) * NB * U + u
                    for w in ([0, 1] if u == 0 else [u + 1] if u + 1 < U else []):
                        if w % (U // CH) == 0:
                            v.wait_ge(pay_in[w // (U // CH)], 16 * (m + 1))
                        one_hots(m * U + w, w, pay2, C2_KEY)
                    v.wait_ge(lin_ready, n + 1)
                    v.wait_ge(gathered[u], 16 * K * (m + 1))
                    nc.vector.tensor_tensor(s1[:, u % R, 0], lin(u)[:, 0], rows[:, u, :, 0:D], ALU.add).then_inc(sum_ready, 1)
            v.wait_ge(acc_done, EP_L3 + 1)
            nc.vector.tensor_tensor(xs[:], xs[:], acc3, ALU.add).then_inc(node_ready, 1)

        @block.scalar
        def _(a):
            def root(to, frm, n):
                a.wait_ge(sqrt_in, n + 1)
                nc.scalar.activation(to, frm, ACT.Sqrt).then_inc(sqrt_out, 1)

            root(rstd[:], var[:], 0)

            def stage_rows(which):
                G2 = EJ // SG // 2
                key_of = 1 - which

                def group(i, h, wait):
                    js = bass.ds((i * 2 + h) * SG, SG)
                    if wait:
                        a.wait_ge(scattered[h], (i + which * G2) * (16 * SG))
                    nc.scalar.copy(stage_at[:, h, :], pos[:, key_of, js])
                    if which == 0:
                        nc.scalar.copy(stage[:, h, :, 0:DA], at16[:, js, :])
                        nc.scalar.copy(stage[:, h, :, C_ATT3:C_ATT3 + DB], at3[:, js, :])
                        nc.scalar.copy(stage[:, h, :, C_ONE], ones[0:EP, 0:SG])
                        nc.scalar.copy(stage[:, h, :, C_W], wgt[:, js])
                        nc.scalar.copy(stage[:, h, :, C_KEY], lo[:, 1, js])
                        nc.scalar.copy(stage[:, h, :, C_OTHER], key[:, 0, js]).then_inc(staged, 1)
                    else:
                        nc.scalar.copy(stage[:, h, :, C2_KEY], lo[:, 0, js])
                        nc.scalar.copy(stage[:, h, :, C2_OTHER], key[:, 1, js]).then_inc(staged, 1)

                if which == 0:
                    for h in range(2):
                        nc.scalar.copy(stage[:, h, :, C_OTHER + 1:C], ones[0:EP, 0:SG * (C - C_OTHER - 1)].rearrange(
                            "p (j c) -> p j c", j=SG))
                    for h in range(2):
                        group(0, h, False)
                with a.Fori(1 - which, G2) as i:
                    for h in range(2):
                        group(i, h, True)

            a.wait_ge(placed, 1)
            stage_rows(0)
            root(inv_deg[:], inv_deg[:], 1)

            with a.Fori(0, NB) as i:
                def payload(u):
                    n = i * U + u
                    a.wait_ge(slots_free, n + U - R + 1)
                    a.wait_ge(tr_ready, n + 1)
                    nc.scalar.copy(payT[:, u % R, :], payT_ps(6 + u % 2)).then_inc(payT_ready, 1)
                payload(0)
                for u in range(U):
                    if u + 1 < U:
                        payload(u + 1)
                    a.wait_ge(sum_ready, i * U + u + 1)
                    nc.scalar.activation(msg[:, u % R], s1[:, u % R, 0], ACT.Relu).then_inc(msg_ready, 1)

            def project(ph, mlp):
                with a.Fori(0, NP) as i:
                    q = i + ph * NP
                    nc.scalar.copy(st[:], hs[:, bass.ds(i * PB, PB), :]).then_inc(st_ready, 1)
                    a.wait_ge(stT_done, q + 1)
                    a.wait_ge(proj_done, q + 1)
                    tp = flat[0:D, 4 * 512:4 * 512 + PB * 128].rearrange("p (k c) -> p k c", k=PB)
                    nc.scalar.copy(hT[:, :, 0:LO], tp[:, :, 0:LO]).then_inc(hT_ready, 1)
                    if mlp:
                        a.wait_ge(mlp_done, i + 1)
                        up = flat[0:D, 0:PB * 128].rearrange("p (k c) -> p k c", k=PB)
                        nc.scalar.activation(uT[:, :, 0:LO], up[:, :, 0:LO], ACT.Gelu, bias=b1c[:, 0:1]).then_inc(uT_ready, 1)

            a.wait_ge(hs_ready, 1)
            project(0, True)
            root(rstd[:], var[:], 2)
            stage_rows(1)
            root(rstd[:], var[:], 3)

            def transposed(u, n2, n):
                a.wait_ge(oh_ready, n + 1)
                a.wait_ge(slots_free, n + U - R + 1)
                nc.scalar.copy(ohb[:, u % R], oh[:, u % R]).then_inc(ohb_ready, 1)

            with a.Fori(0, LAYERS) as l:
                a.wait_ge(hs_ready, l + 2)
                project(l + 1, False)
                with a.Fori(0, NB) as i:
                    m = (l + EP_L2) * NB + i

                    def prepare(u):
                        n2 = (l * NB + i) * U + u
                        n = m * U + u
                        r = u % R
                        a.wait_ge(slots_free, n + U - R + 1)
                        a.wait_ge(tr_ready, n2 + (NB * U + 1))
                        nc.scalar.copy(payT[:, r, :], payT_ps(6)).then_inc(payT_ready, 1)
                        transposed(u, n2, n)
                        a.wait_ge(hid_done, n2 + 1)
                        nc.scalar.activation(hid[:, r], hid_ps, ACT.Relu).then_inc(hid_ready, 1)
                        a.wait_ge(ohT_done, n2 + 1)
                        nc.scalar.copy(ohT[:, r], ohT_ps).then_inc(ohT_ready, 1)
                    prepare(0)
                    for u in range(U):
                        if u + 1 < U:
                            prepare(u + 1)
                        a.wait_ge(logit_ready, (l * NB + i) * U + u + 1)
                        nc.scalar.activation(att[:, u % R], logit[:, u % R], ACT.Sigmoid, bias=ba2c[:, 0:1]).then_inc(att_ready, 1)
                root(rstd[:], var[:], l + 4)
            root(rstd[:], var[:], 4 + LAYERS)
            a.wait_ge(sqrt_in, 6 + LAYERS)
            nc.scalar.activation(bnc[:, 1:2], bnc[:, 1:2], ACT.Sqrt)
            nc.scalar.activation(bnr[:, 3, :], bnr[:, 3, :], ACT.Sqrt).then_inc(sqrt_out, 1)

            a.wait_ge(hs_ready, 2 + LAYERS)
            project(1 + LAYERS, False)
            with a.Fori(0, NB) as i:
                def prepare3(u):
                    n2 = i * U + LAYERS * NB * U + u
                    transposed(u, n2, i * U + EP_L3 * NB * U + u)
                    a.wait_ge(ohT_done, n2 + 1)
                    nc.scalar.copy(ohT[:, u % R], ohT_ps).then_inc(ohT_ready, 1)
                prepare3(0)
                for u in range(U):
                    if u + 1 < U:
                        prepare3(u + 1)
                    a.wait_ge(sum_ready, i * U + (LAYERS + 1) * NB * U + u + 1)
                    nc.scalar.activation(msg[:, u % R], s1[:, u % R, 0], ACT.Silu).then_inc(msg_ready, 1)

        @block.tensor
        def _(pe):
            def mm(to, lhsT, rhs, start=True, stop=True):
                return nc.tensor.matmul(to, lhsT, rhs, start=start, stop=stop, skip_group_check=True)

            pe.sem_inc(proj_done, 1)
            pe.wait_ge(counted, 1)
            flat_cnt = cnt[:].rearrange("p s h -> p (s h)")
            mm(ps[0:EP, 7, 0:2 * HI], before[0:EP, 0:EP], flat_cnt)
            mm(ps[0:EP, 7, 2 * HI:4 * HI], ones[0:EP, 0:EP], flat_cnt).then_inc(prefixed, 1)

            mm(ps[0:LO, 6, 0:2 * HI], zeros[0:EP, 0:LO], zeros[0:EP, 0:2 * HI], stop=False).then_inc(deg_mm, 2)
            G2 = EJ // SG // 2
            for s in range(2):
                with pe.Fori(0, G2) as i:
                    for h in range(2):
                        pe.wait_ge(deg_oh, (i + s * G2) * 2 + h + 1)
                        for j in range(SG):
                            ins = mm(ps[0:LO, 6, s * HI:(s + 1) * HI], oh_lo[:, h, j, :], oh_hi[:, h, j, :], start=False, stop=False)
                        ins.then_inc(deg_mm, 1)
            mm(ps[0:LO, 6, 0:2 * HI], zeros[0:EP, 0:LO], zeros[0:EP, 0:2 * HI], start=False).then_inc(deg_ready, 1)
            pe.wait_ge(placed, 2)
            pe.wait_ge(deg_read, 1)

            def clear(ep):
                if not (isinstance(ep, int) and ep == 0):
                    pe.wait_ge(acc_read, ep)
                for b in range(4):
                    w = min(512, HI * D - b * 512)
                    ins = mm(ps[0:LO, b, 0:w], zeros_b[:, 0:LO], zeros_b[:, 0:w], stop=False)
                return ins

            def finish_pass():
                mm(ps[0:LO, 3, 0:HI * D - 3 * 512], zeros_b[:, 0:LO], zeros_b[:, 0:HI * D - 3 * 512],
                   start=False).then_inc(acc_done, 1)

            def block_of(key_of, i, u, k):
                return pe.value_load(blk[0:1, key_of, bass.ds(i * BODY + (u * K + k), 1)], min_val=0, max_val=(HI - 1) * D)

            def add_up(i, n, u, values, offs):
                for k in range(K):
                    ins = mm(acc[0:LO, bass.ds(offs[k], D)], oh[:, u % R, k, :], values(k), start=False, stop=False)
                ins.then_inc(slots_free, 1)

            clear(0).then_inc(slots_free, U)
            with pe.Fori(0, NB) as i:
                def turn(u):
                    if u % (U // CH) == 0:
                        pe.wait_ge(pay_in[u // (U // CH)], 16 * (i + 1))
                    j = u * K % CT
                    nc.tensor.transpose(payT_ps(6 + u % 2), pay[:, u // (U // CH), j:j + K, :].rearrange("p k c -> p (k c)"),
                                        ident[:]).then_inc(tr_ready, 1)

                def sum_up(u):
                    n = i * U + u
                    offs = [block_of(1, i, u, k) for k in range(K)]
                    pe.wait_ge(oh_ready, n + 1)
                    pe.wait_ge(msg_ready, n + 1)
                    add_up(i, n, u, lambda k: msg[:, u % R, k, :], offs)
                turn(0)
                for u in range(U):
                    if u + 1 < U:
                        turn(u + 1)
                    pe.wait_ge(payT_ready, i * U + u + 1)
                    mm(ps[:, 4 + u % 2, 0:K * D], payT[:, u % R, :], wl0[:].rearrange("p k d -> p (k d)")).then_inc(lin_ready, 1)
                    if u >= 1:
                        sum_up(u - 1)
                sum_up(U - 1)
            finish_pass()

            def turn_blocks(ph, i):
                q = i + ph * NP
                hold(pe, st_ready, q + 1)
                for k in range(PB):
                    ins = nc.tensor.transpose(flat[0:D, 4 * 512 + k * 128:4 * 512 + k * 128 + LO], st[:, k, :], ident[0:LO, 0:LO])
                ins.then_inc(stT_done, 1)
                pe.wait_ge(hT_ready, q + 1)
                hold(pe, proj_read, q + 1)

            with pe.Fori(0, NP) as i:
                turn_blocks(0, i)
                mm(ps[0:D, 0, :].rearrange("p (k c) -> p k c", c=128)[:, :, 0:LO], w1s[:], hT[:, 0:4, 0:LO])
                mm(ps[0:D, 1, 0:LO], w1s[:], hT[:, 4, 0:LO]).then_inc(mlp_done, 1)
                hold(pe, uT_ready, i + 1)
                for k in range(PB):
                    ins = mm(ps[0:LO, 2, k * D:(k + 1) * D], uT[:, k, 0:LO], w2s[:])
                ins.then_inc(proj_done, 1)

            pe.wait_ge(proj_read, NP + 1)
            with pe.Fori(0, STEPS) as s:
                clear(s + 1)
                with pe.Fori(0, NB) as i:
                    m = (s + EP_L1) * NB + i
                    for u in range(U):
                        offs = [block_of(1, i, u, k) for k in range(K)]
                        pe.wait_ge(oh_ready, m * U + u + 1)
                        pe.wait_ge(gathered[u], 16 * K * (m + 1))
                        add_up(i, m * U + u, u, lambda k: rows[:, u, k, 0:D], offs)
                finish_pass()

            def project(ph, w, width):
                with pe.Fori(0, NP) as i:
                    turn_blocks(ph, i)
                    for k in range(PB):
                        ins = mm(flat[0:LO, k * 256:k * 256 + width], hT[:, k, 0:LO], w[:, 0:width])
                    ins.then_inc(proj_done, 1)

            def turn_one_hots(u, n2, last):
                pe.wait_ge(ohb_ready, n2 + 1)
                for k in range(K):
                    ins = nc.tensor.transpose(ohT_ps[:, k, :], ohb[:, u % R, k, :], ident_b[:])
                ins.then_inc(ohT_done, 1)

            def add_local(u, half, offs, start):
                for k in range(K):
                    for part in range(3):
                        table_part = local_b[:, part].rearrange("p h d -> p (h d)")
                        ins = mm(lin(u)[:, half, k, :], ohT[:, u % R, k, :], table_part[:, bass.ds(offs[k], D)],
                                 start=start and part == 0, stop=part == 2)
                return ins

            with pe.Fori(0, LAYERS) as l:
                hold(pe, layer_w, 16 * LW * (l + 1))
                nc.tensor.transpose(ps[0:D, 7, 0:D], wn[:], ident[0:D, 0:D]).then_inc(w_mm, 1)
                hold(pe, w_prep, l + 1)
                mm(ps[0:D, 7, 128:128 + 2 * D], wnT[:], wa1[:].rearrange("p s d -> p (s d)")).then_inc(w_mm, 1)
                hold(pe, hs_ready, l + 2)
                project(l + 1, wcat, 3 * D)
                hold(pe, proj_read, (l + 2) * NP + 1)
                clear(l + EP_L2)
                hold(pe, local_ready, l + 1)
                with pe.Fori(0, NB) as i:
                    m = (l + EP_L2) * NB + i

                    def turn(u):
                        if u % (U // CH) == 0:
                            pe.wait_ge(pay_in[u // (U // CH)], 16 * (m + 1))
                        j = u * K % CT
                        nc.tensor.transpose(payT_ps(6), pay[:, u // (U // CH), j:j + K, :].rearrange("p k c -> p (k c)"),
                                            ident[:]).then_inc(tr_ready, 1)

                    def hidden(u):
                        n2 = (l * NB + i) * U + u
                        pe.wait_ge(payT_ready, n2 + (NB * U + 1))
                        for q in range(K // 2):
                            ins = mm(hid_ps[:, q, :], wt[:, q, :], payT[:, u % R, :])
                        ins.then_inc(hid_done, 1)
                        turn_one_hots(u, n2, None)

                    def products(u):
                        n2 = (l * NB + i) * U + u
                        pe.wait_ge(hid_ready, n2 + 1)
                        for q in range(K // 2):
                            mm(ps[:, 4 + u % 2, q * 128:(q + 1) * 128], hid[:, u % R, q, :], we2[:])
                        mm(ps[:, 4 + u % 2, K * D:2 * K * D], payT[:, u % R, :], wz[:].rearrange("p k d -> p (k d)"), stop=False)
                        add_local(u, 1, offs[u], False).then_inc(lin_ready, 1)

                    def sum_up(u):
                        n2 = (l * NB + i) * U + u
                        pe.wait_ge(msg_ready, n2 + (NB * U + 1))
                        add_up(i, m * U + u, u, lambda k: msg[:, u % R, k, :], offs[u])
                    offs = {0: [block_of(1, i, 0, k) for k in range(K)]}
                    turn(0)
                    hidden(0)
                    for u in range(U):
                        pe.wait_ge(ohT_ready, (l * NB + i) * U + u + 1)
                        if u + 1 < U:
                            turn(u + 1)
                        products(u)
                        if u + 1 < U:
                            hidden(u + 1)
                        if u >= 1:
                            sum_up(u - 1)
                        if u + 1 < U:
                            offs[u + 1] = [block_of(1, i, u + 1, k) for k in range(K)]
                    sum_up(U - 1)
                finish_pass()

            pe.wait_ge(w_prep, LAYERS + 1)
            for h in range(2):
                ins = nc.tensor.transpose(ps[0:D, 7, h * D:(h + 1) * D], w3d[:, h, :], ident[0:D, 0:D])
            ins.then_inc(w_mm, 1)
            pe.wait_ge(hs_ready, LAYERS + 2)
            project(LAYERS + 1, w3T, 2 * D)
            pe.wait_ge(proj_read, (LAYERS + 2) * NP + 1)
            clear(EP_L3)
            pe.wait_ge(local_ready, LAYERS + 1)
            with pe.Fori(0, NB) as i:
                m = i + EP_L3 * NB

                def products3(u):
                    pe.wait_ge(ohT_ready, i * U + LAYERS * NB * U + u + 1)
                    add_local(u, 0, offs[u], True).then_inc(lin_ready, 1)

                def sum_up3(u):
                    pe.wait_ge(msg_ready, i * U + (LAYERS + 1) * NB * U + u + 1)
                    add_up(i, m * U + u, u, lambda k: msg[:, u % R, k, :], offs[u])
                offs = {0: [block_of(0, i, 0, k) for k in range(K)]}
                turn_one_hots(0, i * U + LAYERS * NB * U, None)
                for u in range(U):
                    products3(u)
                    if u + 1 < U:
                        turn_one_hots(u + 1, i * U + LAYERS * NB * U + u + 1, None)
                    if u >= 1:
                        sum_up3(u - 1)
                    if u + 1 < U:
                        offs[u + 1] = [block_of(0, i, u + 1, k) for k in range(K)]
                sum_up3(U - 1)
            finish_pass()


_INS = ['x', 'src', 'dst', 'edge_attr_16', 'edge_attr_3', 'edge_weight',
        'L0_gnn_We', 'L0_gnn_be', 'L0_gnn_W1', 'L0_gnn_b1', 'L0_gnn_W2', 'L0_gnn_b2',
        'L2_gnn_W_node', 'L2_gnn_W_e1', 'L2_gnn_b_e1', 'L2_gnn_W_e2', 'L2_gnn_b_e2', 'L2_gnn_Wa1', 'L2_gnn_ba1',
        'L2_gnn_Wa2', 'L2_gnn_ba2', 'L2_gnn_bias', 'L2_gnn_ln_g', 'L2_gnn_ln_b',
        'L3_gnn_W', 'L3_gnn_bn_gamma', 'L3_gnn_bn_beta', 'L3_gnn_bn_mean', 'L3_gnn_bn_var']
_OUTS = [((N, D), 'float32')]


def kernel(**inputs):
    import numpy as _np
    import concourse.bacc as _bacc
    from concourse import mybir as _mybir
    from concourse.bass_utils import run_bass_kernel_spmd as _run

    nc = _bacc.Bacc("TRN2", target_bir_lowering=False, num_devices=1)
    arrays, args = {}, []
    for name in _INS:
        a = _np.ascontiguousarray(inputs[name])
        arrays[f"in_{name}_dram"] = a
        args.append(nc.dram_tensor(f"in_{name}_dram", a.shape, _mybir.dt.from_np(a.dtype), kind="ExternalInput").ap())
    for i, (shape, dtype) in enumerate(_OUTS):
        dt = _mybir.dt.from_np(_np.dtype(dtype))
        args.append(nc.dram_tensor(f"out_{i}_dram", shape, dt, kind="ExternalOutput").ap())
    gnn_kernel(nc, *args)
    r = _run(nc, [arrays], core_ids=[0])
    got = tuple(r.results[0][f"out_{i}_dram"] for i in range(len(_OUTS)))
    return got[0]
```

```python
from contextlib import ExitStack

import concourse.bass as bass
from concourse import mybir

F32 = mybir.dt.float32
BF16 = mybir.dt.bfloat16
F16 = mybir.dt.float16
I16 = mybir.dt.int16
I32 = mybir.dt.int32
ALU = mybir.AluOpType
ACT = mybir.ActivationFunctionType
AX_X = mybir.AxisListType.X

N, E, D = 3125, 50000, 64
LO, HI = 125, 25
EP, EJ = 125, 400
DA, DB = 16, 3
T = 416
K = 4
U = 8
CH = 2
UC = U // CH
CT = K * UC
BODY = K * U
NB = T // BODY
assert NB * BODY == T and T >= E // 128 + HI
R = 4
STEPS, ALPHA = 10, 0.1
LAYERS = 3
LN_EPS = 1e-5
C = 24
C_ATT3, C_ONE, C_W, C_KEY, C_OTHER = DA, DA + DB, DA + DB + 1, DA + DB + 2, DA + DB + 3
C2, C2_KEY, C2_OTHER = 4, 0, 1
C3, C3_ROW, C3_COL, C3_W = 4, 0, 1, 2
SG = 8
G2 = EJ // SG // 2
ROUND = 12582912.0
CB = 4
CG = -(-HI // CB)
CW = CB * LO
BINS = CG * HI
BS = 8
T3 = 576
assert T3 % BS == 0 and T3 >= E // 128 + BINS and HI - (CG - 1) * CB == 1
EV = 5
assert HI % EV == 0
NR = 7
GB = 3
NG = (HI - NR) // GB
assert NR + NG * GB == HI
SEGS = (BINS, HI, HI)
SEG_AT = (0, BINS, BINS + HI)
BUCKETS = sum(SEGS)
SEG_T = (T3, T, T)
Q = 5
EP_L0, EP_L2, EP_L3 = 0, 1, 1 + LAYERS
PB = 5
NP = HI // PB


def gnn_kernel(nc, x, src, dst, edge_attr_16, edge_attr_3, edge_weight,
               We, be, W1, b1, W2, b2,
               W_node, W_e1, b_e1, W_e2, b_e2, Wa1, ba1, Wa2, ba2, bias2, ln_g, ln_b,
               W3, bn_gamma, bn_beta, bn_mean, bn_var, out):
    with ExitStack() as ctx:
        def sb(name, shape, dt=F32):
            return ctx.enter_context(nc.sbuf_tensor(name, shape, dt))

        def sem(name):
            return ctx.enter_context(nc.semaphore(name))

        rows_dst = nc.dram_tensor("rows_dst", [128 * T, C], F32).ap()
        rows_src = nc.dram_tensor("rows_src", [128 * T, C2], F32).ap()
        rows_bin = nc.dram_tensor("rows_bin", [128 * T3, C3], F32).ap()
        dense = nc.dram_tensor("dense", [CG, 128, HI, CW], F32).ap()
        table = nc.dram_tensor("table", [N, D], F32).ap()
        table2 = nc.dram_tensor("table2", [N, 2 * D], F32).ap()

        iota_row = sb("iota_row", [128, 128])
        iota_row_b = sb("iota_row_b", [128, 128], BF16)
        iota_col_h = sb("iota_col_h", [128, CW], F16)
        iota_p = sb("iota_p", [128, 1])
        ident = sb("ident", [128, 128])
        ident_b = sb("ident_b", [128, 128], BF16)
        before = sb("before", [128, 128])
        ones = sb("ones", [128, 128])
        ones_b = sb("ones_b", [128, EJ], BF16)
        zeros = sb("zeros", [128, CW])
        zeros_b = sb("zeros_b", [128, 512], BF16)
        blk = sb("blk", [1, 2, T], I32)
        blk_id = sb("blk_id", [1, T], I32)
        lo_src = sb("lo_src", [EP, EJ])
        dst_f = sb("dst_f", [EP, EJ])
        pos_src = sb("pos_src", [EP, EJ], I32)
        stage = sb("stage", [EP, 2, SG, C])
        stage_at = sb("stage_at", [EP, 2, SG], I32)

        xs = sb("xs", [LO, HI, D])
        hs = sb("hs", [LO, HI, D])
        hs2 = sb("hs2", [LO, HI, D])
        fs = sb("fs", [LO, HI, D])
        t1 = sb("t1", [LO, HI, D])
        t2 = sb("t2", [LO, HI, D])
        mean = sb("mean", [LO, HI])
        var = sb("var", [LO, HI])
        rstd = sb("rstd", [LO, HI])
        deg_bins = sb("deg_bins", [128, BINS])
        deg = sb("deg", [LO, 2, HI])
        inv_deg = sb("inv_deg", [LO, 2, HI])
        keep = sb("keep", [LO, HI])
        last_in = sb("last_in", [LO, HI])

        wl0 = sb("wl0", [K * C, K, D])
        w1s = sb("w1s", [D, D])
        w2s = sb("w2s", [D, D])
        b1c = sb("b1c", [D, 1])
        b2r = sb("b2r", [LO, D])
        wz = sb("wz", [K * C, K, D])
        wt = sb("wt", [K * C, K // 2, 2 * D])
        we2 = sb("we2", [128, 2 * D])
        wn = sb("wn", [D, D])
        wnT = sb("wnT", [D, D])
        wa1 = sb("wa1", [D, 2, D])
        wcat = sb("wcat", [D, 3 * D])
        wa2r = sb("wa2r", [128, D])
        ba2c = sb("ba2c", [128, 1])
        be2r = sb("be2r", [LO, D])
        biasr = sb("biasr", [LO, D])
        lngr = sb("lngr", [LO, D])
        lnbr = sb("lnbr", [LO, D])
        floors = sb("floors", [LO, LAYERS])
        floor = sb("floor", [LO, 1])
        w3s = sb("w3s", [D, 2 * D])
        bnc = sb("bnc", [D, 2])
        bnr = sb("bnr", [LO, 4, D])
        w3d = sb("w3d", [D, 2, D])
        w3T = sb("w3T", [D, 2 * D])

        WORDS = 35400
        arena = sb("arena", [128, WORDS])
        used = [0]

        def carve(shape, dt=F32):
            n = 1
            for d in shape[1:]:
                n *= d
            w = -(-n // 2) if dt in (BF16, F16) else n
            assert used[0] + w <= WORDS, (used[0], w)
            a = arena[0:shape[0], used[0]:used[0] + w]
            used[0] += w
            if dt != F32:
                a = a.bitcast(dt)[:, 0:n]
            if len(shape) > 2:
                names = "abcd"[:len(shape) - 1]
                a = a.rearrange(f"p ({' '.join(names)}) -> p {' '.join(names)}",
                                **{x: d for x, d in zip(names, shape[1:])})
            return a

        key = carve([EP, 2, EJ])
        lo = carve([EP, 2, EJ])
        hi = carve([EP, 2, EJ])
        col = carve([EP, EJ])
        keys_b = carve([EP, 3, EJ], BF16)
        ta = carve([EP, 2, EJ])
        grp = ta[:, 1, :]
        picked = ta[:, 1, 0:EP]
        ohk = carve([EP, Q, EJ], BF16)
        pos = hi[:, 0, :]
        pos_i = carve([EP, 2, EJ], I32)
        cnt = carve([EP, BUCKETS])
        tiles = carve([EP, BUCKETS])
        tsum = carve([EP, BUCKETS])
        base = carve([EP, BUCKETS])
        iota_t = carve([128, T3])
        start_col = carve([128, 4])
        begun = carve([128, 2, T3], BF16)
        bin_of = carve([1, T3])
        turn_of = carve([1, T3])
        bank_of = carve([1, T3], I32)
        need = carve([1, T3], I32)
        bin_end = carve([1, BINS], I32)
        wgt = carve([EP, EJ])
        at3 = carve([EP, EJ, DB])
        edge_rows = carve([EP, EJ, C])
        bin_rows = carve([EP, EJ, C3])
        key_i = bin_rows.rearrange("p j c -> p (j c)")[:, 0:2 * EJ].bitcast(I32).rearrange("p (s j) -> p s j", s=2)
        fills_from = used[0]
        fill = carve([128, T // 8, C])
        fill2 = carve([128, T, C2])
        fill3 = carve([128, T3, C3])
        used[0] = fills_from
        bin_in = carve([128, T3, C3])
        scal = carve([128, T3, 5])
        used[0] = max(used[0], fills_from + T // 8 * C + T * C2 + T3 * C3)
        at_from = used[0]
        at16 = carve([EP, EJ, DA])
        used[0] = at_from
        sc = carve([128, BS, 5])
        lhs = carve([128, BS, 3, 128], BF16)
        rhs = carve([128, BS, CW], BF16)
        ev = carve([128, EV, CW])
        wpart = begun.rearrange("p s t -> p (s t)")[:, 0:T3]

        used[0] = 0
        pay = carve([128, CH, CT, C])
        pay2 = carve([128, CH, CT, C2])
        at = carve([128, CH, CT], I32)
        rows = carve([128, U, K, 2 * D])
        oh = carve([128, R, K, LO])
        ohb = carve([128, R, K, LO], BF16)
        ohT = carve([LO, R, K, 128], BF16)
        payT = carve([K * C, R, 128])
        hid = carve([128, R, K // 2, 128])
        s1 = carve([128, R, 2, K, D])
        zr = carve([128, R, K, D])
        logit = carve([128, R, K])
        att = carve([128, R, K])
        msg = carve([128, R, K, D])
        tab2 = carve([LO, HI, 2 * D])
        local_b = carve([LO, 3, HI, D], BF16)

        assert used[0] <= (CG - 1) * NR * CW + HI * LO
        used[0] = 0
        kept = carve([128, CG - 1, NR, CW])
        kept_last = carve([128, HI, LO])
        slots_from = used[0]
        slots = carve([128, NG, GB, CW])
        oT = carve([128, 2, CW])
        oT_last = carve([128, LO])
        used[0] = slots_from
        st = carve([LO, PB, D])
        hT = carve([D, PB, 128])
        uT = carve([D, PB, 128])

        ps = ctx.enter_context(nc.psum_tensor("ps", [128, 8, 512], F32))
        flat = ps[:].rearrange("p b c -> p (b c)")
        acc = flat[:, 0:HI * D]
        acc3 = acc[0:LO, :].rearrange("p (h d) -> p h d", d=D)

        def lin(u):
            return ps[:, 4 + u % 2, :].rearrange("p (s k d) -> p s k d", s=2, k=K)

        def payT_ps(bank):
            return ps[0:K * C, bank, 0:128]
        hid_ps = ps[:, 7, 0:256].rearrange("p (q e) -> p q e", q=K // 2)
        ohT_ps = ps[0:LO, 6, 128:128 + K * 64].bitcast(BF16).rearrange("p (k e) -> p k e", k=K)

        loaded = sem("loaded")
        consts = sem("consts")
        dve_consts = sem("dve_consts")
        filled = sem("filled")
        dve_step = sem("dve_step")
        act_step = sem("act_step")
        counted = sem("counted")
        prefixed = sem("prefixed")
        node_ready = sem("node_ready")
        table_in = sem("table_in")
        local_ready = sem("local_ready")
        pay_in = [sem(f"pay_in{c}") for c in range(CH)]
        at_ready = sem("at_ready")
        gathered = [sem(f"gathered{u}") for u in range(U)]
        slots_free = sem("slots_free")
        acc_done = sem("acc_done")
        acc_read = sem("acc_read")
        oh_ready = sem("oh_ready")
        tr_ready = sem("tr_ready")
        payT_ready = sem("payT_ready")
        lin_ready = sem("lin_ready")
        sum_ready = sem("sum_ready")
        msg_ready = sem("msg_ready")
        ohb_ready = sem("ohb_ready")
        ohT_done = sem("ohT_done")
        ohT_ready = sem("ohT_ready")
        hid_done = sem("hid_done")
        hid_ready = sem("hid_ready")
        zr_ready = sem("zr_ready")
        logit_ready = sem("logit_ready")
        att_ready = sem("att_ready")
        st_ready = sem("st_ready")
        stT_done = sem("stT_done")
        hT_ready = sem("hT_ready")
        mlp_done = sem("mlp_done")
        uT_ready = sem("uT_ready")
        proj_done = sem("proj_done")
        proj_read = sem("proj_read")
        layer_w = sem("layer_w")
        layer_w_free = sem("layer_w_free")
        w_prep = sem("w_prep")
        w_mm = sem("w_mm")
        sqrt_in = sem("sqrt_in")
        sqrt_out = sem("sqrt_out")
        hs_ready = sem("hs_ready")
        out_done = sem("out_done")
        held = sem("held")

        starts_ready = sem("starts_ready")
        starts_summed = sem("starts_summed")
        blk_ready = sem("blk_ready")
        loaded0 = sem("loaded0")
        at_loaded = sem("at_loaded")
        lo_ready = sem("lo_ready")
        placed = sem("placed")
        made_rows = sem("made_rows")
        staged = sem("staged")
        scattered = [sem("scattered0"), sem("scattered1")]
        bin_loaded = sem("bin_loaded")
        op_ready = sem("op_ready")
        built = sem("built")
        bank_free = sem("bank_free")
        ev_ready = sem("ev_ready")
        ev_out = [sem(f"ev_out{g}") for g in range(EV)]
        kept_in = sem("kept_in")
        layer1_start = sem("layer1_start")
        slot_in = [sem(f"slot_in{g}") for g in range(NG)]
        slot_used = sem("slot_used")
        group_done = sem("group_done")
        oT_ready = sem("oT_ready")
        turned = sem("turned")
        turned_read = sem("turned_read")
        h_ready = sem("h_ready")

        loads = [(xs[:], x.rearrange("(p h) d -> p h d", p=LO)),
                 (w1s[:], W1), (w2s[:], W2), (b1c[:], b1.unsqueeze(1)),
                 (b2r[:], b2.partition_broadcast(LO)), (w3s[:], W3),
                 (bnc[:, 0:1], bn_gamma.unsqueeze(1)), (bnc[:, 1:2], bn_var.unsqueeze(1))]
        loads += [(bnr[:, i, :], v.partition_broadcast(LO))
                  for i, v in enumerate((bn_gamma, bn_beta, bn_mean, bn_var))]
        block_loads = []
        for k in range(K):
            block_loads += [(wl0[C * k:C * k + DA, k, :], We), (wl0[C * k + C_ONE:C * k + C_ONE + 1, k, :], be.unsqueeze(0))]

        def layer_loads(l):
            a = [(wn[:], W_node[l]), (wa1[:, 0, :], Wa1[l, D:2 * D]), (wa1[:, 1, :], Wa1[l, 0:D]),
                 (we2[0:D, 0:D], W_e2[l]), (we2[D:2 * D, D:2 * D], W_e2[l]),
                 (wa2r[:], Wa2[l].rearrange("c o -> (c o)").partition_broadcast(128)),
                 (ba2c[:], ba2[l].partition_broadcast(128)),
                 (be2r[:], b_e2[l].partition_broadcast(LO)), (biasr[:], bias2[l].partition_broadcast(LO)),
                 (lngr[:], ln_g[l].partition_broadcast(LO)), (lnbr[:], ln_b[l].partition_broadcast(LO))]
            for k in range(K):
                q, f = k // 2, (k % 2) * D
                r, o = C * k + C_ATT3, C * k + C_ONE
                a += [(wz[r:r + DB, k, :], Wa1[l, 2 * D:2 * D + DB]), (wz[o:o + 1, k, :], ba1[l].unsqueeze(0)),
                      (wt[r:r + DB, q, f:f + D], W_e1[l]), (wt[o:o + 1, q, f:f + D], b_e1[l].unsqueeze(0))]
            return a
        LW = 11 + 4 * K

        def hold(eng, semaphore, value):
            eng.wait_ge(semaphore, value)
            eng.sem_inc(held, 1)

        block = ctx.enter_context(nc.Block())

        @block.sync
        def _(sp):
            sp.dma_start(key_i[:, 1, :], dst.rearrange("(p j) -> p j", p=EP)).then_inc(loaded0, 16)
            sp.dma_start(key_i[:, 0, :], src.rearrange("(p j) -> p j", p=EP)).then_inc(loaded0, 16)
            for to, frm in loads:
                sp.dma_start(to, frm).then_inc(loaded, 16)
            sp.dma_start(wgt, edge_weight.rearrange("(p j) -> p j", p=EP)).then_inc(at_loaded, 16)
            sp.dma_start(at16, edge_attr_16.rearrange("(p j) c -> p j c", p=EP)).then_inc(at_loaded, 16)
            sp.dma_start(at3, edge_attr_3.rearrange("(p j) c -> p j c", p=EP)).then_inc(at_loaded, 16)
            sp.wait_ge(consts, 1)
            for to, frm in block_loads:
                sp.dma_start(to, frm).then_inc(loaded, 16)
            sp.dma_start(rows_bin.rearrange("(p t) c -> p t c", p=128), fill3).then_inc(filled, 16)
            by_part = rows_dst.rearrange("(p t) c -> p t c", p=128)
            for i in range(8):
                n = T // 8
                sp.dma_start(by_part[:, i * n:(i + 1) * n, :], fill).then_inc(filled, 16)
            sp.dma_start(rows_src.rearrange("(p t) c -> p t c", p=128), fill2).then_inc(filled, 16)
            sp.wait_ge(filled, 16 * 10)
            for h in range(2):
                sp.wait_ge(scattered[h], 16 * SG * G2)
            sp.dma_start(bin_in, rows_bin.rearrange("(p t) c -> p t c", p=128)).then_inc(bin_loaded, 16)
            def write_table(to, frm, n):
                sp.wait_ge(node_ready, n + 1)
                sp.dma_start(to, frm).then_inc(table_in, 16)

            def stream(ep, frm, to):
                view = frm.rearrange("(p t) c -> p t c", p=128)
                with sp.Fori(0, NB) as i:
                    m = ep * NB + i
                    for c in range(CH):
                        sp.wait_ge(slots_free, m * U + (c + 1) * (U // CH))
                        sp.dma_start(to[:, c, :, :], view[:, bass.ds(i * BODY + c * CT, CT), :]).then_inc(pay_in[c], 16)

            table_sb = table.rearrange("(p h) d -> p h d", p=LO)
            table2_sb = table2.rearrange("(p h) d -> p h d", p=LO)
            write_table(table_sb, hs[:], EP_L0)
            for h in range(2):
                sp.wait_ge(scattered[h], 2 * 16 * SG * G2)
            for g in range(EV):
                sp.wait_ge(ev_out[g], 16 * (BINS // EV + 1))
            stream(EP_L0, rows_dst, pay)

            sp.wait_ge(acc_done, 1)
            for c in range(CG - 1):
                sp.dma_start(kept[:, c], dense[c, :, 0:NR, :]).then_inc(kept_in, 16)
            sp.dma_start(kept_last, dense[CG - 1, :, :, 0:LO]).then_inc(kept_in, 16)
            sp.wait_ge(layer1_start, 1)
            with sp.Fori(0, STEPS) as s:
                with sp.Fori(0, CG - 1) as c:
                    for g in range(NG):
                        sp.wait_ge(slot_used, (s * (CG - 1) + c) * NG + (g + 1))
                        sp.dma_start(slots[:, g], dense[bass.ds(c, 1), :, NR + g * GB:NR + (g + 1) * GB, :].rearrange(
                            "o p b w -> (o p) b w")).then_inc(slot_in[g], 16)
            with sp.Fori(0, LAYERS) as l:
                sp.wait_ge(layer_w_free, l + 1)
                for to, frm in layer_loads(l):
                    sp.dma_start(to, frm).then_inc(layer_w, 16)
                write_table(table2_sb, tab2, l + EP_L2)
                stream(l + EP_L2, rows_dst, pay)
            write_table(table_sb, t1[:], EP_L3)
            for h in range(2):
                sp.wait_ge(scattered[h], 3 * 16 * SG * G2)
            stream(EP_L3, rows_src, pay2)
            sp.wait_ge(node_ready, EP_L3 + 2)
            sp.dma_start(out.rearrange("(p h) d -> p h d", p=LO), xs[:]).then_inc(out_done, 16)
            sp.wait_ge(out_done, 16)

        @block.gpsimd
        def _(pool):
            nc.gpsimd.iota(iota_row[:], [[1, 128]], base=0, channel_multiplier=0, allow_small_or_imprecise_dtypes=True)
            nc.gpsimd.iota(iota_p[:], [[0, 1]], base=0, channel_multiplier=1, allow_small_or_imprecise_dtypes=True)
            nc.gpsimd.iota(iota_t, [[1, T3]], base=0, channel_multiplier=0, allow_small_or_imprecise_dtypes=True)
            nc.gpsimd.memset(wl0[:], 0.0)
            nc.gpsimd.memset(wz[:], 0.0)
            nc.gpsimd.memset(wt[:], 0.0)
            nc.gpsimd.memset(we2[:], 0.0)
            nc.gpsimd.memset(floors[:, 0:LAYERS - 1], 0.0)
            nc.gpsimd.memset(floors[:, LAYERS - 1:LAYERS], -3.0e38)
            nc.gpsimd.memset(fill[:, :, 0:C_KEY], 0.0)
            nc.gpsimd.memset(fill[:, :, C_KEY:C_KEY + 1], -1.0)
            nc.gpsimd.memset(fill[:, :, C_KEY + 1:C], 0.0)
            nc.gpsimd.memset(fill2[:, :, C2_KEY:C2_KEY + 1], -1.0)
            nc.gpsimd.memset(fill2[:, :, C2_KEY + 1:C2], 0.0)
            nc.gpsimd.memset(fill3[:, :, C3_ROW:C3_ROW + 1], -1.0)
            nc.gpsimd.memset(fill3[:, :, C3_ROW + 1:C3], 0.0)
            pool.drain()
            pool.sem_inc(consts, 1)

            def scatter(n, to, copies, places, width):
                def group(i, h, wait):
                    js = bass.ds((i * 2 + h) * SG, SG)
                    if wait:
                        hold(pool, scattered[h], (i + n * G2) * (16 * SG))
                    for lo_c, hi_c, part in copies:
                        if hi_c is None:
                            nc.gpsimd.tensor_copy(stage[:, h, :, lo_c], part[:, js])
                        else:
                            nc.gpsimd.tensor_copy(stage[:, h, :, lo_c:hi_c], part[:, js, :])
                    nc.gpsimd.tensor_copy(stage_at[:, h, :], places[:, js]).then_inc(staged, 1)
                    hold(pool, staged, (i + n * G2) * 2 + (h + 1))
                    for j in range(SG):
                        nc.gpsimd.indirect_dma_start(
                            to, bass.IndirectOffsetOnAxis(ap=stage_at[:, h, j:j + 1], axis=0),
                            stage[:, h, j, 0:width], None).then_inc(scattered[h], 16)
                if n == 0:
                    for h in range(2):
                        group(0, h, False)
                with pool.Fori(1 if n == 0 else 0, G2) as i:
                    for h in range(2):
                        group(i, h, True)

            def gather(ep, p, c_other, frm, width):
                hold(pool, table_in, 16 * (ep + 1))
                with pool.Fori(0, NB) as i:
                    m = ep * NB + i
                    for c in range(CH):
                        pool.wait_ge(pay_in[c], 16 * (m + 1))
                        hold(pool, slots_free, m * U + (c + 1) * (U // CH))
                        nc.gpsimd.tensor_copy(at[:, c, :], p[:, c, :, c_other]).then_inc(at_ready, 1)
                        hold(pool, at_ready, m * CH + c + 1)
                        for u in range(c * U // CH, (c + 1) * U // CH):
                            for k in range(K):
                                j = (u * K + k) % CT
                                nc.gpsimd.indirect_dma_start(
                                    rows[:, u, k, 0:width], None, frm,
                                    bass.IndirectOffsetOnAxis(ap=at[:, c, j:j + 1], axis=0)).then_inc(gathered[u], 16)

            pool.wait_ge(filled, 16 * 10)
            pool.wait_ge(made_rows, 1)
            pool.wait_ge(placed, 1)
            scatter(0, rows_bin, [(0, C3, bin_rows)], pos_i[:, 0, :], C3)
            pool.wait_ge(made_rows, 2)
            pool.wait_ge(placed, 2)
            scatter(1, rows_dst, [(0, C, edge_rows)], pos_i[:, 1, :], C)
            gather(EP_L0, pay, C_OTHER, table, D)
            scatter(2, rows_src, [(C2_KEY, None, lo_src[:]), (C2_OTHER, None, dst_f[:])], pos_src[:], C2)
            with pool.Fori(0, LAYERS) as l:
                gather(l + EP_L2, pay, C_OTHER, table2, 2 * D)
            gather(EP_L3, pay2, C2_OTHER, table, D)

        @block.vector
        def _(v):
            done = [0]

            def link(ins):
                done[0] += 1
                ins.then_inc(dve_step, 1)
                v.wait_ge(dve_step, done[0])

            def steps(loop, count, index):
                start, n = done[0], [0]

                def link_in(ins):
                    n[0] += 1
                    ins.then_inc(dve_step, 1)
                    v.wait_ge(dve_step, index * count + (start + n[0]))
                return link_in

            def over_d(a):
                return a.unsqueeze(2).to_broadcast([LO, HI, D])

            def over_hi(a):
                return a.unsqueeze(1).to_broadcast([LO, HI, D])

            sqrts = [0]

            def layer_norm(link, frm, to, tmp, n):
                link(nc.vector.tensor_reduce(mean[:], frm, AX_X, ALU.add))
                link(nc.vector.tensor_scalar(mean[:], mean[:], 1.0 / D, None, ALU.mult))
                link(nc.vector.tensor_tensor(to, frm, over_d(mean[:]), ALU.subtract))
                link(nc.vector.tensor_tensor(tmp, to, to, ALU.mult))
                link(nc.vector.tensor_reduce(var[:], tmp, AX_X, ALU.add))
                nc.vector.tensor_scalar(var[:], var[:], 1.0 / D, LN_EPS, ALU.mult, ALU.add).then_inc(sqrt_in, 1)
                v.wait_ge(sqrt_out, n + 1)
                link(nc.vector.reciprocal(rstd[:], rstd[:]))
                link(nc.vector.tensor_tensor(to, to, over_d(rstd[:]), ALU.mult))

            LN_LINKS = 7

            v.sem_inc(proj_read, 1)
            v.sem_inc(layer_w_free, 1)
            v.sem_inc(turned_read, 1)
            v.wait_ge(consts, 1)
            nc.vector.memset(ones[:], 1.0)
            nc.vector.memset(ones_b[:], 1.0)
            nc.vector.memset(zeros[:], 0.0)
            nc.vector.memset(zeros_b[:], 0.0)
            nc.vector.tensor_copy(iota_row_b[:], iota_row[:])
            nc.vector.tensor_copy(iota_col_h[:], iota_t[:, 0:CW])
            nc.vector.tensor_scalar(ident[:], iota_row[:], iota_p[:, 0:1], None, ALU.is_equal)
            nc.vector.tensor_scalar(ident_b[:], iota_row[:], iota_p[:, 0:1], None, ALU.is_equal)
            link(nc.vector.tensor_scalar(before[:], iota_row[:], iota_p[:, 0:1], None, ALU.is_gt))
            v.sem_inc(dve_consts, 1)

            v.wait_ge(loaded0, 16 * 2)
            link(nc.vector.tensor_copy(key, key_i))
            link(nc.vector.tensor_scalar(ta, key, 1.0 / HI, -0.48, ALU.mult, ALU.add))
            link(nc.vector.tensor_scalar(ta, ta, ROUND, None, ALU.add))
            link(nc.vector.tensor_scalar(lo, ta, -ROUND, None, ALU.add))
            link(nc.vector.scalar_tensor_tensor(hi, lo, -float(HI), key, ALU.mult, ALU.add))
            link(nc.vector.tensor_scalar(grp, hi[:, 1, :], 1.0 / CB, -(0.5 - 0.5 / CB), ALU.mult, ALU.add))
            link(nc.vector.tensor_scalar(grp, grp, ROUND, None, ALU.add))
            link(nc.vector.tensor_scalar(grp, grp, -ROUND, None, ALU.add))
            nc.vector.scalar_tensor_tensor(keys_b[:, 0, :], grp, float(HI), hi[:, 0, :], ALU.mult, ALU.add)
            nc.vector.tensor_copy(keys_b[:, 1, :], hi[:, 1, :])
            nc.vector.tensor_copy(keys_b[:, 2, :], hi[:, 0, :])
            link(nc.vector.scalar_tensor_tensor(col, grp, -float(CB), hi[:, 1, :], ALU.mult, ALU.add))
            link(nc.vector.scalar_tensor_tensor(col, col, float(LO), lo[:, 1, :], ALU.mult, ALU.add))
            v.sem_inc(lo_ready, 1)

            for s in range(3):
                with v.Fori(0, SEGS[s] // Q) as i:
                    lk = steps(v, 1, i)
                    for q in range(Q):
                        ins = nc.vector.tensor_scalar(ohk[:, q, :], keys_b[:, s, :], iota_t[0:EP, bass.ds(i * Q + q, 1)],
                                                      None, ALU.is_equal, ALU.add,
                                                      accum_out=cnt[:, bass.ds(i * Q + (q + SEG_AT[s]), 1)])
                    lk(ins)
                done[0] += SEGS[s] // Q
            v.sem_inc(counted, 1)
            v.wait_ge(prefixed, 1)
            pre = ps[0:EP, 7, 0:BUCKETS]
            tot = ps[0:EP, 7, BUCKETS:2 * BUCKETS]
            link(nc.vector.tensor_scalar(tiles, tot, 1.0 / 128, 0.5 - 1.0 / 256, ALU.mult, ALU.add))
            link(nc.vector.tensor_scalar(tiles, tiles, ROUND, None, ALU.add))
            link(nc.vector.tensor_scalar(tiles, tiles, -ROUND, 1.0, ALU.add, ALU.max))
            for s in range(3):
                seg = slice(SEG_AT[s], SEG_AT[s] + SEGS[s])
                link(nc.vector.tensor_tensor_scan(tsum[:, seg], ones_b[0:EP, 0:SEGS[s]], tiles[:, seg], 0.0, ALU.mult, ALU.add))
            link(nc.vector.tensor_tensor(tsum, tsum, tiles, ALU.subtract))
            link(nc.vector.scalar_tensor_tensor(base, tsum, 128.0, pre, ALU.mult, ALU.add))
            link(nc.vector.tensor_scalar(base, base, -1.0, None, ALU.add))

            def rank(s, to):
                link(nc.vector.memset(pos, 0.0))
                start, per = done[0], 2 * Q + 1
                with v.Fori(0, SEGS[s] // Q) as i:
                    for q in range(Q):
                        ins = nc.vector.tensor_scalar(ohk[:, q, :], keys_b[:, s, :], iota_t[0:EP, bass.ds(i * Q + q, 1)],
                                                      None, ALU.is_equal)
                    ins.then_inc(dve_step, 1)

                    def scan(q):
                        nc.vector.tensor_tensor_scan(ps[0:EP, q, 0:EJ], ones_b[0:EP, :], ohk[:, q, :],
                                                     base[:, bass.ds(i * Q + (q + SEG_AT[s]), 1)],
                                                     ALU.mult, ALU.add).then_inc(dve_step, 1)
                    v.wait_ge(dve_step, i * per + (start + 1))
                    scan(0)
                    for q in range(Q):
                        if q + 1 < Q:
                            scan(q + 1)
                        hold(v, dve_step, i * per + (start + 2 + 2 * q))
                        nc.vector.copy_predicated(pos, ohk[:, q, :].bitcast(I16), ps[0:EP, q, 0:EJ]).then_inc(dve_step, 1)
                    v.wait_ge(dve_step, (i + 1) * per + start)
                done[0] += SEGS[s] // Q * per
                tq = ta[:, 0, :]
                link(nc.vector.tensor_scalar(tq, pos, 1.0 / 128, -(0.5 - 1.0 / 256), ALU.mult, ALU.add))
                link(nc.vector.tensor_scalar(tq, tq, ROUND, None, ALU.add))
                link(nc.vector.tensor_scalar(tq, tq, -ROUND, None, ALU.add))
                link(nc.vector.scalar_tensor_tensor(pos, tq, -128.0, pos, ALU.mult, ALU.add))
                link(nc.vector.scalar_tensor_tensor(to, pos, float(SEG_T[s]), tq, ALU.mult, ALU.add))
                v.sem_inc(placed, 1)

            rank(0, pos_i[:, 0, :])

            v.wait_ge(loaded, 16 * (len(loads) + len(block_loads)))
            layer_norm(link, xs[:], t1[:], t2[:], 0)
            nc.vector.tensor_scalar(hs[:], t1[:], 0.0, None, ALU.max).then_inc(node_ready, 1)

            rank(1, pos_i[:, 1, :])
            rank(2, pos_src[:])

            parts = [(0, 0, LO), (0, LO, BINS), (1, 0, HI), (2, 0, HI)]
            for x, (s, b0, b1_) in enumerate(parts):
                n = b1_ - b0
                link(nc.vector.tensor_tensor(picked[0:n, 0:n], tsum[0:n, SEG_AT[s] + b0:SEG_AT[s] + b1_], ident[0:n, 0:n], ALU.mult))
                link(nc.vector.tensor_reduce(start_col[0:n, x:x + 1], picked[0:n, 0:n], AX_X, ALU.add))
            for r in range(2):
                for x in (2 * r, 2 * r + 1):
                    s, b0, b1_ = parts[x]
                    ins = nc.vector.tensor_scalar(begun[0:b1_ - b0, x % 2, 0:SEG_T[s]], iota_t[0:b1_ - b0, 0:SEG_T[s]],
                                                  start_col[0:b1_ - b0, x:x + 1], None, ALU.is_ge)
                ins.then_inc(starts_ready, 1)
                v.wait_ge(starts_summed, r + 1)
                if r == 0:
                    sums = ps[0:1, 5:7, 0:T3 // 2]
                    two = "p (b t) -> p b t"
                    link(nc.vector.tensor_scalar(bin_of.rearrange(two, b=2), sums, -1.0, None, ALU.add))
                    link(nc.vector.tensor_scalar(turn_of, bin_of, 1.0 / EV, -(0.5 - 0.5 / EV), ALU.mult, ALU.add))
                    link(nc.vector.tensor_scalar(turn_of, turn_of, ROUND, None, ALU.add))
                    link(nc.vector.tensor_scalar(turn_of, turn_of, -ROUND, None, ALU.add))
                    link(nc.vector.scalar_tensor_tensor(turn_of, turn_of, -float(EV), bin_of, ALU.mult, ALU.add))
                    link(nc.vector.tensor_scalar(bank_of, turn_of, 512.0, None, ALU.mult))
                    link(nc.vector.tensor_scalar(need, bin_of, 1.0, None, ALU.add))
                else:
                    link(nc.vector.tensor_scalar(blk[:, 1, :], ps[0:1, 5, 0:T], float(D), -float(D), ALU.mult, ALU.add))
                    link(nc.vector.tensor_scalar(blk_id[:], ps[0:1, 5, 0:T], float(HI * D - 1), None, ALU.add))
                    link(nc.vector.tensor_scalar(blk[:, 0, :], ps[0:1, 6, 0:T], float(D), -float(D), ALU.mult, ALU.add))
            link(nc.vector.tensor_scalar(bin_end[:, 0:BINS - 1], tsum[0:1, 1:BINS], float(BS), None, ALU.add))
            link(nc.vector.memset(bin_end[:, BINS - 1:BINS], T3 + BS))
            v.sem_inc(blk_ready, 1)

            v.wait_ge(bin_loaded, 16)
            nc.vector.tensor_copy(scal[:, :, 0], bin_in[:, :, C3_ROW])
            nc.vector.tensor_copy(scal[:, :, 1], bin_in[:, :, C3_COL])
            w_rest = bin_in[:, :, C3_W]
            for part in range(3):
                link(nc.vector.tensor_copy(wpart, w_rest))
                ins = nc.vector.tensor_copy(scal[:, :, 2 + part], wpart)
                if part < 2:
                    ins = nc.vector.tensor_tensor(w_rest, w_rest, wpart, ALU.subtract)
                link(ins)
            v.wait_ge(made_rows, 2)
            start = done[0]
            with v.Fori(0, T3 // BS) as i:
                nc.vector.tensor_copy(sc, scal[:, bass.ds(i * BS, BS), :]).then_inc(dve_step, 1)
                v.wait_ge(dve_step, i * 2 + (start + 1))
                for k in range(BS):
                    v.wait_ge(built, i * BS + (k + 1))
                    for part in range(3):
                        nc.vector.tensor_scalar(lhs[:, k, part, :], iota_row_b[:], sc[:, k, 0:1], sc[:, k, 2 + part:3 + part],
                                                ALU.is_equal, ALU.mult)
                    nc.vector.tensor_scalar(rhs[:, k, :], iota_col_h[:], sc[:, k, 1:2], None, ALU.is_equal).then_inc(op_ready, 1)
                v.sem_inc(dve_step, 1)
                v.wait_ge(op_ready, (i + 1) * BS)
            done[0] += 2 * (T3 // BS)

            def one_hots(n, u, p, c_key, c_w=None):
                c = u // (U // CH)
                v.wait_ge(slots_free, n + U - R + 1)
                for k in range(K):
                    j = (u * K + k) % CT
                    ins = nc.vector.tensor_scalar(oh[:, u % R, k, :], iota_row[:, 0:LO], p[:, c, j, c_key:c_key + 1],
                                                  None if c_w is None else p[:, c, j, c_w:c_w + 1], ALU.is_equal,
                                                  *(() if c_w is None else (ALU.mult,)))
                ins.then_inc(oh_ready, 1)

            with v.Fori(0, NB) as i:
                for u in range(U):
                    n = i * U + u
                    if u % (U // CH) == 0:
                        v.wait_ge(pay_in[u // (U // CH)], 16 * (i + 1))
                    one_hots(n, u, pay, C_KEY)
                    v.wait_ge(lin_ready, n + 1)
                    v.wait_ge(gathered[u], 16 * K * (i + 1))
                    nc.vector.tensor_tensor(s1[:, u % R, 0], lin(u)[:, 0], rows[:, u, :, 0:D], ALU.add).then_inc(sum_ready, 1)
            v.wait_ge(acc_done, 1)
            v.wait_ge(bank_free, EV + BINS)
            nc.vector.tensor_reduce(deg[:, 0, :], deg_bins[0:LO, :].rearrange("p (c h) -> p h c", c=CG), AX_X, ALU.add)
            nc.vector.tensor_scalar(deg[:, 1, :], flat[0:LO, HI * D:HI * D + HI], 1.0, None, ALU.add)
            nc.vector.tensor_tensor(hs[:], hs[:], acc3, ALU.add).then_inc(acc_read, 1)
            v.wait_ge(acc_read, 1)
            v.sem_inc(hs_ready, 1)
            link(nc.vector.tensor_scalar(deg[:, 0, :], deg[:, 0, :], 1.0, None, ALU.add))
            with v.Fori(0, NP) as i:
                v.wait_ge(proj_done, i + 2)
                y = ps[0:LO, 2, 0:PB * D].rearrange("p (k d) -> p k d", k=PB)
                nc.vector.tensor_tensor(t1[:, bass.ds(i * PB, PB), :], y, b2r[:].unsqueeze(1).to_broadcast([LO, PB, D]),
                                        ALU.add).then_inc(proj_read, 1)
            v.wait_ge(proj_read, NP + 1)
            link(nc.vector.tensor_tensor(xs[:], xs[:], t1[:], ALU.add))
            v.sem_inc(layer1_start, 1)

            nc.vector.tensor_scalar(inv_deg[:], deg[:], 1e-30, None, ALU.max).then_inc(sqrt_in, 1)
            v.wait_ge(sqrt_out, 2)
            link(nc.vector.reciprocal(inv_deg[:], inv_deg[:]))
            link(nc.vector.scalar_tensor_tensor(inv_deg[:], deg[:], 0.0, inv_deg[:], ALU.is_gt, ALU.mult))
            nc.vector.tensor_scalar(last_in[:], inv_deg[:, 1, :], 1.0 - ALPHA, None, ALU.mult)
            link(nc.vector.scalar_tensor_tensor(keep[:], inv_deg[:, 0, :], 1.0 - ALPHA, inv_deg[:, 1, :], ALU.mult, ALU.mult))

            layer_norm(link, xs[:], t1[:], t2[:], 2)
            link(nc.vector.tensor_scalar(t1[:], t1[:], 0.0, None, ALU.max))
            link(nc.vector.scalar_tensor_tensor(xs[:], t1[:], ALPHA, xs[:], ALU.mult, ALU.add))
            link(nc.vector.tensor_tensor(t1[:], t1[:], over_d(inv_deg[:, 0, :]), ALU.mult))
            nc.vector.tensor_scalar(fs[:], t1[:], ALPHA, None, ALU.mult)
            link(nc.vector.tensor_copy(hs[:], t1[:]))
            v.sem_inc(h_ready, CG)
            start = done[0]

            def next_h(n, first, count, h, h_next):
                bl = bass.ds(first, count)
                sums = ps[0:LO, 7, 0:count * 2 * D].rearrange("p (k c) -> p k c", k=count)
                v.wait_ge(turned, n + 3)
                nc.vector.tensor_tensor(t2[:, bl, :], h[:, bl, :], sums[:, :, 0:D], ALU.add).then_inc(dve_step, 1)
                v.wait_ge(dve_step, n * 2 + (start + 1))
                nc.vector.tensor_tensor(t2[:, bl, :], t2[:, bl, :], sums[:, :, D:2 * D], ALU.add).then_inc(turned_read, 1)
                v.wait_ge(turned_read, n + 2)
                nc.vector.tensor_tensor(t1[:, bl, :], t2[:, bl, :], keep[:, bl].unsqueeze(2).to_broadcast([LO, count, D]),
                                        ALU.mult).then_inc(dve_step, 1)
                v.wait_ge(dve_step, n * 2 + (start + 2))
                nc.vector.tensor_tensor(h_next[:, bl, :], t1[:, bl, :], fs[:, bl, :], ALU.add).then_inc(h_ready, 1)

            with v.Fori(0, STEPS // 2) as s2:
                for half, (h, h_next) in enumerate(((hs, hs2), (hs2, hs))):
                    with v.Fori(0, CG - 1) as c:
                        next_h((s2 * 2 + half) * CG + c, c * CB, CB, h, h_next)
                    next_h((s2 * 2 + half) * CG + (CG - 1), (CG - 1) * CB, 1, h, h_next)
            done[0] += 2 * STEPS * CG
            v.wait_ge(h_ready, CG * (STEPS + 1))
            link(nc.vector.tensor_tensor(t1[:], t2[:], over_d(last_in[:]), ALU.mult))
            link(nc.vector.tensor_tensor(xs[:], xs[:], t1[:], ALU.add))

            layer_norm(link, xs[:], t1[:], t2[:], 3)
            link(nc.vector.tensor_scalar(hs[:], t1[:], 0.0, None, ALU.max))
            COUNT = 16 + LN_LINKS
            with v.Fori(0, LAYERS) as l:
                ln = [0]
                lstart = done[0]

                def lk(ins):
                    ln[0] += 1
                    ins.then_inc(dve_step, 1)
                    v.wait_ge(dve_step, l * COUNT + (lstart + ln[0]))
                v.wait_ge(layer_w, 16 * LW * (l + 1))
                lk(nc.vector.tensor_copy(floor[:], floors[:, bass.ds(l, 1)]))
                v.wait_ge(w_mm, 2 * l + 1)
                nc.vector.tensor_copy(wnT[:], ps[0:D, 7, 0:D]).then_inc(w_prep, 1)
                v.wait_ge(w_mm, 2 * l + 2)
                nc.vector.tensor_copy(wcat[:, 0:D], wn[:])
                lk(nc.vector.tensor_copy(wcat[:, D:3 * D], ps[0:D, 7, 128:128 + 2 * D]))
                v.sem_inc(hs_ready, 1)
                hold(v, table_in, 16 * (l + EP_L2))
                with v.Fori(0, NP) as i:
                    q = (l + 1) * NP + i
                    v.wait_ge(proj_done, q + 2)
                    y = flat[0:LO, 0:PB * 256].rearrange("p (k c) -> p k c", k=PB)
                    bl = bass.ds(i * PB, PB)
                    nc.vector.tensor_tensor(tab2[:, bl, 0:D], y[:, :, 0:D], be2r[:].unsqueeze(1).to_broadcast([LO, PB, D]), ALU.add)
                    nc.vector.tensor_copy(tab2[:, bl, D:2 * D], y[:, :, D:2 * D])
                    nc.vector.tensor_copy(t1[:, bl, :], y[:, :, 2 * D:3 * D]).then_inc(proj_read, 1)
                v.wait_ge(proj_read, (l + 2) * NP + 1)
                v.sem_inc(node_ready, 1)
                lk(nc.vector.tensor_copy(local_b[:, 0], t1[:]))
                lk(nc.vector.tensor_tensor(t1[:], t1[:], local_b[:, 0], ALU.subtract))
                lk(nc.vector.tensor_copy(local_b[:, 1], t1[:]))
                lk(nc.vector.tensor_tensor(t1[:], t1[:], local_b[:, 1], ALU.subtract))
                lk(nc.vector.tensor_copy(local_b[:, 2], t1[:]))
                v.sem_inc(local_ready, 1)
                with v.Fori(0, NB) as i:
                    m = (l + EP_L2) * NB + i
                    for u in range(U):
                        n2 = (l * NB + i) * U + u
                        r = u % R
                        for w in ([0, 1] if u == 0 else [u + 1] if u + 1 < U else []):
                            if w % (U // CH) == 0:
                                v.wait_ge(pay_in[w // (U // CH)], 16 * (m + 1))
                            one_hots(m * U + w, w, pay, C_KEY)
                        v.wait_ge(lin_ready, n2 + (NB * U + 1))
                        v.wait_ge(gathered[u], 16 * K * (m + 1))
                        nc.vector.tensor_tensor(s1[:, r], lin(u), rows[:, u].rearrange("p k (s d) -> p s k d", s=2),
                                                ALU.add).then_inc(sum_ready, 1)
                        v.wait_ge(sum_ready, n2 + (NB * U + 1))
                        nc.vector.scalar_tensor_tensor(zr[:, r], s1[:, r, 1], 0.0, wa2r[:].unsqueeze(1).to_broadcast([128, K, D]),
                                                       ALU.max, ALU.mult).then_inc(zr_ready, 1)
                        v.wait_ge(zr_ready, n2 + 1)
                        nc.vector.tensor_reduce(logit[:, r], zr[:, r], AX_X, ALU.add).then_inc(logit_ready, 1)
                        v.wait_ge(att_ready, n2 + 1)
                        nc.vector.tensor_tensor(msg[:, r], s1[:, r, 0], att[:, r].unsqueeze(2).to_broadcast([128, K, D]),
                                                ALU.mult).then_inc(msg_ready, 1)
                v.wait_ge(acc_done, l + EP_L2 + 1)
                nc.vector.tensor_tensor(t1[:], acc3, over_hi(biasr[:]), ALU.add).then_inc(acc_read, 1)
                v.wait_ge(acc_read, l + EP_L2 + 1)
                layer_norm(lk, t1[:], t2[:], t1[:], l + 4)
                lk(nc.vector.tensor_tensor(t2[:], t2[:], over_hi(lngr[:]), ALU.mult))
                lk(nc.vector.tensor_tensor(t2[:], t2[:], over_hi(lnbr[:]), ALU.add))
                lk(nc.vector.tensor_scalar(t2[:], t2[:], floor[:, 0:1], None, ALU.max))
                lk(nc.vector.tensor_tensor(hs[:], hs[:], t2[:], ALU.add))
                v.sem_inc(layer_w_free, 1)
                for _ in range(COUNT - ln[0]):
                    lk(nc.vector.memset(rstd[:, 0:1], 0.0))
            done[0] += COUNT * LAYERS
            link(nc.vector.tensor_tensor(xs[:], xs[:], hs[:], ALU.add))

            layer_norm(link, xs[:], t1[:], t2[:], 4 + LAYERS)
            link(nc.vector.tensor_scalar(hs[:], t1[:], 0.0, None, ALU.max))
            nc.vector.tensor_scalar(bnc[:, 1:2], bnc[:, 1:2], LN_EPS, None, ALU.add)
            nc.vector.tensor_scalar(bnr[:, 3, :], bnr[:, 3, :], LN_EPS, None, ALU.add).then_inc(sqrt_in, 1)
            v.wait_ge(sqrt_out, 6 + LAYERS)
            link(nc.vector.reciprocal(bnc[:, 1:2], bnc[:, 1:2]))
            link(nc.vector.reciprocal(bnr[:, 3, :], bnr[:, 3, :]))
            link(nc.vector.tensor_tensor(bnc[:, 0:1], bnc[:, 0:1], bnc[:, 1:2], ALU.mult))
            link(nc.vector.tensor_tensor(bnr[:, 0, :], bnr[:, 0, :], bnr[:, 3, :], ALU.mult))
            link(nc.vector.tensor_tensor(bnr[:, 2, :], bnr[:, 2, :], bnr[:, 0, :], ALU.mult))
            link(nc.vector.tensor_tensor(bnr[:, 1, :], bnr[:, 1, :], bnr[:, 2, :], ALU.subtract))
            link(nc.vector.tensor_tensor(w3d[:, 0, :], w3s[:, 0:D], w3s[:, D:2 * D], ALU.subtract))
            link(nc.vector.tensor_scalar(w3d[:, 0, :], w3d[:, 0, :], bnc[:, 0:1], None, ALU.mult))
            nc.vector.tensor_scalar(w3d[:, 1, :], w3s[:, D:2 * D], bnc[:, 0:1], None, ALU.mult).then_inc(w_prep, 1)
            v.wait_ge(w_mm, 2 * LAYERS + 1)
            link(nc.vector.tensor_copy(w3T[:], ps[0:D, 7, 0:2 * D]))
            v.sem_inc(hs_ready, 1)
            with v.Fori(0, NP) as i:
                v.wait_ge(proj_done, i + (LAYERS + 1) * NP + 2)
                y = flat[0:LO, 0:PB * 256].rearrange("p (k c) -> p k c", k=PB)
                bl = bass.ds(i * PB, PB)
                nc.vector.tensor_tensor(t2[:, bl, :], y[:, :, 0:D], bnr[:, 1, :].unsqueeze(1).to_broadcast([LO, PB, D]), ALU.add)
                nc.vector.tensor_copy(t1[:, bl, :], y[:, :, D:2 * D]).then_inc(proj_read, 1)
            v.wait_ge(proj_read, (LAYERS + 2) * NP + 1)
            v.sem_inc(node_ready, 1)
            link(nc.vector.tensor_copy(local_b[:, 0], t2[:]))
            link(nc.vector.tensor_tensor(t2[:], t2[:], local_b[:, 0], ALU.subtract))
            link(nc.vector.tensor_copy(local_b[:, 1], t2[:]))
            link(nc.vector.tensor_tensor(t2[:], t2[:], local_b[:, 1], ALU.subtract))
            link(nc.vector.tensor_copy(local_b[:, 2], t2[:]))
            v.sem_inc(local_ready, 1)
            with v.Fori(0, NB) as i:
                m = i + EP_L3 * NB
                for u in range(U):
                    n = i * U + (LAYERS + 1) * NB * U + u
                    for w in ([0, 1] if u == 0 else [u + 1] if u + 1 < U else []):
                        if w % (U // CH) == 0:
                            v.wait_ge(pay_in[w // (U // CH)], 16 * (m + 1))
                        one_hots(m * U + w, w, pay2, C2_KEY)
                    v.wait_ge(lin_ready, n + 1)
                    v.wait_ge(gathered[u], 16 * K * (m + 1))
                    nc.vector.tensor_tensor(s1[:, u % R, 0], lin(u)[:, 0], rows[:, u, :, 0:D], ALU.add).then_inc(sum_ready, 1)
            v.wait_ge(acc_done, EP_L3 + 1)
            nc.vector.tensor_tensor(xs[:], xs[:], acc3, ALU.add).then_inc(node_ready, 1)

        @block.scalar
        def _(a):
            def root(to, frm, n):
                a.wait_ge(sqrt_in, n + 1)
                nc.scalar.activation(to, frm, ACT.Sqrt).then_inc(sqrt_out, 1)

            a.sem_inc(slot_used, NG)
            for g in range(EV):
                a.sem_inc(ev_out[g], 16)
            a.wait_ge(dve_consts, 1)
            a.wait_ge(lo_ready, 1)
            a.wait_ge(at_loaded, 16 * 3)
            nc.scalar.copy(bin_rows[:, :, C3_ROW], lo[:, 0, :])
            nc.scalar.copy(bin_rows[:, :, C3_COL], col)
            nc.scalar.copy(bin_rows[:, :, C3_W + 1], zeros[0:EP, 0:EJ])
            nc.scalar.copy(bin_rows[:, :, C3_W], wgt).then_inc(made_rows, 1)
            nc.scalar.copy(edge_rows[:, :, 0:DA], at16)
            nc.scalar.copy(edge_rows[:, :, C_ATT3:C_ATT3 + DB], at3)
            nc.scalar.copy(edge_rows[:, :, C_ONE], ones_b[0:EP, :])
            nc.scalar.copy(edge_rows[:, :, C_W], wgt)
            nc.scalar.copy(edge_rows[:, :, C_KEY], lo[:, 1, :])
            nc.scalar.copy(edge_rows[:, :, C_OTHER], key[:, 0, :])
            nc.scalar.copy(edge_rows[:, :, C_OTHER + 1], zeros[0:EP, 0:EJ])
            nc.scalar.copy(lo_src[:], lo[:, 0, :])
            nc.scalar.copy(dst_f[:], key[:, 1, :]).then_inc(made_rows, 1)
            root(rstd[:], var[:], 0)

            a.wait_ge(blk_ready, 1)
            with a.Fori(0, CG) as c:
                with a.Fori(0, HI // EV) as i:
                    m = c * (HI // EV) + i
                    for g in range(EV):
                        end = a.value_load(bin_end[0:1, bass.ds(m * EV + g, 1)], min_val=BS + 1, max_val=BS + T3)
                        a.wait_ge(ev_out[g], 16 * (m + 1))
                        hold(a, built, end)
                        nc.scalar.activation(ev[:, g, :], ps[:, g, 0:CW], ACT.Copy,
                                             accum_out=deg_bins[:, bass.ds(m * EV + g, 1)]).then_inc(ev_ready, 1)
                        a.wait_ge(ev_ready, m * EV + (g + 1))
                        nc.scalar.copy(ps[:, g, 0:CW], zeros[:]).then_inc(bank_free, 1)
                        a.dma_start(dense[bass.ds(c, 1), :, bass.ds(i * EV + g, 1), :].rearrange("o p b w -> (o p) (b w)"),
                                    ev[:, g, :]).then_inc(ev_out[g], 16)

            with a.Fori(0, NB) as i:
                def payload(u):
                    n = i * U + u
                    a.wait_ge(slots_free, n + U - R + 1)
                    a.wait_ge(tr_ready, n + 1)
                    nc.scalar.copy(payT[:, u % R, :], payT_ps(6 + u % 2)).then_inc(payT_ready, 1)
                payload(0)
                for u in range(U):
                    if u + 1 < U:
                        payload(u + 1)
                    a.wait_ge(sum_ready, i * U + u + 1)
                    nc.scalar.activation(msg[:, u % R], s1[:, u % R, 0], ACT.Relu).then_inc(msg_ready, 1)

            def project(ph, mlp):
                with a.Fori(0, NP) as i:
                    q = i + ph * NP
                    nc.scalar.copy(st[:], hs[:, bass.ds(i * PB, PB), :]).then_inc(st_ready, 1)
                    a.wait_ge(stT_done, q + 1)
                    a.wait_ge(proj_done, q + 1)
                    tp = flat[0:D, 4 * 512:4 * 512 + PB * 128].rearrange("p (k c) -> p k c", k=PB)
                    nc.scalar.copy(hT[:, :, 0:LO], tp[:, :, 0:LO]).then_inc(hT_ready, 1)
                    if mlp:
                        a.wait_ge(mlp_done, i + 1)
                        up = flat[0:D, 0:PB * 128].rearrange("p (k c) -> p k c", k=PB)
                        nc.scalar.activation(uT[:, :, 0:LO], up[:, :, 0:LO], ACT.Gelu, bias=b1c[:, 0:1]).then_inc(uT_ready, 1)

            a.wait_ge(hs_ready, 1)
            project(0, True)
            root(inv_deg[:], inv_deg[:], 1)
            root(rstd[:], var[:], 2)

            def take(n, to, frm):
                a.wait_ge(turned, n + 1)
                nc.scalar.copy(to, frm).then_inc(oT_ready, 1)

            with a.Fori(0, STEPS) as s:
                with a.Fori(0, (CG - 1) // 2) as i:
                    for p in range(2):
                        a.wait_ge(slot_used, (s * (CG - 1) + i * 2) * NG + (p + 2) * NG)
                        take(s * CG + i * 2 + p, oT[:, p, :], ps[:, p, 0:CW])
                a.wait_ge(group_done, s + 1)
                take(s * CG + (CG - 1), oT_last, ps[:, 2, 0:LO])
            root(rstd[:], var[:], 3)

            def transposed(u, n2, n):
                a.wait_ge(oh_ready, n + 1)
                a.wait_ge(slots_free, n + U - R + 1)
                nc.scalar.copy(ohb[:, u % R], oh[:, u % R]).then_inc(ohb_ready, 1)

            with a.Fori(0, LAYERS) as l:
                a.wait_ge(hs_ready, l + 2)
                project(l + 1, False)
                with a.Fori(0, NB) as i:
                    m = (l + EP_L2) * NB + i

                    def prepare(u):
                        n2 = (l * NB + i) * U + u
                        n = m * U + u
                        r = u % R
                        a.wait_ge(slots_free, n + U - R + 1)
                        a.wait_ge(tr_ready, n2 + (NB * U + 1))
                        nc.scalar.copy(payT[:, r, :], payT_ps(6)).then_inc(payT_ready, 1)
                        transposed(u, n2, n)
                        a.wait_ge(hid_done, n2 + 1)
                        nc.scalar.activation(hid[:, r], hid_ps, ACT.Relu).then_inc(hid_ready, 1)
                        a.wait_ge(ohT_done, n2 + 1)
                        nc.scalar.copy(ohT[:, r], ohT_ps).then_inc(ohT_ready, 1)
                    prepare(0)
                    for u in range(U):
                        if u + 1 < U:
                            prepare(u + 1)
                        a.wait_ge(logit_ready, (l * NB + i) * U + u + 1)
                        nc.scalar.activation(att[:, u % R], logit[:, u % R], ACT.Sigmoid, bias=ba2c[:, 0:1]).then_inc(att_ready, 1)
                root(rstd[:], var[:], l + 4)
            root(rstd[:], var[:], 4 + LAYERS)
            a.wait_ge(sqrt_in, 6 + LAYERS)
            nc.scalar.activation(bnc[:, 1:2], bnc[:, 1:2], ACT.Sqrt)
            nc.scalar.activation(bnr[:, 3, :], bnr[:, 3, :], ACT.Sqrt).then_inc(sqrt_out, 1)

            a.wait_ge(hs_ready, 2 + LAYERS)
            project(1 + LAYERS, False)
            with a.Fori(0, NB) as i:
                def prepare3(u):
                    n2 = i * U + LAYERS * NB * U + u
                    transposed(u, n2, i * U + EP_L3 * NB * U + u)
                    a.wait_ge(ohT_done, n2 + 1)
                    nc.scalar.copy(ohT[:, u % R], ohT_ps).then_inc(ohT_ready, 1)
                prepare3(0)
                for u in range(U):
                    if u + 1 < U:
                        prepare3(u + 1)
                    a.wait_ge(sum_ready, i * U + (LAYERS + 1) * NB * U + u + 1)
                    nc.scalar.activation(msg[:, u % R], s1[:, u % R, 0], ACT.Silu).then_inc(msg_ready, 1)

        @block.tensor
        def _(pe):
            def mm(to, lhsT, rhs, start=True, stop=True):
                return nc.tensor.matmul(to, lhsT, rhs, start=start, stop=stop, skip_group_check=True)

            pe.sem_inc(proj_done, 1)
            pe.sem_inc(turned, 2)
            pe.sem_inc(built, BS)
            pe.wait_ge(counted, 1)
            mm(ps[0:EP, 7, 0:BUCKETS], before[0:EP, 0:EP], cnt)
            mm(ps[0:EP, 7, BUCKETS:2 * BUCKETS], ones[0:EP, 0:EP], cnt).then_inc(prefixed, 1)
            pe.wait_ge(starts_ready, 1)
            for half in range(2):
                ts = slice(half * (T3 // 2), (half + 1) * (T3 // 2))
                mm(ps[0:1, 5 + half, 0:T3 // 2], ones_b[0:LO, 0:1], begun[0:LO, 0, ts], stop=False)
                ins = mm(ps[0:1, 5 + half, 0:T3 // 2], ones_b[0:BINS - LO, 0:1], begun[0:BINS - LO, 1, ts], start=False)
            ins.then_inc(starts_summed, 1)
            pe.wait_ge(starts_ready, 2)
            for x in range(2):
                ins = mm(ps[0:1, 5 + x, 0:T], ones_b[0:HI, 0:1], begun[0:HI, x, 0:T])
            ins.then_inc(starts_summed, 1)

            pe.wait_ge(blk_ready, 1)
            for g in range(EV):
                ins = mm(ps[:, g, 0:CW], zeros_b[:, 0:128], zeros_b[:, 0:CW], stop=False)
            ins.then_inc(bank_free, EV)

            def load4(at_, lowest, highest):
                _, values = nc.values_load_multi_w_load_instructions(at_, engines=(pe.engine,), min_val=lowest, max_val=highest)
                return values

            with pe.Fori(0, T3 // BS) as i:
                for k in range(BS):
                    if k % 4 == 0:
                        banks = load4(bank_of[0:1, bass.ds(i * BS + k, 4)], 0, (EV - 1) * 512)
                        needs = load4(need[0:1, bass.ds(i * BS + k, 4)], 1, BINS)
                    pe.wait_ge(op_ready, i * BS + (k + 1))
                    hold(pe, bank_free, needs[k % 4])
                    for part in range(3):
                        ins = mm(flat[:, bass.ds(banks[k % 4], CW)], lhs[:, k, part, :], rhs[:, k, :], start=False, stop=False)
                    ins.then_inc(built, 1)
            pe.wait_ge(bank_free, EV + BINS)

            def clear(ep, extra=0):
                if not (isinstance(ep, int) and ep == 0):
                    pe.wait_ge(acc_read, ep)
                for b in range(4):
                    w = min(512, HI * D + extra - b * 512)
                    ins = mm(ps[0:LO, b, 0:w], zeros_b[:, 0:LO], zeros_b[:, 0:w], stop=False)
                return ins

            def finish_pass():
                mm(ps[0:LO, 3, 0:HI * D - 3 * 512], zeros_b[:, 0:LO], zeros_b[:, 0:HI * D - 3 * 512],
                   start=False).then_inc(acc_done, 1)

            def block_of(key_of, i, u, k):
                return pe.value_load(blk[0:1, key_of, bass.ds(i * BODY + (u * K + k), 1)], min_val=0, max_val=(HI - 1) * D)

            def add_up(i, n, u, values, offs):
                for k in range(K):
                    ins = mm(acc[0:LO, bass.ds(offs[k], D)], oh[:, u % R, k, :], values(k), start=False, stop=False)
                ins.then_inc(slots_free, 1)

            clear(0, HI).then_inc(slots_free, U)
            with pe.Fori(0, NB) as i:
                def turn(u):
                    if u % (U // CH) == 0:
                        pe.wait_ge(pay_in[u // (U // CH)], 16 * (i + 1))
                    j = u * K % CT
                    nc.tensor.transpose(payT_ps(6 + u % 2), pay[:, u // (U // CH), j:j + K, :].rearrange("p k c -> p (k c)"),
                                        ident[:]).then_inc(tr_ready, 1)

                def sum_up(u):
                    n = i * U + u
                    offs = [block_of(1, i, u, k) for k in range(K)]
                    pe.wait_ge(oh_ready, n + 1)
                    ids = load4(blk_id[0:1, bass.ds(i * BODY + u * K, K)], HI * D, HI * D + HI - 1)
                    pe.wait_ge(msg_ready, n + 1)
                    for k in range(K):
                        mm(flat[0:LO, bass.ds(ids[k], 1)], oh[:, u % R, k, :],
                           pay[:, u // (U // CH), u * K % CT + k, C_W:C_W + 1], start=False, stop=False)
                    add_up(i, n, u, lambda k: msg[:, u % R, k, :], offs)
                turn(0)
                for u in range(U):
                    if u + 1 < U:
                        turn(u + 1)
                    pe.wait_ge(payT_ready, i * U + u + 1)
                    mm(ps[:, 4 + u % 2, 0:K * D], payT[:, u % R, :], wl0[:].rearrange("p k d -> p (k d)")).then_inc(lin_ready, 1)
                    if u >= 1:
                        sum_up(u - 1)
                sum_up(U - 1)
            finish_pass()

            def turn_blocks(ph, i):
                q = i + ph * NP
                hold(pe, st_ready, q + 1)
                for k in range(PB):
                    ins = nc.tensor.transpose(flat[0:D, 4 * 512 + k * 128:4 * 512 + k * 128 + LO], st[:, k, :], ident[0:LO, 0:LO])
                ins.then_inc(stT_done, 1)
                pe.wait_ge(hT_ready, q + 1)
                hold(pe, proj_read, q + 1)

            with pe.Fori(0, NP) as i:
                turn_blocks(0, i)
                mm(ps[0:D, 0, :].rearrange("p (k c) -> p k c", c=128)[:, :, 0:LO], w1s[:], hT[:, 0:4, 0:LO])
                mm(ps[0:D, 1, 0:LO], w1s[:], hT[:, 4, 0:LO]).then_inc(mlp_done, 1)
                hold(pe, uT_ready, i + 1)
                for k in range(PB):
                    ins = mm(ps[0:LO, 2, k * D:(k + 1) * D], uT[:, k, 0:LO], w2s[:])
                ins.then_inc(proj_done, 1)

            pe.wait_ge(proj_read, NP + 1)
            pe.wait_ge(kept_in, 16 * CG)

            def times(bank, h, b, bin_, width, half, first, last):
                return mm(ps[half * D:(half + 1) * D, bank, 0:width], h[:, b, :], bin_, start=first, stop=last)

            def turn(n, frm, count):
                pe.wait_ge(oT_ready, n + 1)
                pe.wait_ge(turned_read, n + 1)
                for k in range(count):
                    ins = nc.tensor.transpose(ps[0:LO, 7, k * 128:(k + 1) * 128], frm[:, k * LO:(k + 1) * LO], ident[:])
                ins.then_inc(turned, 1)

            with pe.Fori(0, STEPS // 2) as s2:
                for half, h in enumerate((hs, hs2)):
                    s = s2 * 2 + half
                    with pe.Fori(0, (CG - 1) // 2) as i:
                        for p in range(2):
                            c = i * 2 + p
                            flat_kept = kept.rearrange("p c b w -> p (c b w)")

                            def kept_bin(b):
                                return flat_kept[0:LO, bass.ds(c * (NR * CW) + b * CW, CW)]
                            if p == 0:
                                pe.wait_ge(h_ready, (s + 1) * CG)
                            for g in range(NG):
                                pe.wait_ge(slot_in[g], (s * (CG - 1) + c + 1) * 16)
                                for j in range(GB):
                                    b = NR + g * GB + j
                                    if b < 2 * NR:
                                        times(p, h, b - NR, kept_bin(b - NR), CW, 0, b == NR, False)
                                    ins = times(p, h, b, slots[0:LO, g, j, :], CW, 1 if b < 2 * NR else b % 2,
                                                b == NR, b >= HI - 2)
                                ins.then_inc(slot_used, 1)
                                if p == 1 and g == 1:
                                    turn(s * CG + c - 1, oT[:, 0, :], CB)
                        turn(s * CG + i * 2 + 1, oT[:, 1, :], CB)
                    for b in range(HI):
                        ins = times(2, h, b, kept_last[0:LO, b, :], LO, b % 2, b < 2, b >= HI - 2)
                    ins.then_inc(group_done, 1)
                    turn(s * CG + (CG - 1), oT_last, 1)
            pe.wait_ge(turned_read, CG * STEPS + 1)

            def project(ph, w, width):
                with pe.Fori(0, NP) as i:
                    turn_blocks(ph, i)
                    for k in range(PB):
                        ins = mm(flat[0:LO, k * 256:k * 256 + width], hT[:, k, 0:LO], w[:, 0:width])
                    ins.then_inc(proj_done, 1)

            def turn_one_hots(u, n2, last):
                pe.wait_ge(ohb_ready, n2 + 1)
                for k in range(K):
                    ins = nc.tensor.transpose(ohT_ps[:, k, :], ohb[:, u % R, k, :], ident_b[:])
                ins.then_inc(ohT_done, 1)

            def add_local(u, half, offs, start):
                for k in range(K):
                    for part in range(3):
                        table_part = local_b[:, part].rearrange("p h d -> p (h d)")
                        ins = mm(lin(u)[:, half, k, :], ohT[:, u % R, k, :], table_part[:, bass.ds(offs[k], D)],
                                 start=start and part == 0, stop=part == 2)
                return ins

            with pe.Fori(0, LAYERS) as l:
                hold(pe, layer_w, 16 * LW * (l + 1))
                nc.tensor.transpose(ps[0:D, 7, 0:D], wn[:], ident[0:D, 0:D]).then_inc(w_mm, 1)
                hold(pe, w_prep, l + 1)
                mm(ps[0:D, 7, 128:128 + 2 * D], wnT[:], wa1[:].rearrange("p s d -> p (s d)")).then_inc(w_mm, 1)
                hold(pe, hs_ready, l + 2)
                project(l + 1, wcat, 3 * D)
                hold(pe, proj_read, (l + 2) * NP + 1)
                clear(l + EP_L2)
                hold(pe, local_ready, l + 1)
                with pe.Fori(0, NB) as i:
                    m = (l + EP_L2) * NB + i

                    def turn(u):
                        if u % (U // CH) == 0:
                            pe.wait_ge(pay_in[u // (U // CH)], 16 * (m + 1))
                        j = u * K % CT
                        nc.tensor.transpose(payT_ps(6), pay[:, u // (U // CH), j:j + K, :].rearrange("p k c -> p (k c)"),
                                            ident[:]).then_inc(tr_ready, 1)

                    def hidden(u):
                        n2 = (l * NB + i) * U + u
                        pe.wait_ge(payT_ready, n2 + (NB * U + 1))
                        for q in range(K // 2):
                            ins = mm(hid_ps[:, q, :], wt[:, q, :], payT[:, u % R, :])
                        ins.then_inc(hid_done, 1)
                        turn_one_hots(u, n2, None)

                    def products(u):
                        n2 = (l * NB + i) * U + u
                        pe.wait_ge(hid_ready, n2 + 1)
                        for q in range(K // 2):
                            mm(ps[:, 4 + u % 2, q * 128:(q + 1) * 128], hid[:, u % R, q, :], we2[:])
                        mm(ps[:, 4 + u % 2, K * D:2 * K * D], payT[:, u % R, :], wz[:].rearrange("p k d -> p (k d)"), stop=False)
                        add_local(u, 1, offs[u], False).then_inc(lin_ready, 1)

                    def sum_up(u):
                        n2 = (l * NB + i) * U + u
                        pe.wait_ge(msg_ready, n2 + (NB * U + 1))
                        add_up(i, m * U + u, u, lambda k: msg[:, u % R, k, :], offs[u])
                    offs = {0: [block_of(1, i, 0, k) for k in range(K)]}
                    turn(0)
                    hidden(0)
                    for u in range(U):
                        pe.wait_ge(ohT_ready, (l * NB + i) * U + u + 1)
                        if u + 1 < U:
                            turn(u + 1)
                        products(u)
                        if u + 1 < U:
                            hidden(u + 1)
                        if u >= 1:
                            sum_up(u - 1)
                        if u + 1 < U:
                            offs[u + 1] = [block_of(1, i, u + 1, k) for k in range(K)]
                    sum_up(U - 1)
                finish_pass()

            pe.wait_ge(w_prep, LAYERS + 1)
            for h in range(2):
                ins = nc.tensor.transpose(ps[0:D, 7, h * D:(h + 1) * D], w3d[:, h, :], ident[0:D, 0:D])
            ins.then_inc(w_mm, 1)
            pe.wait_ge(hs_ready, LAYERS + 2)
            project(LAYERS + 1, w3T, 2 * D)
            pe.wait_ge(proj_read, (LAYERS + 2) * NP + 1)
            clear(EP_L3)
            pe.wait_ge(local_ready, LAYERS + 1)
            with pe.Fori(0, NB) as i:
                m = i + EP_L3 * NB

                def products3(u):
                    pe.wait_ge(ohT_ready, i * U + LAYERS * NB * U + u + 1)
                    add_local(u, 0, offs[u], True).then_inc(lin_ready, 1)

                def sum_up3(u):
                    pe.wait_ge(msg_ready, i * U + (LAYERS + 1) * NB * U + u + 1)
                    add_up(i, m * U + u, u, lambda k: msg[:, u % R, k, :], offs[u])
                offs = {0: [block_of(0, i, 0, k) for k in range(K)]}
                turn_one_hots(0, i * U + LAYERS * NB * U, None)
                for u in range(U):
                    products3(u)
                    if u + 1 < U:
                        turn_one_hots(u + 1, i * U + LAYERS * NB * U + u + 1, None)
                    if u >= 1:
                        sum_up3(u - 1)
                    if u + 1 < U:
                        offs[u + 1] = [block_of(0, i, u + 1, k) for k in range(K)]
                sum_up3(U - 1)
            finish_pass()


_INS = ['x', 'src', 'dst', 'edge_attr_16', 'edge_attr_3', 'edge_weight',
        'L0_gnn_We', 'L0_gnn_be', 'L0_gnn_W1', 'L0_gnn_b1', 'L0_gnn_W2', 'L0_gnn_b2',
        'L2_gnn_W_node', 'L2_gnn_W_e1', 'L2_gnn_b_e1', 'L2_gnn_W_e2', 'L2_gnn_b_e2', 'L2_gnn_Wa1', 'L2_gnn_ba1',
        'L2_gnn_Wa2', 'L2_gnn_ba2', 'L2_gnn_bias', 'L2_gnn_ln_g', 'L2_gnn_ln_b',
        'L3_gnn_W', 'L3_gnn_bn_gamma', 'L3_gnn_bn_beta', 'L3_gnn_bn_mean', 'L3_gnn_bn_var']
_OUTS = [((N, D), 'float32')]


def kernel(**inputs):
    import numpy as _np
    import concourse.bacc as _bacc
    from concourse import mybir as _mybir
    from concourse.bass_utils import run_bass_kernel_spmd as _run

    nc = _bacc.Bacc("TRN2", target_bir_lowering=False, num_devices=1)
    arrays, args = {}, []
    for name in _INS:
        a = _np.ascontiguousarray(inputs[name])
        arrays[f"in_{name}_dram"] = a
        args.append(nc.dram_tensor(f"in_{name}_dram", a.shape, _mybir.dt.from_np(a.dtype), kind="ExternalInput").ap())
    for i, (shape, dtype) in enumerate(_OUTS):
        dt = _mybir.dt.from_np(_np.dtype(dtype))
        args.append(nc.dram_tensor(f"out_{i}_dram", shape, dt, kind="ExternalOutput").ap())
    gnn_kernel(nc, *args)
    r = _run(nc, [arrays], core_ids=[0])
    got = tuple(r.results[0][f"out_{i}_dram"] for i in range(len(_OUTS)))
    return got[0]
```

```python
from contextlib import ExitStack

import concourse.bass as bass
from concourse import mybir

F32 = mybir.dt.float32
BF16 = mybir.dt.bfloat16
F16 = mybir.dt.float16
I16 = mybir.dt.int16
I32 = mybir.dt.int32
ALU = mybir.AluOpType
ACT = mybir.ActivationFunctionType
AX_X = mybir.AxisListType.X

N, E, D = 3125, 50000, 64
LO, HI = 125, 25
EP, EJ = 125, 400
DA, DB = 16, 3
T = 416
K = 4
U = 8
CH = 4
UC = U // CH
CT = K * UC
BODY = K * U
NB = T // BODY
assert NB * BODY == T and T >= E // 128 + HI
R = 4
STEPS, ALPHA = 10, 0.1
LAYERS = 3
LN_EPS = 1e-5
C = 24
C_ATT3, C_ONE, C_W, C_KEY, C_OTHER = DA, DA + DB, DA + DB + 1, DA + DB + 2, DA + DB + 3
C2, C2_KEY, C2_OTHER = 4, 0, 1
C3, C3_ROW, C3_COL, C3_W = 4, 0, 1, 2
SG = 8
G2 = EJ // SG // 2
ROUND = 12582912.0
CB = 4
CG = -(-HI // CB)
CW = CB * LO
BINS = CG * HI
BS = 8
T3 = 576
assert T3 % (2 * BS) == 0 and T3 >= E // 128 + BINS and HI - (CG - 1) * CB == 1
EV = 5
assert HI % EV == 0 and EV >= 4
NR = 7
GB = 3
NG = (HI - NR) // GB
assert NR + NG * GB == HI
SEGS = (BINS, HI, HI)
SEG_AT = (0, BINS, BINS + HI)
BUCKETS = sum(SEGS)
SEG_T = (T3, T, T)
Q, QR = 25, 5
EP_L0, EP_L2, EP_L3 = 0, 1, 1 + LAYERS
AB, AP, MW = 7, 68, 96
assert (AB - 1) * AP + MW <= 512 and 4 * AB >= HI and AP > D
ACC_LAST = (HI - 1) // AB * 512 + (HI - 1) % AB * AP
PB = 5
NP = HI // PB


def gnn_kernel(nc, x, src, dst, edge_attr_16, edge_attr_3, edge_weight,
               We, be, W1, b1, W2, b2,
               W_node, W_e1, b_e1, W_e2, b_e2, Wa1, ba1, Wa2, ba2, bias2, ln_g, ln_b,
               W3, bn_gamma, bn_beta, bn_mean, bn_var, out):
    with ExitStack() as ctx:
        def sb(name, shape, dt=F32):
            return ctx.enter_context(nc.sbuf_tensor(name, shape, dt))

        def sem(name):
            return ctx.enter_context(nc.semaphore(name))

        rows_dst = nc.dram_tensor("rows_dst", [128 * T, C], F32).ap()
        rows_src = nc.dram_tensor("rows_src", [128 * T, C2], F32).ap()
        rows_bin = nc.dram_tensor("rows_bin", [128 * T3, C3], F32).ap()
        dense = nc.dram_tensor("dense", [CG, 128, HI, CW], F32).ap()
        table = nc.dram_tensor("table", [N, D], F32).ap()
        table2 = nc.dram_tensor("table2", [N, 2 * D], F32).ap()

        iota_row = sb("iota_row", [128, 128])
        iota_row_b = sb("iota_row_b", [128, 128], BF16)
        iota_col_h = sb("iota_col_h", [128, CW], F16)
        iota_p = sb("iota_p", [128, 1])
        ident = sb("ident", [128, 128])
        ident_b = sb("ident_b", [128, 128], BF16)
        before = sb("before", [128, 128])
        ones = sb("ones", [128, 128])
        ones_b = sb("ones_b", [128, EJ], BF16)
        zeros = sb("zeros", [128, CW])
        zeros_b = sb("zeros_b", [128, 512], BF16)
        acc_at = sb("acc_at", [1, 2, T], I32)
        tab_at = sb("tab_at", [1, 2, T], I32)
        lo_src = sb("lo_src", [EP, EJ])
        dst_f = sb("dst_f", [EP, EJ])
        pos_src = sb("pos_src", [EP, EJ], I32)
        stage = sb("stage", [EP, 2, SG, C])
        stage_at = sb("stage_at", [EP, 2, SG], I32)

        xs = sb("xs", [LO, HI, D])
        hs = sb("hs", [LO, HI, D])
        hs2 = sb("hs2", [LO, HI, D])
        fs = sb("fs", [LO, HI, D])
        t1 = sb("t1", [LO, HI, D])
        t2 = sb("t2", [LO, HI, D])
        mean = sb("mean", [LO, HI])
        var = sb("var", [LO, HI])
        rstd = sb("rstd", [LO, HI])
        deg_bins = sb("deg_bins", [128, BINS])
        deg = sb("deg", [LO, 2, HI])
        inv_deg = sb("inv_deg", [LO, 2, HI])
        keep = sb("keep", [LO, HI])
        last_in = sb("last_in", [LO, HI])

        wl0 = sb("wl0", [K * C, K, D])
        w1s = sb("w1s", [D, D])
        w2s = sb("w2s", [D, D])
        b1c = sb("b1c", [D, 1])
        b2r = sb("b2r", [LO, D])
        wz = sb("wz", [K * C, K, D])
        wt = sb("wt", [K * C, K // 2, 2 * D])
        we2 = sb("we2", [128, 2 * D])
        wn = sb("wn", [D, D])
        wnT = sb("wnT", [D, D])
        wa1 = sb("wa1", [D, 2, D])
        wcat = sb("wcat", [D, 3 * D])
        wa2r = sb("wa2r", [128, D])
        ba2c = sb("ba2c", [128, 1])
        be2r = sb("be2r", [LO, D])
        biasr = sb("biasr", [LO, D])
        lngr = sb("lngr", [LO, D])
        lnbr = sb("lnbr", [LO, D])
        floors = sb("floors", [LO, LAYERS])
        floor = sb("floor", [LO, 1])
        w3s = sb("w3s", [D, 2 * D])
        bnc = sb("bnc", [D, 2])
        bnr = sb("bnr", [LO, 4, D])
        w3d = sb("w3d", [D, 2, D])
        w3T = sb("w3T", [D, 2 * D])

        WORDS = 35400
        arena = sb("arena", [128, WORDS])
        used = [0]

        def carve(shape, dt=F32):
            n = 1
            for d in shape[1:]:
                n *= d
            w = -(-n // 2) if dt in (BF16, F16) else n
            assert used[0] + w <= WORDS, (used[0], w)
            a = arena[0:shape[0], used[0]:used[0] + w]
            used[0] += w
            if dt != F32:
                a = a.bitcast(dt)[:, 0:n]
            if len(shape) > 2:
                names = "abcd"[:len(shape) - 1]
                a = a.rearrange(f"p ({' '.join(names)}) -> p {' '.join(names)}",
                                **{x: d for x, d in zip(names, shape[1:])})
            return a

        key = carve([EP, 2, EJ])
        lo = carve([EP, 2, EJ])
        hi = carve([EP, 2, EJ])
        col = carve([EP, EJ])
        keys_b = carve([EP, 3, EJ], BF16)
        ta = carve([EP, 2, EJ])
        grp = ta[:, 1, :]
        picked = ta[:, 1, 0:EP]
        ohk = carve([EP, QR, EJ], BF16)
        pos = hi[:, 0, :]
        pos_i = carve([EP, 2, EJ], I32)
        cnt = carve([EP, BUCKETS])
        tiles = carve([EP, BUCKETS])
        tsum = carve([EP, BUCKETS])
        base = carve([EP, BUCKETS])
        iota_t = carve([128, T3])
        start_col = carve([128, 4])
        begun = carve([128, 2, T3], BF16)
        bin_of = carve([1, T3])
        turn_of = carve([1, T3])
        bank_of = carve([1, T3], I32)
        need = carve([1, T3], I32)
        bin_end = carve([1, BINS], I32)
        wgt = carve([EP, EJ])
        at3 = carve([EP, EJ, DB])
        edge_rows = carve([EP, EJ, C])
        bin_rows = carve([EP, EJ, C3])
        key_i = bin_rows.rearrange("p j c -> p (j c)")[:, 0:2 * EJ].bitcast(I32).rearrange("p (s j) -> p s j", s=2)
        fills_from = used[0]
        fill = carve([128, T // 8, C])
        fill2 = carve([128, T, C2])
        fill3 = carve([128, T3, C3])
        used[0] = fills_from
        bin_in = carve([128, T3, C3])
        scal = carve([128, T3, 2])
        wparts = carve([128, T3, 3], BF16)
        used[0] = max(used[0], fills_from + T // 8 * C + T * C2 + T3 * C3)
        at_from = used[0]
        at16 = carve([EP, EJ, DA])
        used[0] = at_from
        sc = carve([128, 2, BS, 2])
        sw = carve([128, 2, BS, 3], BF16)
        lhs = carve([128, BS, 3, 128], BF16)
        rhs = carve([128, BS, CW], BF16)
        ev = carve([128, EV, CW])

        used[0] = 0
        pay = carve([128, CH, CT, C])
        pay2 = carve([128, CH, CT, C2])
        rows = carve([128, U, K, 2 * D])
        oh = carve([128, R, K, 128])
        ohb = carve([128, R, K, 128], BF16)
        ohT = carve([128, R, K, 128], BF16)
        payT = carve([K * C, R, 128])
        hid = carve([128, R, K // 2, 128])
        s1 = carve([128, R, 2, K, D])
        zr = carve([128, R, K, D])
        logit = carve([128, R, K])
        att = carve([128, R, K])
        msg = carve([128, R, K, MW])
        tab2 = carve([LO, HI, 2 * D])
        local_b = carve([LO, HI, 3, D], BF16)

        assert used[0] <= (CG - 1) * NR * CW + HI * LO
        used[0] = 0
        kept = carve([128, CG - 1, NR, CW])
        kept_last = carve([128, HI, LO])
        slots_from = used[0]
        slots = carve([128, NG, GB, CW])
        oT = carve([128, 2, CW])
        oT_last = carve([128, LO])
        used[0] = slots_from
        hT = carve([D, 2, PB, 128])
        uT = carve([D, 2, PB, 128])

        ps = ctx.enter_context(nc.psum_tensor("ps", [128, 8, 512], F32))
        flat = ps[:].rearrange("p b c -> p (b c)")
        TURN_AT = 6 * 512

        def projected(q, width):
            return flat[0:LO, q % 2 * 1536:q % 2 * 1536 + PB * 256].rearrange("p (k c) -> p k c", k=PB)[:, :, 0:width]

        def mlp_out(i):
            return ps[0:LO, 2 + i % 2 * 3, 0:PB * D].rearrange("p (k d) -> p k d", k=PB)

        FB = HI // AB
        acc_full = ps[0:LO, 0:FB, 0:AB * AP].rearrange("p g (b c) -> p g b c", b=AB)
        acc_rest = ps[0:LO, FB, 0:(HI - FB * AB) * AP].rearrange("p (b c) -> p b c", c=AP)

        def in_full(a):
            return a[:, 0:FB * AB].rearrange("p (g b) d -> p g b d", g=FB)

        def in_rest(a):
            return a[:, FB * AB:HI]

        def lin(u):
            return ps[:, 4 + u % 2, 0:K * D].rearrange("p (k d) -> p k d", k=K)

        LT = 3 * D
        local_ps = ps[:, 4:6, 0:2 * LT].rearrange("p q (k s d) -> p q k s d", k=2, s=3)
        edge_ps = ps[:, 4:6, 2 * LT:2 * LT + 2 * D].rearrange("p q (k d) -> p q k d", k=2)

        def payT_ps(bank):
            return ps[0:K * C, bank, 0:128]
        hid_ps = ps[:, 7, 0:256].rearrange("p (q e) -> p q e", q=K // 2)
        ohT_ps = ps[:, 6, 128:128 + K * 64].bitcast(BF16).rearrange("p (k e) -> p k e", k=K)

        loaded = sem("loaded")
        consts = sem("consts")
        dve_consts = sem("dve_consts")
        filled = sem("filled")
        dve_step = sem("dve_step")
        counted = sem("counted")
        prefixed = sem("prefixed")
        node_ready = sem("node_ready")
        table_in = sem("table_in")
        local_ready = sem("local_ready")
        pay_in = [sem(f"pay_in{c}") for c in range(CH)]
        gathered = [sem(f"gathered{u}") for u in range(U)]
        slots_free = sem("slots_free")
        acc_done = sem("acc_done")
        acc_read = sem("acc_read")
        oh_ready = sem("oh_ready")
        tr_ready = sem("tr_ready")
        payT_ready = sem("payT_ready")
        lin_ready = sem("lin_ready")
        sum_ready = sem("sum_ready")
        msg_ready = sem("msg_ready")
        add_a = sem("add_a")
        add_b = sem("add_b")
        ohT_done = sem("ohT_done")
        ohT_ready = sem("ohT_ready")
        hid_done = sem("hid_done")
        hid_ready = sem("hid_ready")
        zr_ready = sem("zr_ready")
        logit_ready = sem("logit_ready")
        att_ready = sem("att_ready")
        stT_done = sem("stT_done")
        hT_ready = sem("hT_ready")
        mlp_done = sem("mlp_done")
        uT_ready = sem("uT_ready")
        proj_done = sem("proj_done")
        proj_read = sem("proj_read")
        layer_w = sem("layer_w")
        norm_w = sem("norm_w")
        layer_w_free = sem("layer_w_free")
        w_prep = sem("w_prep")
        w_mm = sem("w_mm")
        bn_var_ready = sem("bn_var_ready")
        bn_root_ready = sem("bn_root_ready")
        w3_ready = sem("w3_ready")
        w3_turned = sem("w3_turned")
        sqrt_in = sem("sqrt_in")
        sqrt_out = sem("sqrt_out")
        hs_ready = sem("hs_ready")
        out_done = sem("out_done")
        held = sem("held")

        rank_compared = sem("rank_compared")
        rank_scanned = sem("rank_scanned")
        rank_copied = sem("rank_copied")
        starts_ready = sem("starts_ready")
        starts_summed = sem("starts_summed")
        blk_ready = sem("blk_ready")
        loaded0 = sem("loaded0")
        at_loaded = sem("at_loaded")
        lo_ready = sem("lo_ready")
        placed = sem("placed")
        made_rows = sem("made_rows")
        staged = sem("staged")
        scattered = [sem("scattered0"), sem("scattered1")]
        bin_loaded = sem("bin_loaded")
        op_ready = sem("op_ready")
        built = sem("built")
        bank_free = sem("bank_free")
        ev_ready = sem("ev_ready")
        ev_out = [sem(f"ev_out{g}") for g in range(EV)]
        kept_in = sem("kept_in")
        layer1_start = sem("layer1_start")
        slot_in = [sem(f"slot_in{g}") for g in range(NG)]
        slot_used = sem("slot_used")
        group_done = sem("group_done")
        oT_ready = sem("oT_ready")
        turned = sem("turned")
        turned_read = sem("turned_read")
        h_ready = sem("h_ready")

        loads = [(xs[:], x.rearrange("(p h) d -> p h d", p=LO)),
                 (w1s[:], W1), (w2s[:], W2), (b1c[:], b1.unsqueeze(1)),
                 (b2r[:], b2.partition_broadcast(LO)), (w3s[:], W3),
                 (bnc[:, 0:1], bn_gamma.unsqueeze(1)), (bnc[:, 1:2], bn_var.unsqueeze(1))]
        loads += [(bnr[:, i, :], v.partition_broadcast(LO))
                  for i, v in enumerate((bn_gamma, bn_beta, bn_mean, bn_var))]
        block_loads = []
        for k in range(K):
            block_loads += [(wl0[C * k:C * k + DA, k, :], We), (wl0[C * k + C_ONE:C * k + C_ONE + 1, k, :], be.unsqueeze(0))]

        def layer_loads(l):
            a = [(wn[:], W_node[l]), (wa1[:, 0, :], Wa1[l, D:2 * D]), (wa1[:, 1, :], Wa1[l, 0:D]),
                 (we2[0:D, 0:D], W_e2[l]), (we2[D:2 * D, D:2 * D], W_e2[l]),
                 (wa2r[:], Wa2[l].rearrange("c o -> (c o)").partition_broadcast(128)),
                 (ba2c[:], ba2[l].partition_broadcast(128)),
                 (be2r[:], b_e2[l].partition_broadcast(LO))]
            for k in range(K):
                q, f = k // 2, (k % 2) * D
                r, o = C * k + C_ATT3, C * k + C_ONE
                a += [(wz[r:r + DB, k, :], Wa1[l, 2 * D:2 * D + DB]), (wz[o:o + 1, k, :], ba1[l].unsqueeze(0)),
                      (wt[r:r + DB, q, f:f + D], W_e1[l]), (wt[o:o + 1, q, f:f + D], b_e1[l].unsqueeze(0))]
            return a
        LW = 8 + 4 * K

        def norm_loads(l):
            return [(biasr[:], bias2[l].partition_broadcast(LO)), (lngr[:], ln_g[l].partition_broadcast(LO)),
                    (lnbr[:], ln_b[l].partition_broadcast(LO))]

        def hold(eng, semaphore, value):
            eng.wait_ge(semaphore, value)
            eng.sem_inc(held, 1)

        def load_values(eng, at_, lowest, highest):
            _, values = nc.values_load_multi_w_load_instructions(
                at_, engines=(eng.engine,), min_val=lowest, max_val=highest, skip_runtime_bounds_check_because=
                "the tables are worked out from counts of edges, and every entry is within its bounds by construction")
            return values

        def over_units(ops, turn):
            for u in range(U):
                turn(0, u, min(u, 2), True)
            with ops.Fori(1, NB - 1) as i:
                for u in range(U):
                    turn(i, u, 2, True)
            for u in range(U):
                turn(NB - 1, u, 2, u + 1 < U)

        def of(array, v):
            return array[:, v % R]

        block = ctx.enter_context(nc.Block())

        @block.sync
        def _(sp):
            sp.dma_start(key_i[:, 1, :], dst.rearrange("(p j) -> p j", p=EP)).then_inc(loaded0, 16)
            sp.dma_start(key_i[:, 0, :], src.rearrange("(p j) -> p j", p=EP)).then_inc(loaded0, 16)
            for to, frm in loads:
                sp.dma_start(to, frm).then_inc(loaded, 16)
            sp.dma_start(wgt, edge_weight.rearrange("(p j) -> p j", p=EP)).then_inc(at_loaded, 16)
            sp.dma_start(at16, edge_attr_16.rearrange("(p j) c -> p j c", p=EP)).then_inc(at_loaded, 16)
            sp.dma_start(at3, edge_attr_3.rearrange("(p j) c -> p j c", p=EP)).then_inc(at_loaded, 16)
            sp.wait_ge(consts, 1)
            for to, frm in block_loads:
                sp.dma_start(to, frm).then_inc(loaded, 16)
            sp.dma_start(rows_bin.rearrange("(p t) c -> p t c", p=128), fill3).then_inc(filled, 16)
            by_part = rows_dst.rearrange("(p t) c -> p t c", p=128)
            for i in range(8):
                n = T // 8
                sp.dma_start(by_part[:, i * n:(i + 1) * n, :], fill).then_inc(filled, 16)
            sp.dma_start(rows_src.rearrange("(p t) c -> p t c", p=128), fill2).then_inc(filled, 16)
            sp.wait_ge(filled, 16 * 10)
            for h in range(2):
                sp.wait_ge(scattered[h], 16 * SG * G2)
            sp.dma_start(bin_in, rows_bin.rearrange("(p t) c -> p t c", p=128)).then_inc(bin_loaded, 16)
            def write_projected(to, frm, ph):
                for i in range(NP):
                    sp.wait_ge(proj_read, ph * NP + (i + 2))
                    bl = slice(i * PB, (i + 1) * PB)
                    for p in (slice(0, 112), slice(112, LO)):
                        sp.dma_start(to[p, bl], frm[p, bl]).then_inc(table_in, 16)

            def write_table(to, frm, n):
                sp.wait_ge(node_ready, n + 1)
                for p in (slice(0, 112), slice(112, LO)):
                    sp.dma_start(to[p], frm[p]).then_inc(table_in, 16)

            def stream(ep, frm, to):
                view = frm.rearrange("(p t) c -> p t c", p=128)
                with sp.Fori(0, NB) as i:
                    m = ep * NB + i
                    for c in range(CH):
                        sp.wait_ge(slots_free, m * U + (c + 1) * UC)
                        sp.dma_start(to[:, c, :, :], view[:, bass.ds(i * BODY + c * CT, CT), :]).then_inc(pay_in[c], 16)

            table_sb = table.rearrange("(p h) d -> p h d", p=LO)
            table2_sb = table2.rearrange("(p h) d -> p h d", p=LO)
            write_table(table_sb, hs[:], EP_L0)
            for h in range(2):
                sp.wait_ge(scattered[h], 2 * 16 * SG * G2)
            for g in range(EV):
                sp.wait_ge(ev_out[g], 16 * (BINS // EV + 1))
            stream(EP_L0, rows_dst, pay)

            sp.wait_ge(acc_done, 1)
            for c in range(CG - 1):
                sp.dma_start(kept[:, c], dense[c, :, 0:NR, :]).then_inc(kept_in, 16)
            sp.dma_start(kept_last, dense[CG - 1, :, :, 0:LO]).then_inc(kept_in, 16)
            sp.wait_ge(layer1_start, 1)
            with sp.Fori(0, STEPS) as s:
                with sp.Fori(0, CG - 1) as c:
                    for g in range(NG):
                        sp.wait_ge(slot_used, (s * (CG - 1) + c) * NG + (g + 1))
                        sp.dma_start(slots[:, g], dense[bass.ds(c, 1), :, NR + g * GB:NR + (g + 1) * GB, :].rearrange(
                            "o p b w -> (o p) b w")).then_inc(slot_in[g], 16)
            with sp.Fori(0, LAYERS) as l:
                sp.wait_ge(acc_done, l + EP_L2)
                for to, frm in layer_loads(l):
                    sp.dma_start(to, frm).then_inc(layer_w, 16)
                sp.wait_ge(layer_w_free, l + 1)
                for to, frm in norm_loads(l):
                    sp.dma_start(to, frm).then_inc(norm_w, 16)
                write_projected(table2_sb, tab2, l + 1)
                stream(l + EP_L2, rows_dst, pay)
            write_projected(table_sb, t1[:], LAYERS + 1)
            for h in range(2):
                sp.wait_ge(scattered[h], 3 * 16 * SG * G2)
            stream(EP_L3, rows_src, pay2)
            sp.wait_ge(node_ready, EP_L3 + 2)
            sp.dma_start(out.rearrange("(p h) d -> p h d", p=LO), xs[:]).then_inc(out_done, 16)
            sp.wait_ge(out_done, 16)

        @block.gpsimd
        def _(pool):
            nc.gpsimd.iota(iota_row[:], [[1, 128]], base=0, channel_multiplier=0, allow_small_or_imprecise_dtypes=True)
            nc.gpsimd.iota(iota_p[:], [[0, 1]], base=0, channel_multiplier=1, allow_small_or_imprecise_dtypes=True)
            nc.gpsimd.iota(iota_t, [[1, T3]], base=0, channel_multiplier=0, allow_small_or_imprecise_dtypes=True)
            nc.gpsimd.memset(stage[:], 0.0)
            nc.gpsimd.memset(wl0[:], 0.0)
            nc.gpsimd.memset(wz[:], 0.0)
            nc.gpsimd.memset(wt[:], 0.0)
            nc.gpsimd.memset(we2[:], 0.0)
            nc.gpsimd.memset(floors[:, 0:LAYERS - 1], 0.0)
            nc.gpsimd.memset(floors[:, LAYERS - 1:LAYERS], -3.0e38)
            nc.gpsimd.memset(fill[:, :, 0:C_KEY], 0.0)
            nc.gpsimd.memset(fill[:, :, C_KEY:C_KEY + 1], -1.0)
            nc.gpsimd.memset(fill[:, :, C_KEY + 1:C], 0.0)
            nc.gpsimd.memset(fill2[:, :, C2_KEY:C2_KEY + 1], -1.0)
            nc.gpsimd.memset(fill2[:, :, C2_KEY + 1:C2], 0.0)
            nc.gpsimd.memset(fill3[:, :, C3_ROW:C3_ROW + 1], -1.0)
            nc.gpsimd.memset(fill3[:, :, C3_ROW + 1:C3], 0.0)
            pool.drain()
            pool.sem_inc(consts, 1)

            def scatter(n, to, copies, places, width, other=None):
                def prepare(i, h, wait):
                    js = bass.ds((i * 2 + h) * SG, SG)
                    if wait:
                        hold(pool, scattered[h], (i + n * G2) * (16 * SG))
                    for lo_c, hi_c, part in copies:
                        if hi_c is None and lo_c == other:
                            nc.gpsimd.tensor_copy(stage[:, h, :, lo_c].bitcast(I32), part[:, js])
                        elif hi_c is None:
                            nc.gpsimd.tensor_copy(stage[:, h, :, lo_c], part[:, js])
                        else:
                            nc.gpsimd.tensor_copy(stage[:, h, :, lo_c:hi_c], part[:, js, 0:hi_c - lo_c])
                    nc.gpsimd.tensor_copy(stage_at[:, h, :], places[:, js]).then_inc(staged, 1)

                def send(h, columns):
                    for j in columns:
                        nc.gpsimd.indirect_dma_start(
                            to, bass.IndirectOffsetOnAxis(ap=stage_at[:, h, j:j + 1], axis=0),
                            stage[:, h, j, 0:width], None).then_inc(scattered[h], 16)

                def two_groups(i, first, last):
                    for h in range(2):
                        hold(pool, staged, (i + n * G2) * 2 + (h + 1))
                        send(h, range(SG // 2))
                        if h == 0:
                            prepare(i, 1, not first)
                        elif not last:
                            prepare(i + 1, 0, True)
                        send(h, range(SG // 2, SG))

                prepare(0, 0, n > 0)
                two_groups(0, n == 0, False)
                with pool.Fori(1, G2 - 1) as i:
                    two_groups(i, False, False)
                two_groups(G2 - 1, False, True)

            def gather(ep, p, c_other, frm, width):
                hold(pool, table_in, 32 * (NP * ep + 1))
                with pool.Fori(0, NB) as i:
                    m = ep * NB + i
                    for c in range(CH):
                        pool.wait_ge(pay_in[c], 16 * (m + 1))
                        hold(pool, slots_free, m * U + (c + 1) * UC)
                        for u in range(c * U // CH, (c + 1) * U // CH):
                            for k in range(K):
                                j = (u * K + k) % CT
                                nc.gpsimd.indirect_dma_start(
                                    rows[:, u, k, 0:width], None, frm,
                                    bass.IndirectOffsetOnAxis(ap=p[:, c, j, c_other:c_other + 1].bitcast(I32), axis=0)).then_inc(gathered[u], 16)

            pool.wait_ge(filled, 16 * 10)
            pool.wait_ge(made_rows, 1)
            pool.wait_ge(placed, 1)
            scatter(0, rows_bin, [(0, C3, bin_rows)], pos_i[:, 0, :], C3)
            pool.wait_ge(made_rows, 2)
            pool.wait_ge(placed, 2)
            scatter(1, rows_dst, [(0, C_OTHER, edge_rows), (C_OTHER, None, edge_rows[:, :, C_OTHER])],
                    pos_i[:, 1, :], C, C_OTHER)
            gather(EP_L0, pay, C_OTHER, table, D)
            scatter(2, rows_src, [(C2_KEY, None, lo_src[:]), (C2_OTHER, None, dst_f[:])], pos_src[:], C2, C2_OTHER)
            with pool.Fori(0, LAYERS) as l:
                gather(l + EP_L2, pay, C_OTHER, table2, 2 * D)
            gather(EP_L3, pay2, C2_OTHER, table, D)

        @block.vector
        def _(v):
            done = [0]

            def link(ins):
                done[0] += 1
                ins.then_inc(dve_step, 1)
                v.wait_ge(dve_step, done[0])

            def steps(loop, count, index):
                start, n = done[0], [0]

                def link_in(ins):
                    n[0] += 1
                    ins.then_inc(dve_step, 1)
                    v.wait_ge(dve_step, index * count + (start + n[0]))
                return link_in

            def over_d(a):
                return a.unsqueeze(2).to_broadcast([LO, HI, D])

            def over_hi(a):
                return a.unsqueeze(1).to_broadcast([LO, HI, D])

            sqrts = [0]

            def layer_norm(link, frm, to, tmp, n):
                link(nc.vector.tensor_reduce(mean[:], frm, AX_X, ALU.add))
                link(nc.vector.tensor_scalar(mean[:], mean[:], 1.0 / D, None, ALU.mult))
                link(nc.vector.tensor_tensor(to, frm, over_d(mean[:]), ALU.subtract))
                link(nc.vector.tensor_tensor(tmp, to, to, ALU.mult))
                link(nc.vector.tensor_reduce(var[:], tmp, AX_X, ALU.add))
                nc.vector.tensor_scalar(var[:], var[:], 1.0 / D, LN_EPS, ALU.mult, ALU.add).then_inc(sqrt_in, 1)
                v.wait_ge(sqrt_out, n + 1)
                link(nc.vector.reciprocal(rstd[:], rstd[:]))
                link(nc.vector.tensor_tensor(to, to, over_d(rstd[:]), ALU.mult))

            LN_LINKS = 7

            v.sem_inc(proj_read, 1)
            v.sem_inc(layer_w_free, 1)
            v.sem_inc(turned_read, 1)
            v.wait_ge(consts, 1)
            nc.vector.memset(ones[:], 1.0)
            nc.vector.memset(ones_b[:], 1.0)
            nc.vector.memset(zeros[:], 0.0)
            nc.vector.memset(zeros_b[:], 0.0)
            nc.vector.tensor_copy(iota_row_b[:], iota_row[:])
            nc.vector.tensor_copy(iota_col_h[:], iota_t[:, 0:CW])
            nc.vector.tensor_scalar(ident[:], iota_row[:], iota_p[:, 0:1], None, ALU.is_equal)
            nc.vector.tensor_scalar(ident_b[:], iota_row[:], iota_p[:, 0:1], None, ALU.is_equal)
            link(nc.vector.tensor_scalar(before[:], iota_row[:], iota_p[:, 0:1], None, ALU.is_gt))
            v.sem_inc(dve_consts, 1)

            v.wait_ge(loaded0, 16 * 2)
            link(nc.vector.tensor_copy(key, key_i))
            link(nc.vector.tensor_scalar(ta, key, 1.0 / HI, -0.48, ALU.mult, ALU.add))
            link(nc.vector.tensor_scalar(ta, ta, ROUND, None, ALU.add))
            link(nc.vector.tensor_scalar(lo, ta, -ROUND, None, ALU.add))
            link(nc.vector.scalar_tensor_tensor(hi, lo, -float(HI), key, ALU.mult, ALU.add))
            link(nc.vector.tensor_scalar(grp, hi[:, 1, :], 1.0 / CB, -(0.5 - 0.5 / CB), ALU.mult, ALU.add))
            link(nc.vector.tensor_scalar(grp, grp, ROUND, None, ALU.add))
            link(nc.vector.tensor_scalar(grp, grp, -ROUND, None, ALU.add))
            nc.vector.scalar_tensor_tensor(keys_b[:, 0, :], grp, float(HI), hi[:, 0, :], ALU.mult, ALU.add)
            nc.vector.tensor_copy(keys_b[:, 1, :], hi[:, 1, :])
            nc.vector.tensor_copy(keys_b[:, 2, :], hi[:, 0, :])
            link(nc.vector.scalar_tensor_tensor(col, grp, -float(CB), hi[:, 1, :], ALU.mult, ALU.add))
            link(nc.vector.scalar_tensor_tensor(col, col, float(LO), lo[:, 1, :], ALU.mult, ALU.add))
            v.sem_inc(lo_ready, 1)

            def lay_out(orders, n):
                for s in orders:
                    with v.Fori(0, SEGS[s] // Q) as i:
                        lk = steps(v, Q // QR, i)
                        for q in range(Q):
                            ins = nc.vector.tensor_scalar(ohk[:, q % QR, :], keys_b[:, s, :], iota_t[0:EP, bass.ds(i * Q + q, 1)],
                                                          None, ALU.is_equal, ALU.add,
                                                          accum_out=cnt[:, bass.ds(i * Q + (q + SEG_AT[s]), 1)])
                            if q % QR == QR - 1:
                                lk(ins)
                    done[0] += SEGS[s] // QR
                v.sem_inc(counted, 1)
                v.wait_ge(prefixed, n + 1)
                al = slice(SEG_AT[orders[0]], SEG_AT[orders[-1]] + SEGS[orders[-1]])
                pre = ps[0:EP, 7, al]
                tot = ps[0:EP, 7, BUCKETS + al.start:BUCKETS + al.stop]
                link(nc.vector.tensor_scalar(tiles[:, al], tot, 1.0 / 128, 0.5 - 1.0 / 256, ALU.mult, ALU.add))
                link(nc.vector.tensor_scalar(tiles[:, al], tiles[:, al], ROUND, None, ALU.add))
                link(nc.vector.tensor_scalar(tiles[:, al], tiles[:, al], -ROUND, 1.0, ALU.add, ALU.max))
                for s in orders:
                    seg = slice(SEG_AT[s], SEG_AT[s] + SEGS[s])
                    link(nc.vector.tensor_tensor_scan(tsum[:, seg], ones_b[0:EP, 0:SEGS[s]], tiles[:, seg], 0.0, ALU.mult, ALU.add))
                link(nc.vector.tensor_tensor(tsum[:, al], tsum[:, al], tiles[:, al], ALU.subtract))
                link(nc.vector.scalar_tensor_tensor(base[:, al], tsum[:, al], 128.0, pre, ALU.mult, ALU.add))
                link(nc.vector.tensor_scalar(base[:, al], base[:, al], -1.0, None, ALU.add))

            def rank(s, to):
                link(nc.vector.memset(pos, 0.0))
                with v.Fori(0, SEGS[s] // Q) as i:
                    first = i * Q + SEG_AT[s]

                    def compare(q):
                        if q >= QR:
                            hold(v, rank_copied, first + (q - QR + 1))
                        nc.vector.tensor_scalar(ohk[:, q % QR, :], keys_b[:, s, :], iota_t[0:EP, bass.ds(i * Q + q, 1)],
                                                None, ALU.is_equal).then_inc(rank_compared, 1)

                    def scan(q):
                        hold(v, rank_compared, first + (q + 1))
                        nc.vector.tensor_tensor_scan(ps[0:EP, q % QR, 0:EJ], ones_b[0:EP, :], ohk[:, q % QR, :],
                                                     base[:, bass.ds(i * Q + (q + SEG_AT[s]), 1)],
                                                     ALU.mult, ALU.add).then_inc(rank_scanned, 1)

                    compare(0)
                    compare(1)
                    scan(0)
                    for q in range(Q):
                        if q + 2 < Q:
                            compare(q + 2)
                        if q + 1 < Q:
                            scan(q + 1)
                        hold(v, rank_scanned, first + (q + 1))
                        if q:
                            hold(v, rank_copied, first + q)
                        nc.vector.copy_predicated(pos, ohk[:, q % QR, :].bitcast(I16),
                                                  ps[0:EP, q % QR, 0:EJ]).then_inc(rank_copied, 1)
                    v.wait_ge(rank_copied, first + Q)
                tq = ta[:, 0, :]
                link(nc.vector.tensor_scalar(tq, pos, 1.0 / 128, -(0.5 - 1.0 / 256), ALU.mult, ALU.add))
                link(nc.vector.tensor_scalar(tq, tq, ROUND, None, ALU.add))
                link(nc.vector.tensor_scalar(tq, tq, -ROUND, None, ALU.add))
                link(nc.vector.scalar_tensor_tensor(pos, tq, -128.0, pos, ALU.mult, ALU.add))
                link(nc.vector.scalar_tensor_tensor(to, pos, float(SEG_T[s]), tq, ALU.mult, ALU.add))
                v.sem_inc(placed, 1)

            lay_out((0,), 0)
            rank(0, pos_i[:, 0, :])

            v.wait_ge(loaded, 16 * (len(loads) + len(block_loads)))
            layer_norm(link, xs[:], t1[:], t2[:], 0)
            nc.vector.tensor_scalar(hs[:], t1[:], 0.0, None, ALU.max).then_inc(node_ready, 1)

            lay_out((1, 2), 1)
            rank(1, pos_i[:, 1, :])
            rank(2, pos_src[:])

            nc.vector.tensor_scalar(bnc[:, 1:2], bnc[:, 1:2], LN_EPS, None, ALU.add)
            nc.vector.tensor_scalar(bnr[:, 3, :], bnr[:, 3, :], LN_EPS, None, ALU.add).then_inc(bn_var_ready, 1)
            v.wait_ge(bn_root_ready, 1)
            link(nc.vector.reciprocal(bnc[:, 1:2], bnc[:, 1:2]))
            link(nc.vector.reciprocal(bnr[:, 3, :], bnr[:, 3, :]))
            link(nc.vector.tensor_tensor(bnc[:, 0:1], bnc[:, 0:1], bnc[:, 1:2], ALU.mult))
            link(nc.vector.tensor_tensor(bnr[:, 0, :], bnr[:, 0, :], bnr[:, 3, :], ALU.mult))
            link(nc.vector.tensor_tensor(bnr[:, 2, :], bnr[:, 2, :], bnr[:, 0, :], ALU.mult))
            link(nc.vector.tensor_tensor(bnr[:, 1, :], bnr[:, 1, :], bnr[:, 2, :], ALU.subtract))
            link(nc.vector.tensor_tensor(w3d[:, 0, :], w3s[:, 0:D], w3s[:, D:2 * D], ALU.subtract))
            link(nc.vector.tensor_scalar(w3d[:, 0, :], w3d[:, 0, :], bnc[:, 0:1], None, ALU.mult))
            nc.vector.tensor_scalar(w3d[:, 1, :], w3s[:, D:2 * D], bnc[:, 0:1], None, ALU.mult).then_inc(w3_ready, 1)
            v.wait_ge(w3_turned, 1)
            link(nc.vector.tensor_copy(w3T[:], ps[0:D, 7, 0:2 * D]))

            parts = [(0, 0, LO), (0, LO, BINS), (1, 0, HI), (2, 0, HI)]
            for x, (s, b0, b1_) in enumerate(parts):
                n = b1_ - b0
                link(nc.vector.tensor_tensor(picked[0:n, 0:n], tsum[0:n, SEG_AT[s] + b0:SEG_AT[s] + b1_], ident[0:n, 0:n], ALU.mult))
                link(nc.vector.tensor_reduce(start_col[0:n, x:x + 1], picked[0:n, 0:n], AX_X, ALU.add))
            for r in range(2):
                for x in (2 * r, 2 * r + 1):
                    s, b0, b1_ = parts[x]
                    ins = nc.vector.tensor_scalar(begun[0:b1_ - b0, x % 2, 0:SEG_T[s]], iota_t[0:b1_ - b0, 0:SEG_T[s]],
                                                  start_col[0:b1_ - b0, x:x + 1], None, ALU.is_ge)
                ins.then_inc(starts_ready, 1)
                v.wait_ge(starts_summed, r + 1)
                if r == 0:
                    sums = ps[0:1, 5:7, 0:T3 // 2]
                    two = "p (b t) -> p b t"
                    link(nc.vector.tensor_scalar(bin_of.rearrange(two, b=2), sums, -1.0, None, ALU.add))
                    link(nc.vector.tensor_scalar(turn_of, bin_of, 1.0 / EV, -(0.5 - 0.5 / EV), ALU.mult, ALU.add))
                    link(nc.vector.tensor_scalar(turn_of, turn_of, ROUND, None, ALU.add))
                    link(nc.vector.tensor_scalar(turn_of, turn_of, -ROUND, None, ALU.add))
                    link(nc.vector.scalar_tensor_tensor(turn_of, turn_of, -float(EV), bin_of, ALU.mult, ALU.add))
                    link(nc.vector.tensor_scalar(bank_of, turn_of, 512.0, None, ALU.mult))
                    link(nc.vector.tensor_scalar(need, bin_of, 1.0, None, ALU.add))
                else:
                    for side, bank in ((1, 5), (0, 6)):
                        block_of, bank_no = bin_of[:, 0:T], turn_of[:, 0:T]
                        link(nc.vector.tensor_scalar(block_of, ps[0:1, bank, 0:T], -1.0, None, ALU.add))
                        link(nc.vector.tensor_scalar(tab_at[:, side, :], block_of, float(3 * D), None, ALU.mult))
                        link(nc.vector.tensor_scalar(bank_no, block_of, 1.0 / AB, -(0.5 - 0.5 / AB), ALU.mult, ALU.add))
                        link(nc.vector.tensor_scalar(bank_no, bank_no, ROUND, None, ALU.add))
                        link(nc.vector.tensor_scalar(bank_no, bank_no, -ROUND, float(512 - AB * AP), ALU.add, ALU.mult))
                        link(nc.vector.scalar_tensor_tensor(acc_at[:, side, :], block_of, float(AP), bank_no, ALU.mult, ALU.add))
            link(nc.vector.tensor_scalar(bin_end[:, 0:BINS - 1], tsum[0:1, 1:BINS], float(BS), None, ALU.add))
            link(nc.vector.memset(bin_end[:, BINS - 1:BINS], T3 + BS))
            v.sem_inc(blk_ready, 1)

            v.wait_ge(bin_loaded, 16)
            nc.vector.tensor_copy(scal[:, :, 0], bin_in[:, :, C3_ROW])
            nc.vector.tensor_copy(scal[:, :, 1], bin_in[:, :, C3_COL])
            w_rest = bin_in[:, :, C3_W]
            for part in range(3):
                link(nc.vector.tensor_copy(wparts[:, :, part], w_rest))
                if part < 2:
                    link(nc.vector.tensor_tensor(w_rest, w_rest, wparts[:, :, part], ALU.subtract))
            v.wait_ge(made_rows, 2)
            start = done[0]

            def fetch(n, half):
                nc.vector.tensor_copy(sw[:, half], wparts[:, bass.ds(n * BS, BS), :])
                nc.vector.tensor_copy(sc[:, half], scal[:, bass.ds(n * BS, BS), :]).then_inc(dve_step, 1)

            def operands(n, half, more):
                v.wait_ge(dve_step, n + (start + 1))
                for k in range(BS):
                    if k == BS // 2 and more:
                        v.wait_ge(op_ready, n * BS + BS // 4)
                        fetch(n + 1, 1 - half)
                    v.wait_ge(built, n * BS + (k + 1))
                    nc.vector.scalar_tensor_tensor(lhs[:, k], iota_row_b[:].unsqueeze(1).to_broadcast([128, 3, 128]), sc[:, half, k, 0:1],
                                                   sw[:, half, k, :].unsqueeze(2).to_broadcast([128, 3, 128]), ALU.is_equal, ALU.mult)
                    nc.vector.tensor_scalar(rhs[:, k, :], iota_col_h[:], sc[:, half, k, 1:2], None, ALU.is_equal).then_inc(op_ready, 1)

            bodies = T3 // BS
            fetch(0, 0)
            with v.Fori(0, bodies // 2 - 1) as i:
                operands(i * 2, 0, True)
                operands(i * 2 + 1, 1, True)
            operands(bodies - 2, 0, True)
            operands(bodies - 1, 1, False)
            done[0] += bodies

            def one_hots(m, v_, p, c_key, weights, turned):
                c = v_ % U // UC
                if v_ % UC == 0:
                    v.wait_ge(pay_in[c], 16 * (m + (v_ // U + 1)))
                v.wait_ge(slots_free, m * U + (v_ + U - R + 1))
                j0 = v_ * K % CT
                if weights:
                    nc.vector.tensor_copy(of(msg, v_)[:, :, D], p[:, c, j0:j0 + K, C_W])
                for k in range(K):
                    key_at = p[:, c, j0 + k, c_key:c_key + 1]
                    if turned:
                        nc.vector.tensor_scalar(of(ohb, v_)[:, k, :], iota_row_b[:], key_at, None, ALU.is_equal)
                    ins = nc.vector.tensor_scalar(of(oh, v_)[:, k, :], iota_row_b[:], key_at, None, ALU.is_equal)
                ins.then_inc(oh_ready, 1)

            def by_two(a):
                return a.rearrange("p (q k) d -> p q k d", q=2)

            def add_local_rows(m, v_, n1, edge):
                v.wait_ge(lin_ready, m * U + (v_ + 1))
                v.wait_ge(gathered[v_ % U], 16 * K * (m + 1))
                to, at_ = (1, D) if edge else (0, 0)
                sums = by_two(of(s1, v_)[:, to])
                nc.vector.tensor_tensor(sums, local_ps[:, :, :, 0], by_two(rows[:, v_ % U, :, at_:at_ + D]), ALU.add).then_inc(add_a, 1)
                if edge:
                    nc.vector.tensor_tensor(by_two(of(s1, v_)[:, 0]), edge_ps, by_two(rows[:, v_ % U, :, 0:D]), ALU.add)
                v.wait_ge(add_a, n1 + 1)
                nc.vector.tensor_tensor(sums, sums, local_ps[:, :, :, 1], ALU.add).then_inc(add_b, 1)
                v.wait_ge(add_b, n1 + 1)
                nc.vector.tensor_tensor(sums, sums, local_ps[:, :, :, 2], ALU.add).then_inc(sum_ready, 1)

            v.wait_ge(pay_in[0], 16)
            link(nc.vector.memset(msg, 0.0))

            def turn0(i, u, before, more):
                if before == 0:
                    one_hots(i, u, pay, C_KEY, True, False)
                if more:
                    one_hots(i, u + 1, pay, C_KEY, True, False)
                v.wait_ge(lin_ready, i * U + (u + 1))
                v.wait_ge(gathered[u], 16 * K * (i + 1))
                nc.vector.tensor_tensor(of(s1, u)[:, 0], lin(u), rows[:, u, :, 0:D], ALU.add).then_inc(sum_ready, 1)
            over_units(v, turn0)
            v.wait_ge(acc_done, 1)
            v.wait_ge(bank_free, EV + BINS)
            nc.vector.tensor_reduce(deg[:, 0, :], deg_bins[0:LO, :].rearrange("p (c h) -> p h c", c=CG), AX_X, ALU.add)
            nc.vector.tensor_copy(deg[:, 1, 0:FB * AB].rearrange("p (g b) -> p g b", g=FB), acc_full[:, :, :, D])
            nc.vector.tensor_copy(deg[:, 1, FB * AB:HI], acc_rest[:, :, D])
            nc.vector.tensor_tensor(in_full(hs), in_full(hs), acc_full[:, :, :, 0:D], ALU.add)
            nc.vector.tensor_tensor(in_rest(hs), in_rest(hs), acc_rest[:, :, 0:D], ALU.add).then_inc(acc_read, 1)
            v.wait_ge(acc_read, 1)
            v.sem_inc(hs_ready, 1)
            link(nc.vector.tensor_scalar(deg[:], deg[:], 1.0, None, ALU.add))
            def take_turned(i):
                v.wait_ge(stT_done, i + 1)
                if i >= 2:
                    v.wait_ge(mlp_done, i - 1)
                tp = flat[0:D, TURN_AT:TURN_AT + PB * 128].rearrange("p (k c) -> p k c", k=PB)
                nc.vector.tensor_copy(hT[:, i % 2, :, 0:LO], tp[:, :, 0:LO]).then_inc(hT_ready, 1)

            take_turned(0)
            take_turned(1)
            for i in range(NP):
                v.wait_ge(proj_done, i + 2)
                bl = slice(i * PB, (i + 1) * PB)
                nc.vector.tensor_tensor(t1[:, bl, :], mlp_out(i), b2r[:].unsqueeze(1).to_broadcast([LO, PB, D]),
                                        ALU.add).then_inc(proj_read, 1)
                if i + 2 < NP:
                    take_turned(i + 2)
                v.wait_ge(proj_read, i + 2)
                nc.vector.tensor_tensor(xs[:, bl, :], xs[:, bl, :], t1[:, bl, :], ALU.add)
            v.sem_inc(layer1_start, 1)

            link(nc.vector.tensor_scalar(inv_deg[:], deg[:], 1e-30, None, ALU.max))
            v.sem_inc(sqrt_in, 1)
            v.wait_ge(sqrt_out, 2)
            link(nc.vector.reciprocal(inv_deg[:], inv_deg[:]))
            link(nc.vector.scalar_tensor_tensor(inv_deg[:], deg[:], 0.0, inv_deg[:], ALU.is_gt, ALU.mult))
            nc.vector.tensor_scalar(last_in[:], inv_deg[:, 1, :], 1.0 - ALPHA, None, ALU.mult)
            link(nc.vector.scalar_tensor_tensor(keep[:], inv_deg[:, 0, :], 1.0 - ALPHA, inv_deg[:, 1, :], ALU.mult, ALU.mult))

            layer_norm(link, xs[:], t1[:], t2[:], 2)
            link(nc.vector.tensor_scalar(t1[:], t1[:], 0.0, None, ALU.max))
            link(nc.vector.tensor_tensor(hs[:], t1[:], over_d(inv_deg[:, 0, :]), ALU.mult))
            v.sem_inc(h_ready, CG)
            nc.vector.tensor_scalar(fs[:], hs[:], ALPHA, None, ALU.mult)
            link(nc.vector.scalar_tensor_tensor(xs[:], t1[:], ALPHA, xs[:], ALU.mult, ALU.add))
            start = done[0]

            def next_h(n, first, count, h, h_next):
                bl = bass.ds(first, count)
                sums = ps[0:LO, 7, 0:count * 2 * D].rearrange("p (k c) -> p k c", k=count)
                v.wait_ge(turned, n + 3)
                nc.vector.tensor_tensor(t2[:, bl, :], h[:, bl, :], sums[:, :, 0:D], ALU.add).then_inc(dve_step, 1)
                v.wait_ge(dve_step, n * 2 + (start + 1))
                nc.vector.tensor_tensor(t2[:, bl, :], t2[:, bl, :], sums[:, :, D:2 * D], ALU.add).then_inc(turned_read, 1)
                v.wait_ge(turned_read, n + 2)
                nc.vector.tensor_tensor(t1[:, bl, :], t2[:, bl, :], keep[:, bl].unsqueeze(2).to_broadcast([LO, count, D]),
                                        ALU.mult).then_inc(dve_step, 1)
                v.wait_ge(dve_step, n * 2 + (start + 2))
                nc.vector.tensor_tensor(h_next[:, bl, :], t1[:, bl, :], fs[:, bl, :], ALU.add).then_inc(h_ready, 1)

            with v.Fori(0, STEPS // 2) as s2:
                for half, (h, h_next) in enumerate(((hs, hs2), (hs2, hs))):
                    with v.Fori(0, CG - 1) as c:
                        next_h((s2 * 2 + half) * CG + c, c * CB, CB, h, h_next)
                    next_h((s2 * 2 + half) * CG + (CG - 1), (CG - 1) * CB, 1, h, h_next)
            done[0] += 2 * STEPS * CG
            v.wait_ge(h_ready, CG * (STEPS + 1))
            link(nc.vector.tensor_tensor(t1[:], t2[:], over_d(last_in[:]), ALU.mult))
            link(nc.vector.tensor_tensor(xs[:], xs[:], t1[:], ALU.add))

            link(nc.vector.memset(msg, 0.0))
            layer_norm(link, xs[:], t1[:], t2[:], 3)
            link(nc.vector.tensor_scalar(hs[:], t1[:], 0.0, None, ALU.max))
            COUNT = 9 + LN_LINKS
            with v.Fori(0, LAYERS) as l:
                ln = [0]
                lstart = done[0]

                def lk(ins):
                    ln[0] += 1
                    ins.then_inc(dve_step, 1)
                    v.wait_ge(dve_step, l * COUNT + (lstart + ln[0]))
                v.wait_ge(layer_w, 16 * LW * (l + 1))
                lk(nc.vector.tensor_copy(floor[:], floors[:, bass.ds(l, 1)]))
                v.sem_inc(hs_ready, 1)
                hold(v, table_in, 32 * (NP * l + 1))
                for i in range(NP):
                    v.wait_ge(proj_done, (l + 1) * NP + (i + 2))
                    y = projected(i, 3 * D)
                    bl = slice(i * PB, (i + 1) * PB)
                    nc.vector.tensor_tensor(tab2[:, bl, 0:D], y[:, :, 0:D], be2r[:].unsqueeze(1).to_broadcast([LO, PB, D]), ALU.add)
                    nc.vector.tensor_copy(tab2[:, bl, D:2 * D], y[:, :, D:2 * D])
                    nc.vector.tensor_copy(t1[:, bl, :], y[:, :, 2 * D:3 * D]).then_inc(proj_read, 1)
                v.wait_ge(proj_read, (l + 2) * NP + 1)
                v.sem_inc(node_ready, 1)
                lk(nc.vector.tensor_copy(local_b[:, :, 0], t1[:]))
                lk(nc.vector.tensor_tensor(t1[:], t1[:], local_b[:, :, 0], ALU.subtract))
                lk(nc.vector.tensor_copy(local_b[:, :, 1], t1[:]))
                lk(nc.vector.tensor_tensor(t1[:], t1[:], local_b[:, :, 1], ALU.subtract))
                lk(nc.vector.tensor_copy(local_b[:, :, 2], t1[:]))
                v.sem_inc(local_ready, 1)
                def message(m, v_, n1):
                    v.wait_ge(att_ready, n1 + 1)
                    nc.vector.tensor_tensor(of(msg, v_)[:, :, 0:D], of(s1, v_)[:, 0], of(att, v_).unsqueeze(2).to_broadcast([128, K, D]),
                                            ALU.mult).then_inc(msg_ready, 1)

                def turn2(i, u, before, more):
                    m = (l + EP_L2) * NB + i
                    n1 = (l * NB + i) * U + u
                    if before == 0:
                        one_hots(m, u, pay, C_KEY, False, True)
                    if more:
                        one_hots(m, u + 1, pay, C_KEY, False, True)
                    add_local_rows(m, u, n1, True)
                    v.wait_ge(sum_ready, m * U + (u + 1))
                    nc.vector.scalar_tensor_tensor(of(zr, u), of(s1, u)[:, 1], 0.0, wa2r[:].unsqueeze(1).to_broadcast([128, K, D]),
                                                   ALU.max, ALU.mult).then_inc(zr_ready, 1)
                    if before:
                        message(m, u - 1, (l * NB + i) * U + (u - 1))
                    v.wait_ge(zr_ready, n1 + 1)
                    nc.vector.tensor_reduce(of(logit, u), of(zr, u), AX_X, ALU.add).then_inc(logit_ready, 1)
                over_units(v, turn2)
                message((l + EP_L2) * NB + (NB - 1), U - 1, l * (NB * U) + (NB * U - 1))
                hold(v, norm_w, 16 * 3 * (l + 1))
                v.wait_ge(acc_done, l + EP_L2 + 1)
                nc.vector.tensor_tensor(in_full(t1), acc_full[:, :, :, 0:D],
                                        biasr[:].unsqueeze(1).unsqueeze(1).to_broadcast([LO, FB, AB, D]), ALU.add)
                nc.vector.tensor_tensor(in_rest(t1), acc_rest[:, :, 0:D],
                                        biasr[:].unsqueeze(1).to_broadcast([LO, HI - FB * AB, D]), ALU.add).then_inc(acc_read, 1)
                v.wait_ge(acc_read, l + EP_L2 + 1)
                layer_norm(lk, t1[:], t2[:], t1[:], l + 4)
                lk(nc.vector.tensor_tensor(t2[:], t2[:], over_hi(lngr[:]), ALU.mult))
                lk(nc.vector.tensor_tensor(t2[:], t2[:], over_hi(lnbr[:]), ALU.add))
                lk(nc.vector.scalar_tensor_tensor(hs[:], t2[:], floor[:, 0:1], hs[:], ALU.max, ALU.add))
                v.sem_inc(layer_w_free, 1)
                assert ln[0] == COUNT, ln[0]
            done[0] += COUNT * LAYERS
            link(nc.vector.tensor_tensor(xs[:], xs[:], hs[:], ALU.add))

            layer_norm(link, xs[:], t1[:], t2[:], 4 + LAYERS)
            link(nc.vector.tensor_scalar(hs[:], t1[:], 0.0, None, ALU.max))
            v.sem_inc(hs_ready, 1)
            for i in range(NP):
                v.wait_ge(proj_done, i + (LAYERS + 1) * NP + 2)
                y = projected(i, 2 * D)
                bl = slice(i * PB, (i + 1) * PB)
                nc.vector.tensor_tensor(t2[:, bl, :], y[:, :, 0:D], bnr[:, 1, :].unsqueeze(1).to_broadcast([LO, PB, D]), ALU.add)
                nc.vector.tensor_copy(t1[:, bl, :], y[:, :, D:2 * D]).then_inc(proj_read, 1)
            v.wait_ge(proj_read, (LAYERS + 2) * NP + 1)
            v.sem_inc(node_ready, 1)
            link(nc.vector.tensor_copy(local_b[:, :, 0], t2[:]))
            link(nc.vector.tensor_tensor(t2[:], t2[:], local_b[:, :, 0], ALU.subtract))
            link(nc.vector.tensor_copy(local_b[:, :, 1], t2[:]))
            link(nc.vector.tensor_tensor(t2[:], t2[:], local_b[:, :, 1], ALU.subtract))
            link(nc.vector.tensor_copy(local_b[:, :, 2], t2[:]))
            v.sem_inc(local_ready, 1)
            def turn3(i, u, before, more):
                m = i + EP_L3 * NB
                if before == 0:
                    one_hots(m, u, pay2, C2_KEY, False, True)
                if more:
                    one_hots(m, u + 1, pay2, C2_KEY, False, True)
                add_local_rows(m, u, (i + LAYERS * NB) * U + u, False)
            over_units(v, turn3)
            v.wait_ge(acc_done, EP_L3 + 1)
            nc.vector.tensor_tensor(in_full(xs), in_full(xs), acc_full[:, :, :, 0:D], ALU.add)
            nc.vector.tensor_tensor(in_rest(xs), in_rest(xs), acc_rest[:, :, 0:D], ALU.add).then_inc(node_ready, 1)

        @block.scalar
        def _(a):
            def root(to, frm, n):
                a.wait_ge(sqrt_in, n + 1)
                nc.scalar.activation(to, frm, ACT.Sqrt).then_inc(sqrt_out, 1)

            a.sem_inc(slot_used, NG)
            for g in range(EV):
                a.sem_inc(ev_out[g], 16)
            a.wait_ge(dve_consts, 1)
            a.wait_ge(lo_ready, 1)
            a.wait_ge(at_loaded, 16 * 3)
            nc.scalar.copy(bin_rows[:, :, C3_ROW], lo[:, 0, :])
            nc.scalar.copy(bin_rows[:, :, C3_COL], col)
            nc.scalar.copy(bin_rows[:, :, C3_W + 1], zeros[0:EP, 0:EJ])
            nc.scalar.copy(bin_rows[:, :, C3_W], wgt).then_inc(made_rows, 1)
            nc.scalar.copy(edge_rows[:, :, 0:DA], at16)
            nc.scalar.copy(edge_rows[:, :, C_ATT3:C_ATT3 + DB], at3)
            nc.scalar.copy(edge_rows[:, :, C_ONE], ones_b[0:EP, :])
            nc.scalar.copy(edge_rows[:, :, C_W], wgt)
            nc.scalar.copy(edge_rows[:, :, C_KEY], lo[:, 1, :])
            nc.scalar.copy(edge_rows[:, :, C_OTHER], key[:, 0, :])
            nc.scalar.copy(edge_rows[:, :, C_OTHER + 1], zeros[0:EP, 0:EJ])
            nc.scalar.copy(lo_src[:], lo[:, 0, :])
            nc.scalar.copy(dst_f[:], key[:, 1, :]).then_inc(made_rows, 1)
            root(rstd[:], var[:], 0)
            a.wait_ge(bn_var_ready, 1)
            nc.scalar.activation(bnc[:, 1:2], bnc[:, 1:2], ACT.Sqrt)
            nc.scalar.activation(bnr[:, 3, :], bnr[:, 3, :], ACT.Sqrt).then_inc(bn_root_ready, 1)

            a.wait_ge(blk_ready, 1)
            with a.Fori(0, CG) as c:
                with a.Fori(0, HI // EV) as i:
                    m = c * (HI // EV) + i
                    _, ends = nc.values_load_multi_w_load_instructions(bin_end[0:1, bass.ds(m * EV, EV)], engines=(a.engine,),
                                                                       min_val=BS + 1, max_val=BS + T3)
                    for g in range(EV):
                        a.wait_ge(ev_out[g], 16 * (m + 1))
                        hold(a, built, ends[g])
                        nc.scalar.activation(ev[:, g, :], ps[:, g, 0:CW], ACT.Copy,
                                             accum_out=deg_bins[:, bass.ds(m * EV + g, 1)]).then_inc(ev_ready, 1)
                        a.wait_ge(ev_ready, m * EV + (g + 1))
                        nc.scalar.copy(ps[:, g, 0:CW], zeros[:]).then_inc(bank_free, 1)
                        a.dma_start(dense[bass.ds(c, 1), :, bass.ds(i * EV + g, 1), :].rearrange("o p b w -> (o p) (b w)"),
                                    ev[:, g, :]).then_inc(ev_out[g], 16)

            def payload(m, v_, bank):
                a.wait_ge(slots_free, m * U + (v_ + U - R + 1))
                a.wait_ge(tr_ready, m * U + (v_ + 1))
                nc.scalar.copy(of(payT, v_), payT_ps(bank)).then_inc(payT_ready, 1)

            def turn0(i, u, before, more):
                if before == 0:
                    payload(i, u, 6 + u % 2)
                if more:
                    payload(i, u + 1, 6 + (u + 1) % 2)
                a.wait_ge(sum_ready, i * U + (u + 1))
                nc.scalar.activation(of(msg, u)[:, :, 0:D], of(s1, u)[:, 0], ACT.Relu).then_inc(msg_ready, 1)
            over_units(a, turn0)

            def take_turned(ph):
                for i in range(NP):
                    q = ph * NP + i
                    a.wait_ge(stT_done, q + 1)
                    a.wait_ge(proj_done, q)
                    tp = flat[0:D, TURN_AT:TURN_AT + PB * 128].rearrange("p (k c) -> p k c", k=PB)
                    nc.scalar.copy(hT[:, i % 2, :, 0:LO], tp[:, :, 0:LO]).then_inc(hT_ready, 1)

            for i in range(NP):
                a.wait_ge(mlp_done, i + 1)
                if i >= 2:
                    a.wait_ge(proj_done, i)
                first = i % 2 * 3 * 512
                up = flat[0:D, first:first + PB * 128].rearrange("p (k c) -> p k c", k=PB)
                nc.scalar.activation(uT[:, i % 2, :, 0:LO], up[:, :, 0:LO], ACT.Gelu, bias=b1c[:, 0:1]).then_inc(uT_ready, 1)
            root(inv_deg[:], inv_deg[:], 1)
            root(rstd[:], var[:], 2)

            def take(n, to, frm):
                a.wait_ge(turned, n + 1)
                nc.scalar.copy(to, frm).then_inc(oT_ready, 1)

            with a.Fori(0, STEPS) as s:
                with a.Fori(0, (CG - 1) // 2) as i:
                    for p in range(2):
                        a.wait_ge(slot_used, (s * (CG - 1) + i * 2) * NG + (p + 2) * NG)
                        take(s * CG + i * 2 + p, oT[:, p, :], ps[:, p, 0:CW])
                a.wait_ge(group_done, s + 1)
                take(s * CG + (CG - 1), oT_last, ps[:, 2, 0:LO])
            root(rstd[:], var[:], 3)

            with a.Fori(0, LAYERS) as l:
                a.wait_ge(w_mm, 2 * l + 1)
                nc.scalar.copy(wnT[:], ps[0:D, 7, 0:D]).then_inc(w_prep, 1)
                a.wait_ge(w_mm, 2 * l + 2)
                nc.scalar.copy(wcat[:, 0:D], wn[:])
                nc.scalar.copy(wcat[:, D:3 * D], ps[0:D, 7, 128:128 + 2 * D]).then_inc(w_prep, 1)
                a.wait_ge(hs_ready, l + 2)
                take_turned(l + 1)
                def turn2(i, u, before, more):
                    m = (l + EP_L2) * NB + i

                    def prepare(v_):
                        payload(m, v_, 6)
                        n1 = (l * NB + i) * U + v_
                        a.wait_ge(hid_done, n1 + 1)
                        nc.scalar.activation(of(hid, v_), hid_ps, ACT.Relu).then_inc(hid_ready, 1)
                        a.wait_ge(ohT_done, n1 + 1)
                        nc.scalar.copy(of(ohT, v_), ohT_ps).then_inc(ohT_ready, 1)
                    if before == 0:
                        prepare(u)
                    if more:
                        prepare(u + 1)
                    n1 = (l * NB + i) * U + u
                    a.wait_ge(logit_ready, n1 + 1)
                    nc.scalar.activation(of(att, u), of(logit, u), ACT.Sigmoid, bias=ba2c[:, 0:1]).then_inc(att_ready, 1)
                over_units(a, turn2)
                root(rstd[:], var[:], l + 4)
            root(rstd[:], var[:], 4 + LAYERS)

            a.wait_ge(hs_ready, 2 + LAYERS)
            take_turned(1 + LAYERS)
            def turn3(i, u, before, more):
                m = i + EP_L3 * NB

                def prepare(v_):
                    a.wait_ge(slots_free, m * U + (v_ + U - R + 1))
                    a.wait_ge(ohT_done, (i + LAYERS * NB) * U + (v_ + 1))
                    nc.scalar.copy(of(ohT, v_), ohT_ps).then_inc(ohT_ready, 1)
                if before == 0:
                    prepare(u)
                if more:
                    prepare(u + 1)
                a.wait_ge(sum_ready, m * U + (u + 1))
                nc.scalar.activation(of(msg, u)[:, :, 0:D], of(s1, u)[:, 0], ACT.Silu).then_inc(msg_ready, 1)
            over_units(a, turn3)

        @block.tensor
        def _(pe):
            def mm(to, lhsT, rhs, start=True, stop=True):
                return nc.tensor.matmul(to, lhsT, rhs, start=start, stop=stop, skip_group_check=True)

            pe.sem_inc(proj_done, 1)
            pe.sem_inc(turned, 2)
            pe.sem_inc(built, BS)
            for n, (c0, c1) in enumerate(((0, SEG_AT[1]), (SEG_AT[1], BUCKETS))):
                pe.wait_ge(counted, n + 1)
                mm(ps[0:EP, 7, c0:c1], before[0:EP, 0:EP], cnt[:, c0:c1])
                mm(ps[0:EP, 7, BUCKETS + c0:BUCKETS + c1], ones[0:EP, 0:EP], cnt[:, c0:c1]).then_inc(prefixed, 1)
            pe.wait_ge(w3_ready, 1)
            for h in range(2):
                ins = nc.tensor.transpose(ps[0:D, 7, h * D:(h + 1) * D], w3d[:, h, :], ident[0:D, 0:D])
            ins.then_inc(w3_turned, 1)
            pe.wait_ge(starts_ready, 1)
            for half in range(2):
                ts = slice(half * (T3 // 2), (half + 1) * (T3 // 2))
                mm(ps[0:1, 5 + half, 0:T3 // 2], ones_b[0:LO, 0:1], begun[0:LO, 0, ts], stop=False)
                ins = mm(ps[0:1, 5 + half, 0:T3 // 2], ones_b[0:BINS - LO, 0:1], begun[0:BINS - LO, 1, ts], start=False)
            ins.then_inc(starts_summed, 1)
            pe.wait_ge(starts_ready, 2)
            for x in range(2):
                ins = mm(ps[0:1, 5 + x, 0:T], ones_b[0:HI, 0:1], begun[0:HI, x, 0:T])
            ins.then_inc(starts_summed, 1)

            pe.wait_ge(blk_ready, 1)
            for g in range(EV):
                ins = mm(ps[:, g, 0:CW], zeros_b[:, 0:128], zeros_b[:, 0:CW], stop=False)
            ins.then_inc(bank_free, EV)

            def load4(at_, lowest, highest):
                return load_values(pe, at_, lowest, highest)

            with pe.Fori(0, T3 // BS) as i:
                for k in range(BS):
                    if k % 4 == 0:
                        banks = load4(bank_of[0:1, bass.ds(i * BS + k, 4)], 0, (EV - 1) * 512)
                        needed = pe.value_load(need[0:1, bass.ds(i * BS + k + 3, 1)], min_val=1, max_val=BINS)
                        hold(pe, bank_free, needed)
                    pe.wait_ge(op_ready, i * BS + (k + 1))
                    for part in range(3):
                        ins = mm(flat[:, bass.ds(banks[k % 4], CW)], lhs[:, k, part, :], rhs[:, k, :], start=False, stop=False)
                    ins.then_inc(built, 1)
            pe.wait_ge(bank_free, EV + BINS)

            def clear(ep):
                if not (isinstance(ep, int) and ep == 0):
                    pe.wait_ge(acc_read, ep)
                for b in range(FB + 1):
                    ins = mm(ps[:, b, :], zeros_b[:, 0:128], zeros_b[:], stop=False)
                return ins

            def finish_pass():
                mm(ps[:, FB, :], zeros_b[:, 0:128], zeros_b[:], start=False).then_inc(acc_done, 1)

            def load_unit(table_, side, i, v_, highest):
                return load4(table_[0:1, side, bass.ds(i * BODY + v_ * K, K)], 0, highest)

            def turn_payload(m, v_, bank):
                c = v_ % U // UC
                if v_ % UC == 0:
                    pe.wait_ge(pay_in[c], 16 * (m + (v_ // U + 1)))
                j = v_ * K % CT
                nc.tensor.transpose(payT_ps(bank), pay[:, c, j:j + K, :].rearrange("p k c -> p (k c)"), ident[:]).then_inc(tr_ready, 1)

            def sum_up(i, m, v_, side):
                offs = load_unit(acc_at, side, i, v_, ACC_LAST)
                pe.wait_ge(oh_ready, m * U + (v_ + 1))
                pe.wait_ge(msg_ready, m * U + (v_ + 1))
                for k in range(K):
                    ins = mm(flat[:, bass.ds(offs[k], MW)], of(oh, v_)[:, k, :], of(msg, v_)[:, k, :], start=False, stop=False)
                ins.then_inc(slots_free, 1)

            clear(0).then_inc(slots_free, U)

            def turn0(i, u, before, more):
                if before == 0:
                    turn_payload(i, u, 6 + u % 2)
                if more:
                    turn_payload(i, u + 1, 6 + (u + 1) % 2)
                pe.wait_ge(payT_ready, i * U + (u + 1))
                if before == 2:
                    pe.wait_ge(sum_ready, i * U + (u - 1))
                mm(ps[:, 4 + u % 2, 0:K * D], of(payT, u), wl0[:].rearrange("p k d -> p (k d)")).then_inc(lin_ready, 1)
                if before == 2:
                    sum_up(i, i, u - 2, 1)
            over_units(pe, turn0)
            for v_ in (U - 2, U - 1):
                sum_up(NB - 1, NB - 1, v_, 1)
            finish_pass()

            def turn_next(i):
                for k in range(PB):
                    ins = nc.tensor.transpose(flat[0:D, TURN_AT + k * 128:TURN_AT + k * 128 + LO], hs[:, i * PB + k, :],
                                              ident[0:LO, 0:LO])
                ins.then_inc(stT_done, 1)

            def second_product(i):
                pe.wait_ge(uT_ready, i + 1)
                if i >= 2:
                    pe.wait_ge(proj_read, i)
                for k in range(PB):
                    ins = mm(mlp_out(i)[:, k, :], uT[:, i % 2, k, 0:LO], w2s[:])
                ins.then_inc(proj_done, 1)

            pe.wait_ge(hs_ready, 1)
            turn_next(0)
            for i in range(NP):
                pe.wait_ge(hT_ready, i + 1)
                if i + 1 < NP:
                    turn_next(i + 1)
                mm(ps[0:D, i % 2 * 3, :].rearrange("p (k c) -> p k c", c=128)[:, :, 0:LO], w1s[:], hT[:, i % 2, 0:4, 0:LO])
                mm(ps[0:D, i % 2 * 3 + 1, 0:LO], w1s[:], hT[:, i % 2, 4, 0:LO]).then_inc(mlp_done, 1)
                if i:
                    second_product(i - 1)
            second_product(NP - 1)

            pe.wait_ge(proj_read, NP + 1)
            pe.wait_ge(kept_in, 16 * CG)

            def times(bank, h, b, bin_, width, half, first, last):
                return mm(ps[half * D:(half + 1) * D, bank, 0:width], h[:, b, :], bin_, start=first, stop=last)

            def turn(n, frm, count):
                pe.wait_ge(oT_ready, n + 1)
                pe.wait_ge(turned_read, n + 1)
                for k in range(count):
                    ins = nc.tensor.transpose(ps[0:LO, 7, k * 128:(k + 1) * 128], frm[:, k * LO:(k + 1) * LO], ident[:])
                ins.then_inc(turned, 1)

            with pe.Fori(0, STEPS // 2) as s2:
                for half, h in enumerate((hs, hs2)):
                    s = s2 * 2 + half
                    with pe.Fori(0, (CG - 1) // 2) as i:
                        for p in range(2):
                            c = i * 2 + p
                            flat_kept = kept.rearrange("p c b w -> p (c b w)")

                            def kept_bin(b):
                                return flat_kept[0:LO, bass.ds(c * (NR * CW) + b * CW, CW)]
                            if p == 0:
                                pe.wait_ge(h_ready, (s + 1) * CG)
                            for g in range(NG):
                                pe.wait_ge(slot_in[g], (s * (CG - 1) + c + 1) * 16)
                                for j in range(GB):
                                    b = NR + g * GB + j
                                    if b < 2 * NR:
                                        times(p, h, b - NR, kept_bin(b - NR), CW, 0, b == NR, False)
                                    ins = times(p, h, b, slots[0:LO, g, j, :], CW, 1 if b < 2 * NR else b % 2,
                                                b == NR, b >= HI - 2)
                                ins.then_inc(slot_used, 1)
                                if p == 1 and g == 1:
                                    turn(s * CG + c - 1, oT[:, 0, :], CB)
                        turn(s * CG + i * 2 + 1, oT[:, 1, :], CB)
                    for b in range(HI):
                        ins = times(2, h, b, kept_last[0:LO, b, :], LO, b % 2, b < 2, b >= HI - 2)
                    ins.then_inc(group_done, 1)
                    turn(s * CG + (CG - 1), oT_last, 1)
            pe.wait_ge(turned_read, CG * STEPS + 1)

            def project(ph, w, width):
                turn_next(0)
                for i in range(NP):
                    q = ph * NP + i
                    hold(pe, hT_ready, q + 1)
                    if i + 1 < NP:
                        turn_next(i + 1)
                    hold(pe, proj_read, q)
                    for k in range(PB):
                        ins = mm(projected(i, width)[:, k, :], hT[:, i % 2, k, 0:LO], w[:, 0:width])
                    ins.then_inc(proj_done, 1)

            def turn_one_hots(m, v_):
                pe.wait_ge(oh_ready, m * U + (v_ + 1))
                for k in range(K):
                    ins = nc.tensor.transpose(ohT_ps[:, k, :], of(ohb, v_)[:, k, :], ident_b[:])
                ins.then_inc(ohT_done, 1)

            def add_local(v_, offs):
                table_rows = local_b.rearrange("p h s d -> p (h s d)")
                for k in range(K):
                    ins = mm(ps[:, 4 + k // 2, k % 2 * LT:(k % 2 + 1) * LT], ohT[0:LO, v_ % R, k, :],
                             table_rows[:, bass.ds(offs[k], LT)], start=k % 2 == 0)
                return ins

            with pe.Fori(0, LAYERS) as l:
                hold(pe, layer_w, 16 * LW * (l + 1))
                nc.tensor.transpose(ps[0:D, 7, 0:D], wn[:], ident[0:D, 0:D]).then_inc(w_mm, 1)
                hold(pe, w_prep, 2 * l + 1)
                mm(ps[0:D, 7, 128:128 + 2 * D], wnT[:], wa1[:].rearrange("p s d -> p (s d)")).then_inc(w_mm, 1)
                hold(pe, w_prep, 2 * l + 2)
                hold(pe, hs_ready, l + 2)
                project(l + 1, wcat, 3 * D)
                hold(pe, proj_read, (l + 2) * NP + 1)
                clear(l + EP_L2)
                hold(pe, local_ready, l + 1)
                def turn2(i, u, before, more):
                    m = (l + EP_L2) * NB + i
                    n1 = (l * NB + i) * U + u

                    def hidden(v_):
                        pe.wait_ge(payT_ready, m * U + (v_ + 1))
                        for q in range(K // 2):
                            ins = mm(hid_ps[:, q, :], wt[:, q, :], of(payT, v_))
                        ins.then_inc(hid_done, 1)
                        turn_one_hots(m, v_)
                    offs = load_unit(tab_at, 1, i, u, (HI - 1) * LT)
                    if before == 0:
                        turn_payload(m, u, 6)
                        hidden(u)
                    pe.wait_ge(ohT_ready, n1 + 1)
                    if more:
                        turn_payload(m, u + 1, 6)
                    pe.wait_ge(hid_ready, n1 + 1)
                    pe.wait_ge(sum_ready, m * U + u)
                    add_local(u, offs)
                    for q in range(K // 2):
                        mm(edge_ps[:, q].rearrange("p k d -> p (k d)"), of(hid, u)[:, q, :], we2[:], start=False)
                        ins = mm(local_ps[:, q, :, 0, :], of(payT, u), wz[:, 2 * q:2 * q + 2, :], start=False)
                    ins.then_inc(lin_ready, 1)
                    if more:
                        hidden(u + 1)
                    if before == 2:
                        sum_up(i, m, u - 2, 1)
                over_units(pe, turn2)
                for v_ in (U - 2, U - 1):
                    sum_up(NB - 1, (l + EP_L2) * NB + (NB - 1), v_, 1)
                finish_pass()

            pe.wait_ge(hs_ready, LAYERS + 2)
            project(LAYERS + 1, w3T, 2 * D)
            pe.wait_ge(proj_read, (LAYERS + 2) * NP + 1)
            clear(EP_L3)
            pe.wait_ge(local_ready, LAYERS + 1)
            def turn3(i, u, before, more):
                m = i + EP_L3 * NB
                offs = load_unit(tab_at, 0, i, u, (HI - 1) * LT)
                if before == 0:
                    turn_one_hots(m, u)
                pe.wait_ge(ohT_ready, (i + LAYERS * NB) * U + (u + 1))
                pe.wait_ge(sum_ready, m * U + u)
                add_local(u, offs).then_inc(lin_ready, 1)
                if more:
                    turn_one_hots(m, u + 1)
                if before == 2:
                    sum_up(i, m, u - 2, 0)
            over_units(pe, turn3)
            for v_ in (U - 2, U - 1):
                sum_up(NB - 1, EP_L3 * NB + NB - 1, v_, 0)
            finish_pass()


_INS = ['x', 'src', 'dst', 'edge_attr_16', 'edge_attr_3', 'edge_weight',
        'L0_gnn_We', 'L0_gnn_be', 'L0_gnn_W1', 'L0_gnn_b1', 'L0_gnn_W2', 'L0_gnn_b2',
        'L2_gnn_W_node', 'L2_gnn_W_e1', 'L2_gnn_b_e1', 'L2_gnn_W_e2', 'L2_gnn_b_e2', 'L2_gnn_Wa1', 'L2_gnn_ba1',
        'L2_gnn_Wa2', 'L2_gnn_ba2', 'L2_gnn_bias', 'L2_gnn_ln_g', 'L2_gnn_ln_b',
        'L3_gnn_W', 'L3_gnn_bn_gamma', 'L3_gnn_bn_beta', 'L3_gnn_bn_mean', 'L3_gnn_bn_var']
_OUTS = [((N, D), 'float32')]


def kernel(**inputs):
    import numpy as _np
    import concourse.bacc as _bacc
    from concourse import mybir as _mybir
    from concourse.bass_utils import run_bass_kernel_spmd as _run

    nc = _bacc.Bacc("TRN2", target_bir_lowering=False, num_devices=1)
    arrays, args = {}, []
    for name in _INS:
        a = _np.ascontiguousarray(inputs[name])
        arrays[f"in_{name}_dram"] = a
        args.append(nc.dram_tensor(f"in_{name}_dram", a.shape, _mybir.dt.from_np(a.dtype), kind="ExternalInput").ap())
    for i, (shape, dtype) in enumerate(_OUTS):
        dt = _mybir.dt.from_np(_np.dtype(dtype))
        args.append(nc.dram_tensor(f"out_{i}_dram", shape, dt, kind="ExternalOutput").ap())
    gnn_kernel(nc, *args)
    r = _run(nc, [arrays], core_ids=[0])
    got = tuple(r.results[0][f"out_{i}_dram"] for i in range(len(_OUTS)))
    return got[0]
```
